# Optimizing a Trainium2 kernel written in Bass

```python
import numpy as np
import jax
import jax.numpy as jnp

def _softmax(x, axis=-1):
    return jax.nn.softmax(x, axis=axis)
def _gelu(x):
    return jax.nn.gelu(x, approximate=True)
def _silu(x):
    return jax.nn.silu(x)
def _sigmoid(x):
    return jax.nn.sigmoid(x)
def _layernorm(x, axis=-1, eps=1e-5):
    m = jnp.mean(x, axis=axis, keepdims=True)
    v = jnp.var(x, axis=axis, keepdims=True)
    return (x - m) / jnp.sqrt(v + eps)
def _scatter_add(tgt, idx, src, axis=0):
    return tgt.at[idx].add(src)
def _segment_sum(src, seg, n):
    return jax.ops.segment_sum(src, seg, n)

kernel_name = 'mk_conv_seq_d2_conv_nchw1024_83b884'

def setup_inputs(seed: int = 0):
    np.random.seed(seed)
    _w = jnp.asarray
    def _rec_inputs():
        import jax
        import jax.numpy as jnp
        _gk = jax.random.key(seed)
        x = -0.0003957 + 1 * jax.random.normal(jax.random.fold_in(_gk, 1), (64, 1024, 14, 14), jnp.float32)
        return x
    x = _rec_inputs()
    def _L0_conv_setup():
        import jax, jax.numpy as jnp
        import numpy as np
        EPS = 1e-05

        def _conv(x, w, b, stride, pad):
            y = jax.lax.conv_general_dilated(x, w, window_strides=(stride, stride), padding=[(pad, pad), (pad, pad)], dimension_numbers=('NCHW', 'OIHW', 'NCHW'))
            return y + b.reshape(1, -1, 1, 1)

        def _bn(x, gamma, beta):
            mean = jnp.mean(x, axis=(0, 2, 3), keepdims=True)
            var = jnp.var(x, axis=(0, 2, 3), keepdims=True)
            xn = (x - mean) * jax.lax.rsqrt(var + EPS)
            return gamma.reshape(1, -1, 1, 1) * xn + beta.reshape(1, -1, 1, 1)
        key = jax.random.key(seed)
        ks = jax.random.split(key, 8)
        N, Cin, H, W = (64, 1024, 14, 14)
        P = 256
        Cout = P * 4

        def kaiming(k, shape):
            fan_in = shape[1] * shape[2] * shape[3]
            return jax.random.normal(k, shape, jnp.float32) * np.float32(np.sqrt(2.0 / fan_in))
        return {'x': jax.random.normal(ks[0], (N, Cin, H, W), jnp.float32), 'w1': kaiming(ks[1], (P, Cin, 1, 1)), 'b1': jnp.zeros((P,), jnp.float32), 'g1': jnp.ones((P,), jnp.float32), 'be1': jnp.zeros((P,), jnp.float32), 'w2': kaiming(ks[2], (P, P, 3, 3)), 'b2': jnp.zeros((P,), jnp.float32), 'g2': jnp.ones((P,), jnp.float32), 'be2': jnp.zeros((P,), jnp.float32), 'w3': kaiming(ks[3], (Cout, P, 1, 1)), 'b3': jnp.zeros((Cout,), jnp.float32), 'g3': jnp.ones((Cout,), jnp.float32), 'be3': jnp.zeros((Cout,), jnp.float32), 'residual_scale': jnp.zeros((1,), jnp.float32)}
    _L0_conv_all = _L0_conv_setup()
    _L0_conv_in = {k: v for k, v in _L0_conv_all.items() if k in ('w1', 'b1', 'g1', 'be1', 'w2', 'b2', 'g2', 'be2', 'w3', 'b3', 'g3', 'be3', 'residual_scale', )}
    del _L0_conv_all

    def _L1_conv_setup():
        import jax, jax.numpy as jnp
        import numpy as np

        def conv(x, w, stride=1, pad=0):
            return jax.lax.conv_general_dilated(x, w, (stride, stride), [(pad, pad), (pad, pad)], dimension_numbers=('NCHW', 'OIHW', 'NCHW'))

        def group_norm(x, scale, bias, groups=32, eps=1e-05):
            B, C, H, W = x.shape
            xg = x.reshape(B, groups, C // groups, H, W)
            m = xg.mean(axis=(2, 3, 4), keepdims=True)
            v = xg.var(axis=(2, 3, 4), keepdims=True)
            xn = ((xg - m) * jax.lax.rsqrt(v + eps)).reshape(B, C, H, W)
            return xn * scale[None, :, None, None] + bias[None, :, None, None]

        def bilinear_sample(x, py, px):
            B, C, H, W = x.shape
            y0 = jnp.floor(py)
            x0 = jnp.floor(px)
            wy1 = py - y0
            wx1 = px - x0
            xf = x.reshape(B, C, H * W)
            Ksp = py.shape[1:]

            def corner(yi, xi, wy, wx):
                valid = (yi >= 0) & (yi < H) & (xi >= 0) & (xi < W)
                yc = jnp.clip(yi, 0, H - 1).astype(jnp.int32)
                xc = jnp.clip(xi, 0, W - 1).astype(jnp.int32)
                idx = (yc * W + xc).reshape(B, 1, -1)
                v = jnp.take_along_axis(xf, idx, axis=2).reshape(B, C, *Ksp)
                w = (wy * wx * valid).astype(x.dtype)[:, None]
                return v * w
            return corner(y0, x0, 1.0 - wy1, 1.0 - wx1) + corner(y0, x0 + 1, 1.0 - wy1, wx1) + corner(y0 + 1, x0, wy1, 1.0 - wx1) + corner(y0 + 1, x0 + 1, wy1, wx1)
        key = jax.random.key(seed)
        ks = jax.random.split(key, 8)
        B, Cin, H, W = (4, 1024, 64, 64)
        Cb = 256
        x = jax.random.normal(ks[0], (B, Cin, H, W), dtype=jnp.float32)
        w1 = jax.random.normal(ks[1], (Cb, Cin, 1, 1), dtype=jnp.float32) * (1.0 / np.sqrt(Cin))
        w_off = jax.random.normal(ks[2], (27, Cb, 3, 3), dtype=jnp.float32) * 0.01
        b_off = jnp.zeros((27,), dtype=jnp.float32)
        w2 = jax.random.normal(ks[3], (Cb, Cb, 3, 3), dtype=jnp.float32) * (1.0 / np.sqrt(Cb * 9))
        w3 = jax.random.normal(ks[4], (Cin, Cb, 1, 1), dtype=jnp.float32) * (1.0 / np.sqrt(Cb))
        return {'x': x, 'w1': w1, 'gn1_scale': jnp.ones((Cb,), jnp.float32), 'gn1_bias': jnp.zeros((Cb,), jnp.float32), 'w_off': w_off, 'b_off': b_off, 'w2': w2, 'gn2_scale': jnp.ones((Cb,), jnp.float32), 'gn2_bias': jnp.zeros((Cb,), jnp.float32), 'w3': w3, 'gn3_scale': jnp.ones((Cin,), jnp.float32), 'gn3_bias': jnp.zeros((Cin,), jnp.float32), 'stride': 4}
    _L1_conv_all = _L1_conv_setup()
    _L1_conv_in = {k: v for k, v in _L1_conv_all.items() if k in ('w1', 'gn1_scale', 'gn1_bias', 'w_off', 'b_off', 'w2', 'gn2_scale', 'gn2_bias', 'w3', 'gn3_scale', 'gn3_bias', )}
    del _L1_conv_all

    return {
        "x": x,
        "L0_conv_w1": _L0_conv_in["w1"],
        "L0_conv_b1": _L0_conv_in["b1"],
        "L0_conv_g1": _L0_conv_in["g1"],
        "L0_conv_be1": _L0_conv_in["be1"],
        "L0_conv_w2": _L0_conv_in["w2"],
        "L0_conv_b2": _L0_conv_in["b2"],
        "L0_conv_g2": _L0_conv_in["g2"],
        "L0_conv_be2": _L0_conv_in["be2"],
        "L0_conv_w3": _L0_conv_in["w3"],
        "L0_conv_b3": _L0_conv_in["b3"],
        "L0_conv_g3": _L0_conv_in["g3"],
        "L0_conv_be3": _L0_conv_in["be3"],
        "L0_conv_residual_scale": _L0_conv_in["residual_scale"],
        "L1_conv_w1": _L1_conv_in["w1"],
        "L1_conv_gn1_scale": _L1_conv_in["gn1_scale"],
        "L1_conv_gn1_bias": _L1_conv_in["gn1_bias"],
        "L1_conv_w_off": _L1_conv_in["w_off"],
        "L1_conv_b_off": _L1_conv_in["b_off"],
        "L1_conv_w2": _L1_conv_in["w2"],
        "L1_conv_gn2_scale": _L1_conv_in["gn2_scale"],
        "L1_conv_gn2_bias": _L1_conv_in["gn2_bias"],
        "L1_conv_w3": _L1_conv_in["w3"],
        "L1_conv_gn3_scale": _L1_conv_in["gn3_scale"],
        "L1_conv_gn3_bias": _L1_conv_in["gn3_bias"],
    }

def reference(x, L0_conv_w1, L0_conv_b1, L0_conv_g1, L0_conv_be1, L0_conv_w2, L0_conv_b2, L0_conv_g2, L0_conv_be2, L0_conv_w3, L0_conv_b3, L0_conv_g3, L0_conv_be3, L0_conv_residual_scale, L1_conv_w1, L1_conv_gn1_scale, L1_conv_gn1_bias, L1_conv_w_off, L1_conv_b_off, L1_conv_w2, L1_conv_gn2_scale, L1_conv_gn2_bias, L1_conv_w3, L1_conv_gn3_scale, L1_conv_gn3_bias):
    import jax
    import jax.numpy as jnp
    def _L0_conv_ref(x, w1, b1, g1, be1, w2, b2, g2, be2, w3, b3, g3, be3, residual_scale):
        import jax, jax.numpy as jnp
        import numpy as np
        EPS = 1e-05

        def _conv(x, w, b, stride, pad):
            y = jax.lax.conv_general_dilated(x, w, window_strides=(stride, stride), padding=[(pad, pad), (pad, pad)], dimension_numbers=('NCHW', 'OIHW', 'NCHW'))
            return y + b.reshape(1, -1, 1, 1)

        def _bn(x, gamma, beta):
            mean = jnp.mean(x, axis=(0, 2, 3), keepdims=True)
            var = jnp.var(x, axis=(0, 2, 3), keepdims=True)
            xn = (x - mean) * jax.lax.rsqrt(var + EPS)
            return gamma.reshape(1, -1, 1, 1) * xn + beta.reshape(1, -1, 1, 1)
        out = jax.nn.relu(_bn(_conv(x, w1, b1, 1, 0), g1, be1))
        out = jax.nn.relu(_bn(_conv(out, w2, b2, 1, 1), g2, be2))
        out = _bn(_conv(out, w3, b3, 1, 0), g3, be3)
        out = jax.nn.softplus(residual_scale)[0] * out
        out = x + out
        return jax.nn.relu(out)

    def _L1_conv_ref(x, w1, gn1_scale, gn1_bias, w_off, b_off, w2, gn2_scale, gn2_bias, w3, gn3_scale, gn3_bias, stride):
        import jax, jax.numpy as jnp
        import numpy as np

        def conv(x, w, stride=1, pad=0):
            return jax.lax.conv_general_dilated(x, w, (stride, stride), [(pad, pad), (pad, pad)], dimension_numbers=('NCHW', 'OIHW', 'NCHW'))

        def group_norm(x, scale, bias, groups=32, eps=1e-05):
            B, C, H, W = x.shape
            xg = x.reshape(B, groups, C // groups, H, W)
            m = xg.mean(axis=(2, 3, 4), keepdims=True)
            v = xg.var(axis=(2, 3, 4), keepdims=True)
            xn = ((xg - m) * jax.lax.rsqrt(v + eps)).reshape(B, C, H, W)
            return xn * scale[None, :, None, None] + bias[None, :, None, None]

        def bilinear_sample(x, py, px):
            B, C, H, W = x.shape
            y0 = jnp.floor(py)
            x0 = jnp.floor(px)
            wy1 = py - y0
            wx1 = px - x0
            xf = x.reshape(B, C, H * W)
            Ksp = py.shape[1:]

            def corner(yi, xi, wy, wx):
                valid = (yi >= 0) & (yi < H) & (xi >= 0) & (xi < W)
                yc = jnp.clip(yi, 0, H - 1).astype(jnp.int32)
                xc = jnp.clip(xi, 0, W - 1).astype(jnp.int32)
                idx = (yc * W + xc).reshape(B, 1, -1)
                v = jnp.take_along_axis(xf, idx, axis=2).reshape(B, C, *Ksp)
                w = (wy * wx * valid).astype(x.dtype)[:, None]
                return v * w
            return corner(y0, x0, 1.0 - wy1, 1.0 - wx1) + corner(y0, x0 + 1, 1.0 - wy1, wx1) + corner(y0 + 1, x0, wy1, 1.0 - wx1) + corner(y0 + 1, x0 + 1, wy1, wx1)
        out = conv(x, w1)
        out = jax.nn.relu(group_norm(out, gn1_scale, gn1_bias))
        om = conv(out, w_off, pad=1) + b_off[None, :, None, None]
        K = 9
        off_x = om[:, :K]
        off_y = om[:, K:2 * K]
        mask = jax.nn.sigmoid(om[:, 2 * K:])
        B, C, H, W = out.shape
        ky, kx = jnp.meshgrid(jnp.arange(3), jnp.arange(3), indexing='ij')
        ky = (ky.reshape(K) - 1).astype(om.dtype)
        kx = (kx.reshape(K) - 1).astype(om.dtype)
        grid_y = jnp.arange(H, dtype=om.dtype)[None, :, None] + ky[:, None, None]
        grid_x = jnp.arange(W, dtype=om.dtype)[None, None, :] + kx[:, None, None]
        py = grid_y[None] + off_y
        px = grid_x[None] + off_x
        sampled = bilinear_sample(out, py, px) * mask[:, None]
        out = jnp.einsum('bckhw,ock->bohw', sampled, w2.reshape(w2.shape[0], w2.shape[1], K))
        out = jax.nn.relu(group_norm(out, gn2_scale, gn2_bias))
        out = conv(out, w3)
        out = group_norm(out, gn3_scale, gn3_bias)
        return jax.nn.relu(out + x)

    def _gn(v, G=32, eps=1e-5):
        B_, C_, H_, W_ = v.shape
        g = v.reshape(B_, G, C_ // G, H_, W_)
        m = jnp.mean(g, axis=(2, 3, 4), keepdims=True)
        s = jnp.var(g, axis=(2, 3, 4), keepdims=True)
        return ((g - m) / jnp.sqrt(s + eps)).reshape(v.shape)

    def _ln_c(v, eps=1e-6):
        m = jnp.mean(v, axis=1, keepdims=True)
        s = jnp.var(v, axis=1, keepdims=True)
        return (v - m) / jnp.sqrt(s + eps)

    def _ln_t(v, eps=1e-5):
        m = jnp.mean(v, axis=-1, keepdims=True)
        s = jnp.var(v, axis=-1, keepdims=True)
        return (v - m) / jnp.sqrt(s + eps)

    def _to_tokens(v):
        B_, C_, H_, W_ = v.shape
        return v.reshape(B_, C_, H_ * W_).transpose(0, 2, 1)
    def _from_tokens(t, like):
        B_, C_, H_, W_ = like.shape
        return t.transpose(0, 2, 1).reshape(B_, C_, H_, W_)

    x = _L0_conv_ref(x, L0_conv_w1, L0_conv_b1, L0_conv_g1, L0_conv_be1, L0_conv_w2, L0_conv_b2, L0_conv_g2, L0_conv_be2, L0_conv_w3, L0_conv_b3, L0_conv_g3, L0_conv_be3, L0_conv_residual_scale)
    x = _L1_conv_ref(x, L1_conv_w1, L1_conv_gn1_scale, L1_conv_gn1_bias, L1_conv_w_off, L1_conv_b_off, L1_conv_w2, L1_conv_gn2_scale, L1_conv_gn2_bias, L1_conv_w3, L1_conv_gn3_scale, L1_conv_gn3_bias, 4)
    return x


_drawn_inputs = setup_inputs


def setup_inputs(seed=0):
    import zlib

    import numpy as np

    out = dict(_drawn_inputs(seed))
    spreads = {'L0_conv_b1': (0.0, 0.1),
     'L0_conv_g1': (1.0, 0.2),
     'L0_conv_be1': (0.0, 0.1),
     'L0_conv_b2': (0.0, 0.1),
     'L0_conv_g2': (1.0, 0.2),
     'L0_conv_be2': (0.0, 0.1),
     'L0_conv_b3': (0.0, 0.1),
     'L0_conv_g3': (1.0, 0.2),
     'L0_conv_be3': (0.0, 0.1),
     'L1_conv_gn1_scale': (1.0, 0.2),
     'L1_conv_gn1_bias': (0.0, 0.1),
     'L1_conv_b_off': (0.0, 0.1),
     'L1_conv_gn2_scale': (1.0, 0.2),
     'L1_conv_gn2_bias': (0.0, 0.1),
     'L1_conv_gn3_scale': (1.0, 0.2),
     'L1_conv_gn3_bias': (0.0, 0.1)}
    factors = {}
    for name, (base, spread) in spreads.items():
        noise = np.random.default_rng([zlib.crc32(name.encode()), seed]).standard_normal(out[name].shape)
        drawn = base * np.exp(spread * noise) if base else spread * noise
        out[name] = jnp.asarray(drawn.astype(out[name].dtype))
    for name, factor in factors.items():
        out[name] = (out[name] * factor).astype(out[name].dtype)
    return out
```

```python
from contextlib import ExitStack

import concourse.bass as bass
from concourse import mybir

F32 = mybir.dt.float32
F32R = mybir.dt.float32r
ALU = mybir.AluOpType
ACT = mybir.ActivationFunctionType
AX_X = mybir.AxisListType.X

P = 128
NIMG, CIN, CMID, SIDE = 64, 1024, 256, 14
PIX = SIDE * SIDE
PAIR = 2 * PIX
PAIRS = NIMG // 2
KX = CIN // P
KM = CMID // P
TAPS = 9
EPS = 1e-5
PAD = SIDE + 2
BANK = 512
HALF = PIX // 2
ROWS = SIDE // 2
GROUPS = 5
UNITS = 2 * GROUPS
TILES = 2 * UNITS
OFFCH = 27
RING = 4
POOL_UNITS = (0, 2, 4, 6, 8)


def at_least(eng, sem, value):
    if not isinstance(value, int) or value > 0:
        eng.wait_ge(sem, value)


def at_least_alone(eng, sem, value, past):
    if not isinstance(value, int):
        eng.wait_ge(past[0], past[1])
    at_least(eng, sem, value)


def product3(nc, out, w_hi, w_lo, x_hi, x_lo, start, stop):
    nc.tensor.matmul(out, w_hi, x_hi, start=start, stop=False)
    nc.tensor.matmul(out, w_hi, x_lo, start=False, stop=False)
    return nc.tensor.matmul(out, w_lo, x_hi, start=False, stop=stop)


def by_two(eng, step, unrolled=1):
    for lap in range(unrolled):
        step(2 * lap, lap, 0)
        step(2 * lap + 1, lap, 1)
    with eng.Fori(unrolled, PAIRS // 2) as lap:
        step(2 * lap, lap, 0)
        step(2 * lap + 1, lap, 1)


def split_weights(nc, ctx, name, source, shape, prior=None):
    hi = ctx.enter_context(nc.sbuf_tensor(name + "_hi", [P] + shape, F32R))
    lo = ctx.enter_context(nc.sbuf_tensor(name + "_lo", [P] + shape, F32R))
    letters = "abcd"[: len(shape)]
    flat = f"p {' '.join(letters)} -> p ({' '.join(letters)})" if len(shape) > 1 else None
    count = 1
    for n in shape:
        count *= n

    def view(t):
        return t[:].rearrange(flat) if flat else t[:]

    with ExitStack() as inner:
        stage = inner.enter_context(nc.sbuf_tensor(name + "_stage", [P, count], F32))
        loaded = inner.enter_context(nc.semaphore(name + "_loaded"))
        hi_made = inner.enter_context(nc.semaphore(name + "_hi_made"))
        block = inner.enter_context(nc.Block())

        @block.sync
        def _(sp):
            sp.dma_start(stage[:], source).then_inc(loaded, 16)

        @block.scalar
        def _(act):
            act.wait_ge(loaded, 16)
            nc.scalar.activation(view(hi), stage[:], ACT.Copy).then_inc(hi_made, 1)

        @block.vector
        def _(dve):
            dve.wait_ge(hi_made, 1)
            nc.vector.tensor_tensor(view(lo), stage[:], view(hi).bitcast(F32), ALU.subtract)

    return hi, lo


def bn_coefficients(nc, name, stats, tiles, gamma, beta, bias, half_neg, scale, shift, residual=None):
    with ExitStack() as ctx:
        mv = ctx.enter_context(nc.sbuf_tensor(name + "_mv", [P, tiles, 2], F32))
        var = ctx.enter_context(nc.sbuf_tensor(name + "_var", [P, tiles], F32))
        rstd = ctx.enter_context(nc.sbuf_tensor(name + "_rstd", [P, tiles], F32))
        mean = ctx.enter_context(nc.sbuf_tensor(name + "_mean", [P, tiles], F32))
        soft = ctx.enter_context(nc.sbuf_tensor(name + "_soft", [P, 4], F32))
        step = ctx.enter_context(nc.semaphore(name + "_step"))
        var_ready = ctx.enter_context(nc.semaphore(name + "_var_ready"))
        rstd_ready = ctx.enter_context(nc.semaphore(name + "_rstd_ready"))
        soft_abs = ctx.enter_context(nc.semaphore(name + "_soft_abs"))
        soft_exp = ctx.enter_context(nc.semaphore(name + "_soft_exp"))
        soft_ln = ctx.enter_context(nc.semaphore(name + "_soft_ln"))
        block = ctx.enter_context(nc.Block())

        @block.scalar
        def _(act):
            if residual is not None:
                nc.scalar.activation(soft[:, 0:1], residual, ACT.Abs).then_inc(soft_abs, 1)
                act.wait_ge(soft_abs, 1)
                nc.scalar.activation(soft[:, 1:2], soft[:, 0:1], ACT.Exp, scale=-1.0).then_inc(soft_exp, 1)
                act.wait_ge(soft_exp, 1)
                nc.scalar.activation(soft[:, 2:3], soft[:, 1:2], ACT.Ln, bias=1.0).then_inc(soft_ln, 1)

        @block.gpsimd
        def _(pool):
            pool.wait_ge(var_ready, 1)
            nc.gpsimd.tensor_tensor(rstd[:], var[:], half_neg[:, 0:tiles], ALU.pow).then_inc(rstd_ready, 1)

        @block.vector
        def _(dve):
            done = [0]

            def then(ins):
                done[0] += 1
                ins.then_inc(step, 1)
                dve.wait_ge(step, done[0])

            for t in range(tiles):
                last = nc.vector.bn_aggr(mv[:, t, :], stats[:, t, :, :].rearrange("p a b -> p (a b)"))
            then(last)
            nc.vector.tensor_scalar(var[:], mv[:, :, 1], EPS, None, ALU.add).then_inc(var_ready, 1)
            then(nc.vector.tensor_tensor(mean[:], mv[:, :, 0], bias, ALU.add))
            dve.wait_ge(rstd_ready, 1)
            then(nc.vector.tensor_tensor(scale[:], rstd[:], gamma, ALU.mult))
            then(nc.vector.tensor_tensor(mean[:], bias, mean[:], ALU.subtract))
            then(nc.vector.tensor_tensor(mean[:], mean[:], scale[:], ALU.mult))
            then(nc.vector.tensor_tensor(shift[:], mean[:], beta, ALU.add))
            if residual is not None:
                dve.wait_ge(soft_ln, 1)
                then(nc.vector.scalar_tensor_tensor(soft[:, 3:4], residual, 0.0, soft[:, 2:3], ALU.max, ALU.add))
                then(nc.vector.tensor_scalar(scale[:], scale[:], soft[:, 3:4], None, ALU.mult))
                then(nc.vector.tensor_scalar(shift[:], shift[:], soft[:, 3:4], None, ALU.mult))


def conv1_phase(nc, x, w1, h, stats):
    with ExitStack() as ctx:
        w_hi, w_lo = split_weights(nc, ctx, "w1a", w1, [KX, KM, P])
        x_in = ctx.enter_context(nc.sbuf_tensor("x_in", [P, 2, 2, KX, PIX], F32))
        x_hi = ctx.enter_context(nc.sbuf_tensor("x_hi", [P, 2, 2, KX // 2, PIX], F32R))
        x_lo = ctx.enter_context(nc.sbuf_tensor("x_lo", [P, 2, 2, KX // 2, PIX], F32R))
        acc = ctx.enter_context(nc.psum_tensor("conv1_acc", [P, 2, KM, BANK], F32))
        x_loaded = [ctx.enter_context(nc.semaphore(f"x_loaded{s}")) for s in range(2)]
        hi_made = ctx.enter_context(nc.semaphore("x_hi_made"))
        lo_made = ctx.enter_context(nc.semaphore("x_lo_made"))
        half_multiplied = ctx.enter_context(nc.semaphore("half_multiplied"))
        h_written = ctx.enter_context(nc.semaphore("h_written"))
        hk = KX // 2
        block = ctx.enter_context(nc.Block())

        @block.sync
        def _(sp):
            def load(pair, lap, slot):
                at_least_alone(sp, lo_made, 2 * (pair - 1), (lo_made, 1))
                sp.dma_start(x_in[:, slot].rearrange("p i k s -> p i (k s)"), x[pair]).then_inc(x_loaded[slot], 16)
            by_two(sp, load)

        @block.scalar
        def _(act):
            def write_h(pair, slot):
                at_least_alone(act, half_multiplied, 2 * pair + 2, (hi_made, 1))
                nc.scalar.activation(h[:, :, bass.ds(pair * PAIR, PAIR)], acc[:, slot, :, 0:PAIR],
                                     ACT.Copy).then_inc(h_written, 1)

            def step(pair, lap, slot):
                act.wait_ge(x_loaded[slot], 16 * (lap + 1))
                for f in range(2):
                    at_least(act, half_multiplied, 2 * pair - 1 + f)
                    nc.scalar.activation(x_hi[:, f].rearrange("p i k s -> p i (k s)"),
                                         x_in[:, slot, :, f * hk:(f + 1) * hk].rearrange("p i k s -> p i (k s)"),
                                         ACT.Copy).then_inc(hi_made, 1)
                if not isinstance(pair, int) or pair > 0:
                    write_h(pair - 1, 1 - slot)
            by_two(act, step)
            write_h(PAIRS - 1, (PAIRS - 1) % 2)

        @block.vector
        def _(dve):
            def count(pair):
                at_least(dve, h_written, pair + 1)
                for t in range(KM):
                    nc.vector.bn_stats(stats[:, t, bass.ds(pair, 1), :].rearrange("p a b -> p (a b)"),
                                       h[:, t, bass.ds(pair * PAIR, PAIR)])

            def step(pair, lap, slot):
                for f in range(2):
                    at_least(dve, hi_made, 2 * pair + f + 1)
                    at_least(dve, half_multiplied, 2 * pair - 1 + f)
                    nc.vector.tensor_tensor(x_lo[:, f].rearrange("p i k s -> p i (k s)"),
                                            x_in[:, slot, :, f * hk:(f + 1) * hk].rearrange("p i k s -> p i (k s)"),
                                            x_hi[:, f].rearrange("p i k s -> p i (k s)").bitcast(F32),
                                            ALU.subtract).then_inc(lo_made, 1)
                if not isinstance(pair, int) or pair > 0:
                    count(pair - 1)
            by_two(dve, step)
            count(PAIRS - 1)

        @block.tensor
        def _(pe):
            def step(pair, lap, slot):
                at_least(pe, h_written, pair - 1)
                for f in range(2):
                    at_least(pe, lo_made, 2 * pair + f + 1)
                    for t in range(KM):
                        for k in range(hk):
                            last = product3(nc, acc[:, slot, t, 0:PAIR].rearrange("p (i s) -> p i s", i=2),
                                            w_hi[:, f * hk + k, t, :], w_lo[:, f * hk + k, t, :],
                                            x_hi[:, f, :, k, :], x_lo[:, f, :, k, :],
                                            start=(f == 0 and k == 0), stop=(f == 1 and k == hk - 1))
                    last.then_inc(half_multiplied, 1)
            by_two(pe, step)


def conv2_phase(nc, w2, h, scale, shift, stats):
    with ExitStack() as ctx:
        w_hi, w_lo = split_weights(nc, ctx, "w2a", w2, [KM, TAPS, KM, P])
        act_f = ctx.enter_context(nc.sbuf_tensor("act_f", [P, 2, KM, PAIR], F32))
        pad_hi = ctx.enter_context(nc.sbuf_tensor("pad_hi", [P, 2, 2 * KM, PAD, PAD], F32R))
        pad_lo = ctx.enter_context(nc.sbuf_tensor("pad_lo", [P, 2, 2 * KM, PAD, PAD], F32R))
        acc = ctx.enter_context(nc.psum_tensor("conv2_acc", [P, 2, KM, BANK], F32))
        cleared = ctx.enter_context(nc.semaphore("pads_cleared"))
        act_made = ctx.enter_context(nc.semaphore("act_made"))
        hi_made = ctx.enter_context(nc.semaphore("pad_hi_made"))
        lo_made = ctx.enter_context(nc.semaphore("pad_lo_made"))
        multiplied = ctx.enter_context(nc.semaphore("conv2_multiplied"))
        h_written = ctx.enter_context(nc.semaphore("h_rewritten"))
        block = ctx.enter_context(nc.Block())

        def inside(t, slot):
            return t[:, slot, :, 1:1 + SIDE, 1:1 + SIDE]

        def squares(t):
            return t.rearrange("p k (i y x) -> p (k i) y x", i=2, y=SIDE)

        @block.scalar
        def _(act):
            act.wait_ge(cleared, 1)

            def write_h(pair, slot):
                at_least_alone(act, multiplied, pair + 1, (lo_made, 1))
                nc.scalar.activation(h[:, :, bass.ds(pair * PAIR, PAIR)], acc[:, slot, :, 0:PAIR],
                                     ACT.Copy).then_inc(h_written, 1)

            def step(pair, lap, slot):
                at_least_alone(act, lo_made, pair - 1, (hi_made, 1))
                for t in range(KM):
                    last = nc.scalar.activation(act_f[:, slot, t, :], h[:, t, bass.ds(pair * PAIR, PAIR)], ACT.Relu,
                                                bias=shift[:, t:t + 1], scale=scale[:, t:t + 1])
                last.then_inc(act_made, 1)
                at_least(act, act_made, pair + 1)
                at_least(act, multiplied, pair - 1)
                nc.scalar.activation(inside(pad_hi, slot), squares(act_f[:, slot]), ACT.Copy).then_inc(hi_made, 1)
                if not isinstance(pair, int) or pair > 0:
                    write_h(pair - 1, 1 - slot)
            by_two(act, step)
            write_h(PAIRS - 1, (PAIRS - 1) % 2)

        @block.vector
        def _(dve):
            nc.vector.memset(pad_hi[:].bitcast(F32), 0.0)
            nc.vector.memset(pad_lo[:].bitcast(F32), 0.0).then_inc(cleared, 1)
            dve.wait_ge(cleared, 1)

            def count(pair):
                at_least(dve, h_written, pair + 1)
                for t in range(KM):
                    nc.vector.bn_stats(stats[:, t, bass.ds(pair, 1), :].rearrange("p a b -> p (a b)"),
                                       h[:, t, bass.ds(pair * PAIR, PAIR)])

            def step(pair, lap, slot):
                at_least(dve, hi_made, pair + 1)
                at_least(dve, multiplied, pair - 1)
                nc.vector.tensor_tensor(inside(pad_lo, slot), squares(act_f[:, slot]),
                                        inside(pad_hi, slot).bitcast(F32), ALU.subtract).then_inc(lo_made, 1)
                if not isinstance(pair, int) or pair > 0:
                    count(pair - 1)
            by_two(dve, step)
            count(PAIRS - 1)

        @block.tensor
        def _(pe):
            def step(pair, lap, slot):
                at_least(pe, h_written, pair - 1)
                at_least(pe, lo_made, pair + 1)
                for t in range(KM):
                    for k in range(KM):
                        for tap in range(TAPS):
                            y, z = divmod(tap, 3)
                            last = product3(nc, acc[:, slot, t, 0:PAIR].rearrange("p (i y x) -> p i y x", i=2, y=SIDE),
                                            w_hi[:, k, tap, t, :], w_lo[:, k, tap, t, :],
                                            pad_hi[:, slot, 2 * k:2 * k + 2, y:y + SIDE, z:z + SIDE],
                                            pad_lo[:, slot, 2 * k:2 * k + 2, y:y + SIDE, z:z + SIDE],
                                            start=(k == 0 and tap == 0), stop=(k == KM - 1 and tap == TAPS - 1))
                last.then_inc(multiplied, 1)
            by_two(pe, step)


def conv3_phase(nc, w3, h, scale, shift, stats, y3):
    with ExitStack() as ctx:
        w_hi, w_lo = split_weights(nc, ctx, "w3a", w3, [KM, KX, P])
        act_f = ctx.enter_context(nc.sbuf_tensor("act3_f", [P, 2, KM, PAIR], F32))
        act_hi = ctx.enter_context(nc.sbuf_tensor("act3_hi", [P, 2, KM, PAIR], F32R))
        act_lo = ctx.enter_context(nc.sbuf_tensor("act3_lo", [P, 2, KM, PAIR], F32R))
        y_out = ctx.enter_context(nc.sbuf_tensor("y_out", [P, 2, 2, KX, PIX], F32))
        acc = ctx.enter_context(nc.psum_tensor("conv3_acc", [P, KX, BANK], F32))
        act_made = ctx.enter_context(nc.semaphore("act3_made"))
        hi_made = ctx.enter_context(nc.semaphore("act3_hi_made"))
        lo_made = ctx.enter_context(nc.semaphore("act3_lo_made"))
        multiplied = ctx.enter_context(nc.semaphore("conv3_multiplied"))
        y_written = ctx.enter_context(nc.semaphore("y_written"))
        counted = ctx.enter_context(nc.semaphore("y_counted"))
        y_stored = [ctx.enter_context(nc.semaphore(f"y_stored{s}")) for s in range(2)]
        block = ctx.enter_context(nc.Block())

        @block.sync
        def _(sp):
            def store(pair, lap, slot):
                at_least_alone(sp, y_written, 4 * pair + 4, (y_written, 1))
                sp.dma_start(y3[pair], y_out[:, slot].rearrange("p i k s -> p i (k s)")).then_inc(y_stored[slot], 16)
            by_two(sp, store)
            for slot in range(2):
                sp.wait_ge(y_stored[slot], 16 * (PAIRS // 2))

        @block.scalar
        def _(act):
            def write_y(pair, lap, slot):
                at_least(act, y_stored[slot], 16 * lap)
                at_least(act, counted, pair - 1)
                for q in range(4):
                    at_least(act, multiplied, 4 * pair + q + 1)
                    nc.scalar.activation(
                        y_out[:, slot, :, 2 * q:2 * q + 2, :].rearrange("p i k s -> p k i s"),
                        acc[:, 2 * q:2 * q + 2, 0:PAIR].rearrange("p k (i s) -> p k i s", i=2),
                        ACT.Copy).then_inc(y_written, 1)

            def step(pair, lap, slot):
                at_least_alone(act, lo_made, pair - 1, (hi_made, 1))
                for t in range(KM):
                    last = nc.scalar.activation(act_f[:, slot, t, :], h[:, t, bass.ds(pair * PAIR, PAIR)], ACT.Relu,
                                                bias=shift[:, t:t + 1], scale=scale[:, t:t + 1])
                last.then_inc(act_made, 1)
                at_least(act, act_made, pair + 1)
                at_least(act, multiplied, 4 * (pair - 1))
                nc.scalar.activation(act_hi[:, slot], act_f[:, slot], ACT.Copy).then_inc(hi_made, 1)
                if not isinstance(pair, int) or pair > 0:
                    write_y(pair - 1, lap if slot else lap - 1, 1 - slot)
            by_two(act, step, unrolled=2)
            write_y(PAIRS - 1, PAIRS // 2 - 1, 1)

        @block.vector
        def _(dve):
            def count(pair, slot):
                for t in range(KX):
                    if t % 2 == 0:
                        at_least(dve, y_written, 4 * pair + t // 2 + 1)
                    last = nc.vector.bn_stats(stats[:, t, bass.ds(pair, 1), :].rearrange("p a b -> p (a b)"),
                                              y_out[:, slot, :, t, :])
                last.then_inc(counted, 1)

            def step(pair, lap, slot):
                at_least(dve, hi_made, pair + 1)
                at_least(dve, multiplied, 4 * (pair - 1))
                nc.vector.tensor_tensor(act_lo[:, slot], act_f[:, slot], act_hi[:, slot].bitcast(F32),
                                        ALU.subtract).then_inc(lo_made, 1)
                if not isinstance(pair, int) or pair > 0:
                    count(pair - 1, 1 - slot)
            by_two(dve, step)
            count(PAIRS - 1, 1)

        @block.tensor
        def _(pe):
            def step(pair, lap, slot):
                at_least(pe, lo_made, pair + 1)
                for t in range(KX):
                    if t % 2 == 0:
                        at_least(pe, y_written, 4 * (pair - 1) + t // 2 + 1)
                    for k in range(KM):
                        last = product3(nc, acc[:, t, 0:PAIR], w_hi[:, k, t, :], w_lo[:, k, t, :],
                                        act_hi[:, slot, k, :], act_lo[:, slot, k, :],
                                        start=(k == 0), stop=(k == KM - 1))
                    if t % 2:
                        last.then_inc(multiplied, 1)
            by_two(pe, step)


class Pair:

    def __init__(self, turn, c):
        self.n = 3 * turn + c
        self.buf = c % 3
        self.lap = turn + c // 3


def by_iteration(eng, step):
    def at(after):
        step(*(Pair(0, n) if 0 <= n < PAIRS else None for n in range(after - 2, after + 2)))

    turns = PAIRS // 3 - 1
    for after in range(-1, 3):
        at(after)
    with eng.Fori(0, turns) as turn:
        for after in range(3, 6):
            step(*(Pair(turn, n) for n in range(after - 2, after + 2)))
    for after in range(3 * (turns + 1), PAIRS + 2):
        at(after)


class GroupNorm:

    SQUARED, SUMMED_M2, REDUCED_MEAN, REDUCED, MOMENTS, MEAN2, VAR, SCALE, SHIFTED, COEF = range(1, 11)
    STEPS = 10

    def __init__(self, nc, ctx, name, tiles, gamma, beta):
        def sb(part, shape):
            return ctx.enter_context(nc.sbuf_tensor(f"{name}_{part}", [P] + shape, F32))
        self.nc, self.tiles, self.gamma, self.beta = nc, tiles, gamma, beta
        self.stats = sb("stats", [2, tiles, 6])
        self.square = sb("square", [2, tiles * 2])
        self.sums = sb("sums", [2, 2])
        self.moments = sb("moments", [2, 2])
        self.mean2 = sb("mean2", [2])
        self.var = sb("var", [2])
        self.rstd = sb("rstd", [2])
        self.scale = sb("scale", [2, tiles])
        self.product = sb("product", [2, tiles])
        self.shift = sb("shift", [2, tiles])
        self.done = ctx.enter_context(nc.semaphore(f"{name}_done"))
        self.counted = ctx.enter_context(nc.semaphore(f"{name}_counted"))
        self.grouped = ctx.enter_context(nc.semaphore(f"{name}_grouped"))
        self.rooted = ctx.enter_context(nc.semaphore(f"{name}_rooted"))

    def reduce(self, dve, n):
        nc, base = self.nc, self.STEPS * n
        parts = self.stats[:].rearrange("p i t (e k) -> p i (t e) k", k=3)
        dve.wait_ge(self.counted, n + 1)
        nc.vector.tensor_tensor(self.square[:], parts[:, :, :, 1], parts[:, :, :, 1],
                                ALU.mult).then_inc(self.done, 1)
        dve.wait_ge(self.done, base + self.SQUARED)
        nc.vector.scalar_tensor_tensor(self.square[:], parts[:, :, :, 2], 1.0 / HALF, self.square[:],
                                       ALU.mult, ALU.add).then_inc(self.done, 1)
        at_least(dve, self.grouped, n)
        nc.vector.tensor_reduce(self.sums[:, 0, :], parts[:, :, :, 1], AX_X, ALU.add).then_inc(self.done, 1)
        dve.wait_ge(self.done, base + self.SUMMED_M2)
        nc.vector.tensor_reduce(self.sums[:, 1, :], self.square[:], AX_X, ALU.add).then_inc(self.done, 1)

    def group(self, pe, n, ones, out):
        pe.wait_ge(self.done, self.STEPS * n + self.REDUCED)
        self.nc.tensor.matmul(out, ones[:], self.sums[:].rearrange("p m i -> p (m i)"), start=True,
                              stop=True).then_inc(self.grouped, 1)

    def root(self, pool, n, half_neg):
        pool.wait_ge(self.done, self.STEPS * n + self.VAR)
        self.nc.gpsimd.tensor_tensor(self.rstd[:], self.var[:], half_neg[:, 0:2], ALU.pow).then_inc(self.rooted, 1)

    def moments_of(self, dve, n, sums):
        nc, base = self.nc, self.STEPS * n
        dve.wait_ge(self.grouped, n + 1)
        nc.vector.tensor_scalar(self.moments[:].rearrange("p m i -> p (m i)"), sums, 1.0 / (4 * 2 * self.tiles), None,
                                ALU.mult).then_inc(self.done, 1)
        dve.wait_ge(self.done, base + self.MOMENTS)
        nc.vector.tensor_tensor(self.mean2[:], self.moments[:, 0, :], self.moments[:, 0, :],
                                ALU.mult).then_inc(self.done, 1)
        dve.wait_ge(self.done, base + self.MEAN2)
        nc.vector.scalar_tensor_tensor(self.var[:], self.moments[:, 1, :], EPS, self.mean2[:], ALU.add,
                                       ALU.subtract).then_inc(self.done, 1)

    def coefficients(self, dve, n):
        nc, base = self.nc, self.STEPS * n
        dve.wait_ge(self.rooted, n + 1)
        for i in range(2):
            last = nc.vector.tensor_scalar(self.scale[:, i, :], self.gamma, self.rstd[:, i:i + 1], None, ALU.mult)
        last.then_inc(self.done, 1)
        dve.wait_ge(self.done, base + self.SCALE)
        for i in range(2):
            last = nc.vector.tensor_scalar(self.product[:, i, :], self.scale[:, i, :], self.moments[:, 0, i:i + 1],
                                           None, ALU.mult)
        last.then_inc(self.done, 1)
        dve.wait_ge(self.done, base + self.SHIFTED)
        for i in range(2):
            last = nc.vector.tensor_tensor(self.shift[:, i, :], self.beta, self.product[:, i, :], ALU.subtract)
        last.then_inc(self.done, 1)


def deformable_phase(nc, x, y3, scale, shift, w, consts, sampled_at, hats_at, out):
    with ExitStack() as ctx:
        w1_hi, w1_lo = split_weights(nc, ctx, "w1b", w["w1"], [KX, KM, P])
        wo_hi, wo_lo = split_weights(nc, ctx, "wob", w["woff"], [KM, 3, 96])
        w2_hi, w2_lo = split_weights(nc, ctx, "w2b", w["w2"], [KM, TAPS, KM, P])
        w3_hi, w3_lo = split_weights(nc, ctx, "w3b", w["w3"], [KM, KX, P])

        def sb(name, shape, dt=F32):
            return ctx.enter_context(nc.sbuf_tensor(name, shape, dt))

        def ps(name, shape):
            return ctx.enter_context(nc.psum_tensor(name, shape, F32))

        def sem(name):
            return ctx.enter_context(nc.semaphore(name))

        x1 = sb("x1", [P, 3, 2, KX, PIX])
        x1_hi = sb("x1_hi", [P, RING, 2, PIX], F32R)
        x1_lo = sb("x1_lo", [P, RING, 2, PIX], F32R)
        a_f = sb("a_f", [P, KM, 2, PIX])
        a_hi = sb("a_hi", [P, KM, PAIR], F32R)
        a_lo = sb("a_lo", [P, KM, PAIR], F32R)
        aT_hi = sb("aT_hi", [HALF, 2, 2, CMID], F32R)
        aT_lo = sb("aT_lo", [HALF, 2, 2, CMID], F32R)
        om = sb("om", [OFFCH, 2, SIDE, SIDE])
        offs = sb("offs", [TAPS * SIDE, 3, 2, PIX])
        hats = sb("hats", [HALF, 2, 3, 2 * PIX])
        s_hi = sb("s_hi", [HALF, 2, 2, 2 * PIX], F32R)
        s_lo = sb("s_lo", [HALF, 2, 2, 2 * PIX], F32R)
        v_hi = sb("v_hi", [P, 2, KM, 2, 2, PIX], F32R)
        v_lo = sb("v_lo", [P, 2, KM, 2, 2, PIX], F32R)
        b_f = sb("b_f", [P, KM, 2, PIX])
        b_hi = sb("b_hi", [P, KM, PAIR], F32R)
        b_lo = sb("b_lo", [P, KM, PAIR], F32R)
        y = sb("y", [P, 2, KX, PIX])
        gn1 = GroupNorm(nc, ctx, "gn1", KM, consts["gn1_scale"], consts["gn1_bias"])
        gn2 = GroupNorm(nc, ctx, "gn2", KM, consts["gn2_scale"], consts["gn2_bias"])
        gn3 = GroupNorm(nc, ctx, "gn3", KX, consts["gn3_scale"], consts["gn3_bias"])

        waited = sb("waited", [P, 1])

        work = ps("work", [P, 3, BANK])
        sample = ps("sample", [P, 2, BANK])
        deform = ps("deform", [P, KM, BANK])
        sums = ps("sums_ps", [P, BANK])

        x_loaded = [[sem(f"x1_loaded{b}_{i}") for i in range(2)] for b in range(3)]
        y_loaded = sem("y_loaded")
        plus_y = sem("plus_y")
        x1_made = sem("x1_made")
        x1_hi_made = sem("x1_hi_made")
        x1_lo_made = sem("x1_lo_made")
        conv1_used = sem("conv1_used")
        a_raw = sem("a_raw")
        a_made = sem("a_made")
        a_hi_made = sem("a_hi_made")
        a_lo_made = sem("a_lo_made")
        offset_products = sem("offset_products")
        om_step = sem("om_step")
        om_stored = sem("om_stored")
        offs_loaded = sem("offs_loaded")
        distance = sem("distance")
        distance_abs = sem("distance_abs")
        hat_made = sem("hat_made")
        mask_made = sem("mask_made")
        masked = sem("masked")
        hats_stored = sem("hats_stored")
        hats_loaded = [sem(f"hats_loaded{s}") for s in range(2)]
        transposed = sem("transposed")
        aT_hi_made = sem("aT_hi_made")
        aT_lo_made = sem("aT_lo_made")
        s_made = [sem(f"s_made{s}") for s in range(2)]
        s_hi_made = sem("s_hi_made")
        s_lo_made = sem("s_lo_made")
        sampled = sem("sampled")
        v_hi_made = sem("v_hi_made")
        v_lo_made = sem("v_lo_made")
        deformed = sem("deformed")
        b_raw = sem("b_raw")
        b_made = sem("b_made")
        b_hi_made = sem("b_hi_made")
        b_lo_made = sem("b_lo_made")
        conv3_done = sem("conv3_done")
        y_written = sem("y_written")
        y_scaled = sem("y_scaled")
        added = sem("added")
        rectified = sem("rectified")
        scaled_by_act = sem("scaled_by_act")
        out_stored = [[sem(f"out_stored{b}_{i}") for i in range(2)] for b in range(3)]
        half_neg, ones, ident = consts["half_neg"], consts["ones"], consts["ident"]
        block = ctx.enter_context(nc.Block())

        def taps_of(g):
            return 2 if g < GROUPS - 1 else 1

        def cols(g):
            return taps_of(g) * PIX

        def make_weights(engine, eng, p, u):
            n = cols(u // 2)
            eng.wait_ge(hats_loaded[u % 2], 48 * (GROUPS * p.n + u // 2 + 1))
            engine.tensor_tensor(hats[:, u % 2, 0:2, 0:n], hats[:, u % 2, 0:2, 0:n],
                                 hats[:, u % 2, 2:3, 0:n].broadcast_to([HALF, 2, n]), ALU.mult).then_inc(s_made[u % 2], 1)

        @block.sync
        def _(sp):
            def load_y(p):
                at_least_alone(sp, added, 2 * (p.n - 2), (hats_stored, 16))
                sp.dma_start(y[:].rearrange("p i k s -> p i (k s)"), y3[p.n]).then_inc(y_loaded, 16)

            def load_hats(p, u):
                g, i = divmod(u, 2)
                slot, n = u % 2, cols(g)
                at_least(sp, s_lo_made, UNITS * p.n + u - 1)
                t0 = 2 * g * PIX
                for half in range(2):
                    src = hats_at[0, i, half * ROWS:(half + 1) * ROWS, t0:t0 + n]
                    sp.dma_start(hats[:, slot, half, 0:n], src.unsqueeze(1).broadcast_to([ROWS, SIDE, n])
                                 ).then_inc(hats_loaded[slot], 16)
                src = hats_at[1, i, :, t0:t0 + n]
                sp.dma_start(hats[:, slot, 2, 0:n], src.unsqueeze(0).broadcast_to([ROWS, SIDE, n])
                             ).then_inc(hats_loaded[slot], 16)

            def move_offsets(p):
                at_least(sp, hats_stored, 64 * p.n)
                sp.wait_ge(om_step, TAPS * (p.n + 1))
                sp.dma_start(sampled_at[:, :], om[:].rearrange("p i y x -> p (i y x)")).then_inc(om_stored, 16)
                sp.wait_ge(om_stored, 16 * (p.n + 1))
                for c, first in enumerate((TAPS, 0, 2 * TAPS)):
                    sp.dma_start(offs[:, c].rearrange("p i s -> p (i s)"),
                                 sampled_at[first:first + TAPS, :].unsqueeze(1).broadcast_to([TAPS, SIDE, PAIR])
                                 ).then_inc(offs_loaded, 16)

            def store_hats(p, now):
                if now is not None:
                    for s in range(2):
                        sp.wait_ge(hats_loaded[s], 48 * GROUPS * p.n)
                sp.wait_ge(masked, p.n + 1)
                for yx in range(2):
                    for i in range(2):
                        sp.dma_start(hats_at[yx, i].rearrange("q (k s) -> k q s", s=PIX), offs[:, yx, i, :]
                                     ).then_inc(hats_stored, 16)
                sp.wait_ge(hats_stored, 64 * (p.n + 1))

            def step(before, now, after, coming):
                if now is not None:
                    for u in range(2, UNITS):
                        load_hats(now, u)
                if after is not None:
                    move_offsets(after)
                if coming is not None:
                    load_y(coming)
                if after is not None:
                    store_hats(after, now)
                    load_hats(after, 0)
                    load_hats(after, 1)
            by_iteration(sp, step)

        @block.scalar
        def _(act):
            def load_x(p):
                for i in range(2):
                    at_least(act, out_stored[p.buf][i], 16 * p.lap)
                    act.dma_start(x1[:, p.buf, i].rearrange("p k s -> p (k s)"),
                                  x[p.n][:, i, :]).then_inc(x_loaded[p.buf][i], 16)

            def store_out(p, i):
                act.wait_ge(rectified, 2 * p.n + i + 1)
                act.dma_start(out[p.n][:, i, :], x1[:, p.buf, i].rearrange("p k s -> p (k s)")
                              ).then_inc(out_stored[p.buf][i], 16)

            def make_x1(p, k):
                at_least(act, plus_y, 8 * p.n + k + 1)
                nc.scalar.activation(x1[:, p.buf, :, k, :], x1[:, p.buf, :, k, :], ACT.Relu,
                                     bias=shift[:, k:k + 1]).then_inc(x1_made, 1)
                at_least(act, x1_made, 8 * p.n + k + 1)
                at_least(act, conv1_used, 8 * p.n + k + 1 - RING)
                nc.scalar.activation(x1_hi[:, k % RING], x1[:, p.buf, :, k, :], ACT.Copy).then_inc(x1_hi_made, 1)

            def raw_a(p):
                at_least(act, conv1_used, 8 * (p.n + 1))
                at_least(act, transposed, 2 * p.n)
                nc.scalar.activation(a_f[:].rearrange("p k i s -> p k (i s)"), work[:, 0:2, 0:PAIR],
                                     ACT.Copy).then_inc(a_raw, 1)

            def make_a(p):
                act.wait_ge(gn1.done, gn1.STEPS * p.n + gn1.COEF)
                for k in range(KM):
                    for i in range(2):
                        last = nc.scalar.activation(a_f[:, k, i, :], a_f[:, k, i, :], ACT.Relu,
                                                    bias=gn1.shift[:, i, k:k + 1], scale=gn1.scale[:, i, k:k + 1])
                last.then_inc(a_made, 1)
                act.wait_ge(a_made, p.n + 1)
                at_least(act, offset_products, p.n)
                nc.scalar.activation(a_hi[:], a_f[:].rearrange("p k i s -> p k (i s)"), ACT.Copy).then_inc(a_hi_made, 1)

            def make_hats(p):
                act.wait_ge(distance, p.n + 1)
                flat = offs[:, 0:2].rearrange("p c i s -> p (c i s)")
                nc.scalar.activation(flat, flat, ACT.Abs).then_inc(distance_abs, 1)
                act.wait_ge(distance_abs, p.n + 1)
                nc.scalar.activation(flat, flat, ACT.Relu, bias=1.0, scale=-1.0).then_inc(hat_made, 1)
                mask = offs[:, 2].rearrange("p i s -> p (i s)")
                nc.scalar.activation(mask, mask, ACT.Sigmoid).then_inc(mask_made, 1)

            def transposed_hi(p, i):
                act.wait_ge(transposed, 2 * p.n + i + 1)
                if i == 0:
                    at_least(act, deformed, GROUPS * p.n)
                nc.scalar.activation(aT_hi[:, i].rearrange("p h c -> p (h c)"), work[0:HALF, i, :],
                                     ACT.Copy).then_inc(aT_hi_made, 1)

            def weights_hi(p, u):
                g = u // 2
                at_least(act, s_made[u % 2], GROUPS * p.n + u // 2 + 1)
                at_least(act, sampled, TILES * p.n + 2 * (u - 1))
                nc.scalar.activation(s_hi[:, u % 2, :, 0:cols(g)], hats[:, u % 2, 0:2, 0:cols(g)],
                                     ACT.Copy).then_inc(s_hi_made, 1)

            def sampled_hi(p, t):
                g, i, c = t // 4, t // 2 % 2, t % 2
                at_least(act, sampled, TILES * p.n + t + 1)
                if t % 4 == 0:
                    at_least(act, deformed, GROUPS * p.n + (g - 1 if g > 1 else 0))
                nc.scalar.activation(v_hi[:, g % 2, c, 0:taps_of(g), i, :],
                                     sample[:, t % 2, 0:cols(g)].rearrange("p (k s) -> p k s", s=PIX),
                                     ACT.Copy).then_inc(v_hi_made, 1)

            def raw_b(p):
                act.wait_ge(deformed, GROUPS * (p.n + 1))
                nc.scalar.activation(b_f[:].rearrange("p k i s -> p k (i s)"), deform[:, :, 0:PAIR],
                                     ACT.Copy).then_inc(b_raw, 1)

            def make_b(p):
                act.wait_ge(gn2.done, gn2.STEPS * p.n + gn2.COEF)
                for k in range(KM):
                    for i in range(2):
                        last = nc.scalar.activation(b_f[:, k, i, :], b_f[:, k, i, :], ACT.Relu,
                                                    bias=gn2.shift[:, i, k:k + 1], scale=gn2.scale[:, i, k:k + 1])
                last.then_inc(b_made, 1)
                act.wait_ge(b_made, p.n + 1)
                at_least(act, conv3_done, 8 * p.n)
                nc.scalar.activation(b_hi[:], b_f[:].rearrange("p k i s -> p k (i s)"), ACT.Copy).then_inc(b_hi_made, 1)

            def write_y(p, k, after):
                if k == 0 and after is not None:
                    at_least(act, plus_y, 8 * (after.n + 1))
                elif k == 0:
                    at_least(act, added, 2 * p.n)
                at_least(act, conv3_done, 8 * p.n + k + 1)
                nc.scalar.activation(y[:, :, k, :], work[:, (k + 2) % 3, 0:PAIR].rearrange("p (i s) -> p i s", i=2),
                                     ACT.Copy).then_inc(y_written, 1)

            def scale_y(p):
                act.wait_ge(gn3.done, gn3.STEPS * p.n + gn3.COEF)
                for k in range(KX):
                    last = nc.scalar.activation(y[:, 1, k, :], y[:, 1, k, :], ACT.Identity,
                                                bias=gn3.shift[:, 1, k:k + 1], scale=gn3.scale[:, 1, k:k + 1])
                last.then_inc(scaled_by_act, 1)

            def rectify(p, i):
                act.wait_ge(added, 2 * p.n + i + 1)
                flat = x1[:, p.buf, i].rearrange("p k s -> p (k s)")
                nc.scalar.activation(flat, flat, ACT.Relu).then_inc(rectified, 1)

            def step(before, now, after, coming):
                if before is not None:
                    raw_b(before)
                for k in range(4, KX):
                    if after is not None:
                        make_x1(after, k)
                    if k % 2 and now is not None:
                        weights_hi(now, k // 2 - 2)
                if before is not None:
                    make_b(before)
                if after is not None:
                    raw_a(after)
                for t in range(4):
                    if now is not None:
                        sampled_hi(now, t)
                    if before is not None and t:
                        write_y(before, 2 * t - 2, after)
                        write_y(before, 2 * t - 1, after)
                    if t == 2 and now is not None:
                        weights_hi(now, 2)
                if now is not None:
                    weights_hi(now, 3)
                if before is not None:
                    write_y(before, 6, after)
                    write_y(before, 7, after)
                for t in range(4, TILES):
                    if now is not None:
                        sampled_hi(now, t)
                        if t % 2 and t < 16:
                            weights_hi(now, t // 2 + 2)
                    if t == 4 and after is not None:
                        make_a(after)
                    if t == 6 and before is not None:
                        scale_y(before)
                    if t in (12, 13) and before is not None:
                        rectify(before, t - 12)
                    if t in (13, 14) and before is not None:
                        store_out(before, t - 13)
                    if t == 15 and coming is not None:
                        load_x(coming)
                    if t == 15 and after is not None:
                        make_hats(after)
                    if t >= 16 and coming is not None:
                        make_x1(coming, t - 16)
                if after is not None:
                    transposed_hi(after, 0)
                    transposed_hi(after, 1)
            by_iteration(act, step)
            for b in range(3):
                for i in range(2):
                    act.wait_ge(out_stored[b][i], 16 * ((PAIRS - b + 2) // 3))

        @block.gpsimd
        def _(pool):
            def scale_y(p):
                pool.wait_ge(gn3.done, gn3.STEPS * p.n + gn3.COEF)
                nc.gpsimd.tensor_tensor(waited[:], gn3.scale[:, 0, 0:1], gn3.shift[:, 0, 0:1], ALU.mult)
                for k in range(KX):
                    last = nc.gpsimd.tensor_scalar(y[:, 0, k, :], y[:, 0, k, :], gn3.scale[:, 0, k:k + 1],
                                                   gn3.shift[:, 0, k:k + 1], ALU.mult, ALU.add)
                last.then_inc(y_scaled, 1)

            def step(before, now, after, coming):
                if before is not None:
                    gn2.root(pool, before.n, half_neg)
                if now is not None:
                    for u in range(4):
                        if u in POOL_UNITS:
                            make_weights(nc.gpsimd, pool, now, u)
                if after is not None:
                    gn1.root(pool, after.n, half_neg)
                if now is not None and 4 in POOL_UNITS:
                    make_weights(nc.gpsimd, pool, now, 4)
                if before is not None:
                    gn3.root(pool, before.n, half_neg)
                    scale_y(before)
                if now is not None:
                    for u in range(5, UNITS):
                        if u in POOL_UNITS:
                            make_weights(nc.gpsimd, pool, now, u)
            by_iteration(pool, step)

        @block.vector
        def _(dve):
            def add_y(p, k):
                if k == 0:
                    for i in range(2):
                        dve.wait_ge(x_loaded[p.buf][i], 16 * (p.lap + 1))
                    dve.wait_ge(y_loaded, 16 * (p.n + 1))
                nc.vector.scalar_tensor_tensor(x1[:, p.buf, :, k, :], y[:, :, k, :],
                                               scale[:, k:k + 1], x1[:, p.buf, :, k, :], ALU.mult,
                                               ALU.add).then_inc(plus_y, 1)

            def x1_rest(p, k):
                at_least(dve, x1_hi_made, 8 * p.n + k + 1)
                at_least(dve, conv1_used, 8 * p.n + k + 1 - RING)
                nc.vector.tensor_tensor(x1_lo[:, k % RING], x1[:, p.buf, :, k, :], x1_hi[:, k % RING].bitcast(F32),
                                        ALU.subtract).then_inc(x1_lo_made, 1)

            def count(gn, t, raw, n):
                dve.wait_ge(raw, n + 1)
                for i in range(2):
                    for k in range(KM):
                        last = nc.vector.bn_stats(gn.stats[:, i, k, :], t[:, k, i, :])
                last.then_inc(gn.counted, 1)
                gn.reduce(dve, n)

            def a_rest(p):
                dve.wait_ge(a_hi_made, p.n + 1)
                at_least(dve, offset_products, p.n)
                nc.vector.tensor_tensor(a_lo[:], a_f[:].rearrange("p k i s -> p k (i s)"), a_hi[:].bitcast(F32),
                                        ALU.subtract).then_inc(a_lo_made, 1)

            def b_rest(p):
                dve.wait_ge(b_hi_made, p.n + 1)
                at_least(dve, conv3_done, 8 * p.n)
                nc.vector.tensor_tensor(b_lo[:], b_f[:].rearrange("p k i s -> p k (i s)"), b_hi[:].bitcast(F32),
                                        ALU.subtract).then_inc(b_lo_made, 1)

            def add_taps(p, first, end):
                if first == 0:
                    dve.wait_ge(offset_products, p.n + 1)
                    at_least(dve, om_stored, 16 * p.n)
                order = [4] + [t for t in range(TAPS) if t != 4]
                for done, tap in list(enumerate(order))[first:end]:
                    dy, dx = tap // 3 - 1, tap % 3 - 1
                    at = 32 * (tap % 3)
                    prod = work[at:at + OFFCH, tap // 3, 0:PAIR].rearrange("p (i y x) -> p i y x", i=2, y=SIDE)
                    if done == 0:
                        nc.vector.tensor_scalar(om[:], prod, consts["b_off"], None, ALU.add).then_inc(om_step, 1)
                        continue
                    dve.wait_ge(om_step, TAPS * p.n + done)
                    y0, y1 = max(0, -dy), SIDE - max(0, dy)
                    z0, z1 = max(0, -dx), SIDE - max(0, dx)
                    part = om[:, :, y0:y1, z0:z1]
                    nc.vector.tensor_tensor(part, prod[:, :, y0 + dy:y1 + dy, z0 + dx:z1 + dx], part,
                                            ALU.add).then_inc(om_step, 1)

            def distances(p):
                dve.wait_ge(offs_loaded, 48 * (p.n + 1))
                for c in range(2):
                    last = nc.vector.tensor_tensor(offs[:, c], offs[:, c],
                                                   consts["grid"][:, c, :].unsqueeze(1).broadcast_to([TAPS * SIDE, 2, PIX]), ALU.add)
                last.then_inc(distance, 1)

            def mask_hats(p):
                dve.wait_ge(hat_made, p.n + 1)
                dve.wait_ge(mask_made, p.n + 1)
                nc.vector.tensor_tensor(offs[:, 0], offs[:, 0], offs[:, 2], ALU.mult).then_inc(masked, 1)

            def transposed_rest(p, i):
                dve.wait_ge(aT_hi_made, 2 * p.n + i + 1)
                nc.vector.tensor_tensor(aT_lo[:, i].rearrange("p h c -> p (h c)"), work[0:HALF, i, :],
                                        aT_hi[:, i].rearrange("p h c -> p (h c)").bitcast(F32),
                                        ALU.subtract).then_inc(aT_lo_made, 1)

            def weights_rest(p, u):
                n = cols(u // 2)
                dve.wait_ge(s_hi_made, UNITS * p.n + u + 1)
                at_least(dve, sampled, TILES * p.n + 2 * (u - 1))
                nc.vector.tensor_tensor(s_lo[:, u % 2, :, 0:n], hats[:, u % 2, 0:2, 0:n],
                                        s_hi[:, u % 2, :, 0:n].bitcast(F32), ALU.subtract).then_inc(s_lo_made, 1)

            def sampled_rest(p, t):
                g, i, c = t // 4, t // 2 % 2, t % 2
                at_least(dve, v_hi_made, TILES * p.n + t + 1)
                if t % 4 == 0:
                    at_least(dve, deformed, GROUPS * p.n + (g - 1 if g > 1 else 0))
                nc.vector.tensor_tensor(v_lo[:, g % 2, c, 0:taps_of(g), i, :],
                                        sample[:, t % 2, 0:cols(g)].rearrange("p (k s) -> p k s", s=PIX),
                                        v_hi[:, g % 2, c, 0:taps_of(g), i, :].bitcast(F32),
                                        ALU.subtract).then_inc(v_lo_made, 1)

            def count_y(p, k):
                dve.wait_ge(y_written, 8 * p.n + k + 1)
                for i in range(2):
                    last = nc.vector.bn_stats(gn3.stats[:, i, k, :], y[:, i, k, :])
                if k == KX - 1:
                    last.then_inc(gn3.counted, 1)

            def add_x1(p, i):
                if i == 0:
                    dve.wait_ge(y_scaled, p.n + 1)
                else:
                    dve.wait_ge(scaled_by_act, p.n + 1)
                flat = x1[:, p.buf, i].rearrange("p k s -> p (k s)")
                nc.vector.tensor_tensor(flat, y[:, i].rearrange("p k s -> p (k s)"), flat, ALU.add).then_inc(added, 1)

            def my_weights(p, u):
                if u not in POOL_UNITS:
                    make_weights(nc.vector, dve, p, u)

            def step(before, now, after, coming):
                if before is not None:
                    count(gn2, b_f, b_raw, before.n)
                for k in range(4, KX):
                    if after is not None:
                        add_y(after, k)
                        x1_rest(after, k - 1)
                    if now is not None and k < 6:
                        my_weights(now, k - 4)
                    if k == 5 and before is not None:
                        gn2.moments_of(dve, before.n, sums[:, 4:8])
                    if k == 6 and before is not None:
                        gn2.coefficients(dve, before.n)
                    if k == 6 and now is not None:
                        weights_rest(now, 0)
                if after is not None:
                    x1_rest(after, 7)
                if now is not None:
                    weights_rest(now, 1)
                if before is not None:
                    b_rest(before)
                for t in range(4):
                    if now is not None:
                        sampled_rest(now, t)
                    if t == 1 and after is not None:
                        count(gn1, a_f, a_raw, after.n)
                    if before is not None and t:
                        count_y(before, 2 * t - 2)
                        count_y(before, 2 * t - 1)
                    if t == 2 and now is not None:
                        my_weights(now, 2)
                        weights_rest(now, 2)
                if now is not None:
                    my_weights(now, 3)
                    weights_rest(now, 3)
                if after is not None:
                    gn1.moments_of(dve, after.n, sums[:, 0:4])
                if before is not None:
                    count_y(before, 6)
                if after is not None:
                    gn1.coefficients(dve, after.n)
                if before is not None:
                    count_y(before, 7)
                    gn3.reduce(dve, before.n)
                for t in range(4, TILES):
                    if now is not None:
                        sampled_rest(now, t)
                        if t % 2 and t < 16:
                            my_weights(now, t // 2 + 2)
                    if t == 4 and before is not None:
                        gn3.moments_of(dve, before.n, sums[:, 8:12])
                    if t == 5:
                        if before is not None:
                            gn3.coefficients(dve, before.n)
                        if after is not None:
                            a_rest(after)
                    if now is not None and t % 2 and t < 16:
                        weights_rest(now, t // 2 + 2)
                    if after is not None and t in (8, 9, 10, 11):
                        add_taps(after, *{8: (0, 3), 9: (3, 5), 10: (5, 7), 11: (7, TAPS)}[t])
                    if t in (11, 12) and before is not None:
                        add_x1(before, t - 11)
                    if t == 14 and after is not None:
                        distances(after)
                    if t == 16 and after is not None:
                        mask_hats(after)
                    if t >= 16 and coming is not None:
                        add_y(coming, t - 16)
                        if t > 16:
                            x1_rest(coming, t - 17)
                if after is not None:
                    transposed_rest(after, 0)
                    transposed_rest(after, 1)
            by_iteration(dve, step)

        @block.tensor
        def _(pe):
            def conv1(p, k):
                if k == 0:
                    at_least(pe, aT_lo_made, 2 * p.n)
                at_least(pe, x1_lo_made, 8 * p.n + k + 1)
                for t in range(KM):
                    last = product3(nc, work[:, t, 0:PAIR].rearrange("p (i s) -> p i s", i=2),
                                    w1_hi[:, k, t, :], w1_lo[:, k, t, :], x1_hi[:, k % RING], x1_lo[:, k % RING],
                                    start=(k == 0), stop=(k == KX - 1))
                last.then_inc(conv1_used, 1)

            def offsets(p):
                pe.wait_ge(a_lo_made, p.n + 1)
                for g in range(3):
                    for k in range(KM):
                        last = product3(nc, work[0:96, g, 0:PAIR], wo_hi[:, k, g, :], wo_lo[:, k, g, :],
                                        a_hi[:, k, :], a_lo[:, k, :], start=(k == 0), stop=(k == KM - 1))
                last.then_inc(offset_products, 1)

            def transposes(p):
                at_least(pe, om_step, TAPS * (p.n + 1))
                for i in range(2):
                    for h in range(2):
                        for k in range(KM):
                            last = nc.tensor.transpose(work[0:HALF, i, (h * KM + k) * P:(h * KM + k + 1) * P],
                                                       a_f[:, k, i, h * HALF:(h + 1) * HALF], ident[:])
                    last.then_inc(transposed, 1)

            def sample_tile(p, t):
                g, i, c = t // 4, t // 2 % 2, t % 2
                u, n = t // 2, cols(g)
                if t == 0:
                    at_least(pe, aT_lo_made, 2 * p.n + 2)
                if c == 0:
                    at_least(pe, s_lo_made, UNITS * p.n + u + 1)
                at_least(pe, v_lo_made, TILES * p.n + t - 1)
                for h in range(2):
                    last = product3(nc, sample[:, t % 2, 0:n], aT_hi[:, i, h, c * P:(c + 1) * P],
                                    aT_lo[:, i, h, c * P:(c + 1) * P], s_hi[:, u % 2, h, 0:n], s_lo[:, u % 2, h, 0:n],
                                    start=(h == 0), stop=(h == 1))
                last.then_inc(sampled, 1)

            def deform_part(p, g, part):
                k, t = divmod(part, 2)
                if part == 0:
                    at_least(pe, v_lo_made, TILES * p.n + 4 * g + 4)
                    if g == 0:
                        at_least(pe, b_raw, p.n)
                for tap in range(taps_of(g)):
                    last = product3(nc, deform[:, t, 0:PAIR], w2_hi[:, k, 2 * g + tap, t, :],
                                    w2_lo[:, k, 2 * g + tap, t, :],
                                    v_hi[:, g % 2, k, tap].rearrange("p i s -> p (i s)"),
                                    v_lo[:, g % 2, k, tap].rearrange("p i s -> p (i s)"),
                                    start=(g == 0 and k == 0 and tap == 0),
                                    stop=(g == GROUPS - 1 and k == KM - 1 and tap == taps_of(g) - 1))
                if part == 3:
                    last.then_inc(deformed, 1)

            def conv3(p, k, now, after):
                bank = (k + 2) % 3
                if k == 0:
                    pe.wait_ge(b_lo_made, p.n + 1)
                if k == 1 and after is not None:
                    pe.wait_ge(a_raw, after.n + 1)
                if k >= 3:
                    at_least(pe, y_written, 8 * p.n + k - 2)
                if k == 1 and after is None:
                    if now is not None:
                        pe.wait_ge(aT_lo_made, 2 * (now.n + 1))
                    pe.wait_ge(y_written, 8 * p.n)
                for c in range(KM):
                    last = product3(nc, work[:, bank, 0:PAIR], w3_hi[:, c, k, :], w3_lo[:, c, k, :],
                                    b_hi[:, c, :], b_lo[:, c, :], start=(c == 0), stop=(c == KM - 1))
                last.then_inc(conv3_done, 1)

            def step(before, now, after, coming):
                for k in range(KX):
                    if after is not None:
                        conv1(after, k)
                    if k == 4 and before is not None:
                        at_least(pe, added, 2 * before.n)
                        gn2.group(pe, before.n, ones, sums[:, 4:8])
                for t in range(4):
                    if now is not None:
                        sample_tile(now, t)
                    if before is not None and t:
                        conv3(before, 2 * t - 2, now, after)
                        conv3(before, 2 * t - 1, now, after)
                if after is not None:
                    if before is not None:
                        pe.wait_ge(gn2.done, gn2.STEPS * before.n + gn2.MOMENTS)
                    gn1.group(pe, after.n, ones, sums[:, 0:4])
                if before is not None:
                    conv3(before, 6, now, after)
                    conv3(before, 7, now, after)
                for t in range(4, TILES):
                    if now is not None:
                        sample_tile(now, t)
                        deform_part(now, t // 4 - 1, t % 4)
                    if t == 4 and before is not None:
                        if after is not None:
                            pe.wait_ge(gn1.done, gn1.STEPS * after.n + gn1.MOMENTS)
                        else:
                            pe.wait_ge(gn2.done, gn2.STEPS * before.n + gn2.MOMENTS)
                        gn3.group(pe, before.n, ones, sums[:, 8:12])
                    if t == 7 and after is not None:
                        if before is not None:
                            pe.wait_ge(y_written, 8 * (before.n + 1))
                        else:
                            pe.wait_ge(a_raw, after.n + 1)
                        offsets(after)
                if now is not None:
                    for q in range(4):
                        deform_part(now, GROUPS - 1, q)
                if after is not None:
                    transposes(after)
            by_iteration(pe, step)


def build(nc, x, w, vectors, grid, ident, ones, b_off, out):
    y3 = nc.dram_tensor("y3_scratch", [PAIRS, P, 2, KX * PIX], F32).ap()
    offsets_at = nc.dram_tensor("offset_scratch", [OFFCH, PAIR], F32).ap()
    hats_at = nc.dram_tensor("hat_scratch", [2, 2, SIDE, TAPS * PIX], F32).ap()
    x_v = x.rearrange("(g i) (p k) s -> g p i (k s)", i=2, p=P)
    out_v = out.rearrange("(g i) (p k) s -> g p i (k s)", i=2, p=P)
    with ExitStack() as ctx:
        def sb(name, shape, dt=F32):
            return ctx.enter_context(nc.sbuf_tensor(name, shape, dt))
        vec = {n: sb("v_" + n, [P, a.shape[0] // P]) for n, a in vectors.items()}
        resid = sb("v_resid", [P, 1])
        grid_s = sb("grid_s", [TAPS * SIDE, 2, PIX])
        ident_s = sb("ident_s", [P, P])
        ones_s = sb("ones_s", [P, P])
        b_off_s = sb("b_off_s", [OFFCH, 1])
        half_neg = sb("half_neg", [P, KX])
        scale1, shift1 = sb("scale1", [P, KM]), sb("shift1", [P, KM])
        scale2, shift2 = sb("scale2", [P, KM]), sb("shift2", [P, KM])
        scale3, shift3 = sb("scale3", [P, KX]), sb("shift3", [P, KX])
        with ExitStack() as inner:
            loaded = inner.enter_context(nc.semaphore("consts_loaded"))
            block = inner.enter_context(nc.Block())

            @block.sync
            def _(sp):
                pieces = [(t[:], vectors[n].rearrange("(p k) -> p k", p=P)) for n, t in vec.items()]
                pieces += [(resid[:], w["residual"].unsqueeze(0).broadcast_to([P, 1])), (grid_s[:], grid),
                           (ident_s[:], ident), (ones_s[:], ones), (b_off_s[:], b_off)]
                for dst, src in pieces:
                    sp.dma_start(dst, src).then_inc(loaded, 16)
                sp.wait_ge(loaded, 16 * len(pieces))

            @block.vector
            def _(dve):
                nc.vector.memset(half_neg[:], -0.5)

        with ExitStack() as inner:
            h = inner.enter_context(nc.sbuf_tensor("h", [P, KM, PAIRS * PAIR], F32))
            with nc.sbuf_tensor("stats1", [P, KM, PAIRS, 6], F32) as stats:
                conv1_phase(nc, x_v, w["w1a"], h, stats)
                bn_coefficients(nc, "bn1", stats, KM, vec["g1"][:], vec["be1"][:], vec["b1"][:], half_neg, scale1, shift1)
            with nc.sbuf_tensor("stats2", [P, KM, PAIRS, 6], F32) as stats:
                conv2_phase(nc, w["w2a"], h, scale1, shift1, stats)
                bn_coefficients(nc, "bn2", stats, KM, vec["g2"][:], vec["be2"][:], vec["b2"][:], half_neg, scale2, shift2)
            with nc.sbuf_tensor("stats3", [P, KX, PAIRS, 6], F32) as stats:
                conv3_phase(nc, w["w3a"], h, scale2, shift2, stats, y3)
                bn_coefficients(nc, "bn3", stats, KX, vec["g3"][:], vec["be3"][:], vec["b3"][:], half_neg, scale3, shift3,
                                residual=resid[:])
        consts = {n: vec[n][:] for n in vec} | {
            "grid": grid_s, "ident": ident_s, "ones": ones_s, "b_off": b_off_s[:], "half_neg": half_neg}
        deformable_phase(nc, x_v, y3, scale3, shift3,
                         {"w1": w["w1b"], "woff": w["woff"], "w2": w["w2b"], "w3": w["w3b"]},
                         consts, offsets_at, hats_at, out_v)


def _conv1x1(a, kin, kout):
    return a.reshape(P, kout, P, kin).transpose(2, 3, 1, 0).reshape(P, kin * kout * P)


def _conv3x3(a):
    return a.reshape(P, KM, P, KM, TAPS).transpose(2, 3, 4, 1, 0).reshape(P, KM * TAPS * KM * P)


def kernel(**inputs):
    import numpy as np
    import concourse.bacc as bacc
    from concourse.bass_utils import run_bass_kernel_spmd

    a = {n: np.asarray(v) for n, v in inputs.items()}
    woff = np.zeros((P, KM, 3, 3, 32), np.float32)
    woff[..., 0:OFFCH] = a["L1_conv_w_off"].reshape(OFFCH, P, KM, 3, 3).transpose(1, 2, 3, 4, 0)
    tap, q, iy, ix = np.meshgrid(np.arange(TAPS), np.arange(SIDE), np.arange(SIDE), np.arange(SIDE), indexing="ij")
    grid = np.stack([iy + tap // 3 - 1 - q, ix + tap % 3 - 1 - q], axis=2)
    arrays = {
        "x": a["x"].reshape(NIMG, CIN, PIX),
        "w1a": _conv1x1(a["L0_conv_w1"], KX, KM), "w2a": _conv3x3(a["L0_conv_w2"]),
        "w3a": _conv1x1(a["L0_conv_w3"], KM, KX), "residual": a["L0_conv_residual_scale"],
        "w1b": _conv1x1(a["L1_conv_w1"], KX, KM), "w2b": _conv3x3(a["L1_conv_w2"]),
        "w3b": _conv1x1(a["L1_conv_w3"], KM, KX), "woff": woff.reshape(P, KM * 3 * 96),
        "grid": grid.reshape(TAPS * SIDE, 2, PIX).astype(np.float32),
        "ident": np.eye(P, dtype=np.float32),
        "ones": np.kron(np.eye(P // 4, dtype=np.float32), np.ones((4, 4), np.float32)),
        "b_off": a["L1_conv_b_off"].reshape(OFFCH, 1),
    }
    vectors = {n: a["L0_conv_" + n] for n in ("b1", "g1", "be1", "b2", "g2", "be2", "b3", "g3", "be3")}
    vectors |= {n: a["L1_conv_" + n] for n in ("gn1_scale", "gn1_bias", "gn2_scale", "gn2_bias", "gn3_scale", "gn3_bias")}
    nc = bacc.Bacc("TRN2", target_bir_lowering=False, num_devices=1, dynamic_dma_scratch_size=1024)
    feeds = {"in_" + n: np.ascontiguousarray(v) for n, v in (arrays | vectors).items()}
    t = {n[3:]: nc.dram_tensor(n, v.shape, F32, kind="ExternalInput").ap() for n, v in feeds.items()}
    out = nc.dram_tensor("out", (NIMG, CIN, PIX), F32, kind="ExternalOutput").ap()
    w = {n: t[n] for n in ("w1a", "w2a", "w3a", "w1b", "w2b", "w3b", "woff", "residual")}
    build(nc, t["x"], w, {n: t[n] for n in vectors}, t["grid"], t["ident"], t["ones"], t["b_off"], out)
    got = run_bass_kernel_spmd(nc, [feeds], core_ids=[0])
    return got.results[0]["out"].reshape(NIMG, CIN, SIDE, SIDE)
```

```python
from contextlib import ExitStack

import concourse.bass as bass
from concourse import mybir

F32 = mybir.dt.float32
F32R = mybir.dt.float32r
ALU = mybir.AluOpType
ACT = mybir.ActivationFunctionType
AX_X = mybir.AxisListType.X

P = 128
NIMG, CIN, CMID, SIDE = 64, 1024, 256, 14
PIX = SIDE * SIDE
PAIR = 2 * PIX
PAIRS = NIMG // 2
KX = CIN // P
KM = CMID // P
TAPS = 9
EPS = 1e-5
PAD = SIDE + 2
BANK = 512
HALF = PIX // 2
ROWS = SIDE // 2
GROUPS = 5
UNITS = 2 * GROUPS
TILES = 2 * UNITS
OFFCH = 27
RING = 4
RECTIFY_AT = {8: (0, 4), 10: (4, 8), 11: (8, 10), 12: (10, 14), 13: (14, 16)}
STORE_AT = (11, 14)
LOAD_AT = (14, 16)
HATS_AT = 15
POOL_UNITS = (0, 1, 2, 4, 6, 8)


def at_least(eng, sem, value):
    if not isinstance(value, int) or value > 0:
        eng.wait_ge(sem, value)


def at_least_alone(eng, sem, value, past):
    if not isinstance(value, int):
        eng.wait_ge(past[0], past[1])
    at_least(eng, sem, value)


def product3(nc, out, w_hi, w_lo, x_hi, x_lo, start, stop):
    nc.tensor.matmul(out, w_hi, x_hi, start=start, stop=False)
    nc.tensor.matmul(out, w_hi, x_lo, start=False, stop=False)
    return nc.tensor.matmul(out, w_lo, x_hi, start=False, stop=stop)


def by_two(eng, step, unrolled=1):
    for lap in range(unrolled):
        step(2 * lap, lap, 0)
        step(2 * lap + 1, lap, 1)
    with eng.Fori(unrolled, PAIRS // 2) as lap:
        step(2 * lap, lap, 0)
        step(2 * lap + 1, lap, 1)


def split_weights(nc, ctx, name, source, shape, prior=None):
    hi = ctx.enter_context(nc.sbuf_tensor(name + "_hi", [P] + shape, F32R))
    lo = ctx.enter_context(nc.sbuf_tensor(name + "_lo", [P] + shape, F32R))
    letters = "abcd"[: len(shape)]
    flat = f"p {' '.join(letters)} -> p ({' '.join(letters)})" if len(shape) > 1 else None
    count = 1
    for n in shape:
        count *= n

    def view(t):
        return t[:].rearrange(flat) if flat else t[:]

    with ExitStack() as inner:
        stage = inner.enter_context(nc.sbuf_tensor(name + "_stage", [P, count], F32))
        loaded = inner.enter_context(nc.semaphore(name + "_loaded"))
        hi_made = inner.enter_context(nc.semaphore(name + "_hi_made"))
        block = inner.enter_context(nc.Block())

        @block.sync
        def _(sp):
            sp.dma_start(stage[:], source).then_inc(loaded, 16)

        @block.scalar
        def _(act):
            act.wait_ge(loaded, 16)
            nc.scalar.activation(view(hi), stage[:], ACT.Copy).then_inc(hi_made, 1)

        @block.vector
        def _(dve):
            dve.wait_ge(hi_made, 1)
            nc.vector.tensor_tensor(view(lo), stage[:], view(hi).bitcast(F32), ALU.subtract)

    return hi, lo


def bn_coefficients(nc, name, stats, tiles, gamma, beta, bias, half_neg, scale, shift, residual=None):
    with ExitStack() as ctx:
        mv = ctx.enter_context(nc.sbuf_tensor(name + "_mv", [P, tiles, 2], F32))
        var = ctx.enter_context(nc.sbuf_tensor(name + "_var", [P, tiles], F32))
        rstd = ctx.enter_context(nc.sbuf_tensor(name + "_rstd", [P, tiles], F32))
        mean = ctx.enter_context(nc.sbuf_tensor(name + "_mean", [P, tiles], F32))
        soft = ctx.enter_context(nc.sbuf_tensor(name + "_soft", [P, 4], F32))
        step = ctx.enter_context(nc.semaphore(name + "_step"))
        var_ready = ctx.enter_context(nc.semaphore(name + "_var_ready"))
        rstd_ready = ctx.enter_context(nc.semaphore(name + "_rstd_ready"))
        soft_abs = ctx.enter_context(nc.semaphore(name + "_soft_abs"))
        soft_exp = ctx.enter_context(nc.semaphore(name + "_soft_exp"))
        soft_ln = ctx.enter_context(nc.semaphore(name + "_soft_ln"))
        block = ctx.enter_context(nc.Block())

        @block.scalar
        def _(act):
            if residual is not None:
                nc.scalar.activation(soft[:, 0:1], residual, ACT.Abs).then_inc(soft_abs, 1)
                act.wait_ge(soft_abs, 1)
                nc.scalar.activation(soft[:, 1:2], soft[:, 0:1], ACT.Exp, scale=-1.0).then_inc(soft_exp, 1)
                act.wait_ge(soft_exp, 1)
                nc.scalar.activation(soft[:, 2:3], soft[:, 1:2], ACT.Ln, bias=1.0).then_inc(soft_ln, 1)

        @block.gpsimd
        def _(pool):
            pool.wait_ge(var_ready, 1)
            nc.gpsimd.tensor_tensor(rstd[:], var[:], half_neg[:, 0:tiles], ALU.pow).then_inc(rstd_ready, 1)

        @block.vector
        def _(dve):
            done = [0]

            def then(ins):
                done[0] += 1
                ins.then_inc(step, 1)
                dve.wait_ge(step, done[0])

            for t in range(tiles):
                last = nc.vector.bn_aggr(mv[:, t, :], stats[:, t, :, :].rearrange("p a b -> p (a b)"))
            then(last)
            nc.vector.tensor_scalar(var[:], mv[:, :, 1], EPS, None, ALU.add).then_inc(var_ready, 1)
            then(nc.vector.tensor_tensor(mean[:], mv[:, :, 0], bias, ALU.add))
            dve.wait_ge(rstd_ready, 1)
            then(nc.vector.tensor_tensor(scale[:], rstd[:], gamma, ALU.mult))
            then(nc.vector.tensor_tensor(mean[:], bias, mean[:], ALU.subtract))
            then(nc.vector.tensor_tensor(mean[:], mean[:], scale[:], ALU.mult))
            then(nc.vector.tensor_tensor(shift[:], mean[:], beta, ALU.add))
            if residual is not None:
                dve.wait_ge(soft_ln, 1)
                then(nc.vector.scalar_tensor_tensor(soft[:, 3:4], residual, 0.0, soft[:, 2:3], ALU.max, ALU.add))
                then(nc.vector.tensor_scalar(scale[:], scale[:], soft[:, 3:4], None, ALU.mult))
                then(nc.vector.tensor_scalar(shift[:], shift[:], soft[:, 3:4], None, ALU.mult))


def conv1_phase(nc, x, w1, h, stats):
    with ExitStack() as ctx:
        w_hi, w_lo = split_weights(nc, ctx, "w1a", w1, [KX, KM, P])
        x_in = ctx.enter_context(nc.sbuf_tensor("x_in", [P, 2, 2, KX, PIX], F32))
        x_hi = ctx.enter_context(nc.sbuf_tensor("x_hi", [P, 2, 2, KX // 2, PIX], F32R))
        x_lo = ctx.enter_context(nc.sbuf_tensor("x_lo", [P, 2, 2, KX // 2, PIX], F32R))
        acc = ctx.enter_context(nc.psum_tensor("conv1_acc", [P, 2, KM, BANK], F32))
        x_loaded = [ctx.enter_context(nc.semaphore(f"x_loaded{s}")) for s in range(2)]
        hi_made = ctx.enter_context(nc.semaphore("x_hi_made"))
        lo_made = ctx.enter_context(nc.semaphore("x_lo_made"))
        half_multiplied = ctx.enter_context(nc.semaphore("half_multiplied"))
        h_written = ctx.enter_context(nc.semaphore("h_written"))
        hk = KX // 2
        block = ctx.enter_context(nc.Block())

        @block.sync
        def _(sp):
            def load(pair, lap, slot):
                at_least_alone(sp, lo_made, 2 * (pair - 1), (lo_made, 1))
                sp.dma_start(x_in[:, slot].rearrange("p i k s -> p i (k s)"), x[pair]).then_inc(x_loaded[slot], 16)
            by_two(sp, load)

        @block.scalar
        def _(act):
            def write_h(pair, slot):
                at_least_alone(act, half_multiplied, 2 * pair + 2, (hi_made, 1))
                nc.scalar.activation(h[:, :, bass.ds(pair * PAIR, PAIR)], acc[:, slot, :, 0:PAIR],
                                     ACT.Copy).then_inc(h_written, 1)

            def step(pair, lap, slot):
                act.wait_ge(x_loaded[slot], 16 * (lap + 1))
                for f in range(2):
                    at_least(act, half_multiplied, 2 * pair - 1 + f)
                    nc.scalar.activation(x_hi[:, f].rearrange("p i k s -> p i (k s)"),
                                         x_in[:, slot, :, f * hk:(f + 1) * hk].rearrange("p i k s -> p i (k s)"),
                                         ACT.Copy).then_inc(hi_made, 1)
                if not isinstance(pair, int) or pair > 0:
                    write_h(pair - 1, 1 - slot)
            by_two(act, step)
            write_h(PAIRS - 1, (PAIRS - 1) % 2)

        @block.vector
        def _(dve):
            def count(pair):
                at_least(dve, h_written, pair + 1)
                for t in range(KM):
                    nc.vector.bn_stats(stats[:, t, bass.ds(pair, 1), :].rearrange("p a b -> p (a b)"),
                                       h[:, t, bass.ds(pair * PAIR, PAIR)])

            def step(pair, lap, slot):
                for f in range(2):
                    at_least(dve, hi_made, 2 * pair + f + 1)
                    at_least(dve, half_multiplied, 2 * pair - 1 + f)
                    nc.vector.tensor_tensor(x_lo[:, f].rearrange("p i k s -> p i (k s)"),
                                            x_in[:, slot, :, f * hk:(f + 1) * hk].rearrange("p i k s -> p i (k s)"),
                                            x_hi[:, f].rearrange("p i k s -> p i (k s)").bitcast(F32),
                                            ALU.subtract).then_inc(lo_made, 1)
                if not isinstance(pair, int) or pair > 0:
                    count(pair - 1)
            by_two(dve, step)
            count(PAIRS - 1)

        @block.tensor
        def _(pe):
            def step(pair, lap, slot):
                at_least(pe, h_written, pair - 1)
                for f in range(2):
                    at_least(pe, lo_made, 2 * pair + f + 1)
                    for t in range(KM):
                        for k in range(hk):
                            last = product3(nc, acc[:, slot, t, 0:PAIR].rearrange("p (i s) -> p i s", i=2),
                                            w_hi[:, f * hk + k, t, :], w_lo[:, f * hk + k, t, :],
                                            x_hi[:, f, :, k, :], x_lo[:, f, :, k, :],
                                            start=(f == 0 and k == 0), stop=(f == 1 and k == hk - 1))
                    last.then_inc(half_multiplied, 1)
            by_two(pe, step)


def conv2_phase(nc, w2, h, scale, shift, stats):
    with ExitStack() as ctx:
        w_hi, w_lo = split_weights(nc, ctx, "w2a", w2, [KM, TAPS, KM, P])
        act_f = ctx.enter_context(nc.sbuf_tensor("act_f", [P, 2, KM, PAIR], F32))
        pad_hi = ctx.enter_context(nc.sbuf_tensor("pad_hi", [P, 2, 2 * KM, PAD, PAD], F32R))
        pad_lo = ctx.enter_context(nc.sbuf_tensor("pad_lo", [P, 2, 2 * KM, PAD, PAD], F32R))
        acc = ctx.enter_context(nc.psum_tensor("conv2_acc", [P, 2, KM, BANK], F32))
        cleared = ctx.enter_context(nc.semaphore("pads_cleared"))
        act_made = ctx.enter_context(nc.semaphore("act_made"))
        hi_made = ctx.enter_context(nc.semaphore("pad_hi_made"))
        lo_made = ctx.enter_context(nc.semaphore("pad_lo_made"))
        multiplied = ctx.enter_context(nc.semaphore("conv2_multiplied"))
        h_written = ctx.enter_context(nc.semaphore("h_rewritten"))
        block = ctx.enter_context(nc.Block())

        def inside(t, slot):
            return t[:, slot, :, 1:1 + SIDE, 1:1 + SIDE]

        def squares(t):
            return t.rearrange("p k (i y x) -> p (k i) y x", i=2, y=SIDE)

        @block.scalar
        def _(act):
            act.wait_ge(cleared, 1)

            def write_h(pair, slot):
                at_least_alone(act, multiplied, pair + 1, (lo_made, 1))
                nc.scalar.activation(h[:, :, bass.ds(pair * PAIR, PAIR)], acc[:, slot, :, 0:PAIR],
                                     ACT.Copy).then_inc(h_written, 1)

            def step(pair, lap, slot):
                at_least_alone(act, lo_made, pair - 1, (hi_made, 1))
                for t in range(KM):
                    last = nc.scalar.activation(act_f[:, slot, t, :], h[:, t, bass.ds(pair * PAIR, PAIR)], ACT.Relu,
                                                bias=shift[:, t:t + 1], scale=scale[:, t:t + 1])
                last.then_inc(act_made, 1)
                at_least(act, act_made, pair + 1)
                at_least(act, multiplied, pair - 1)
                nc.scalar.activation(inside(pad_hi, slot), squares(act_f[:, slot]), ACT.Copy).then_inc(hi_made, 1)
                if not isinstance(pair, int) or pair > 0:
                    write_h(pair - 1, 1 - slot)
            by_two(act, step)
            write_h(PAIRS - 1, (PAIRS - 1) % 2)

        @block.vector
        def _(dve):
            nc.vector.memset(pad_hi[:].bitcast(F32), 0.0)
            nc.vector.memset(pad_lo[:].bitcast(F32), 0.0).then_inc(cleared, 1)
            dve.wait_ge(cleared, 1)

            def count(pair):
                at_least(dve, h_written, pair + 1)
                for t in range(KM):
                    nc.vector.bn_stats(stats[:, t, bass.ds(pair, 1), :].rearrange("p a b -> p (a b)"),
                                       h[:, t, bass.ds(pair * PAIR, PAIR)])

            def step(pair, lap, slot):
                at_least(dve, hi_made, pair + 1)
                at_least(dve, multiplied, pair - 1)
                nc.vector.tensor_tensor(inside(pad_lo, slot), squares(act_f[:, slot]),
                                        inside(pad_hi, slot).bitcast(F32), ALU.subtract).then_inc(lo_made, 1)
                if not isinstance(pair, int) or pair > 0:
                    count(pair - 1)
            by_two(dve, step)
            count(PAIRS - 1)

        @block.tensor
        def _(pe):
            def step(pair, lap, slot):
                at_least(pe, h_written, pair - 1)
                at_least(pe, lo_made, pair + 1)
                for t in range(KM):
                    for k in range(KM):
                        for tap in range(TAPS):
                            y, z = divmod(tap, 3)
                            last = product3(nc, acc[:, slot, t, 0:PAIR].rearrange("p (i y x) -> p i y x", i=2, y=SIDE),
                                            w_hi[:, k, tap, t, :], w_lo[:, k, tap, t, :],
                                            pad_hi[:, slot, 2 * k:2 * k + 2, y:y + SIDE, z:z + SIDE],
                                            pad_lo[:, slot, 2 * k:2 * k + 2, y:y + SIDE, z:z + SIDE],
                                            start=(k == 0 and tap == 0), stop=(k == KM - 1 and tap == TAPS - 1))
                last.then_inc(multiplied, 1)
            by_two(pe, step)


def conv3_phase(nc, w3, h, scale, shift, stats, y3):
    with ExitStack() as ctx:
        w_hi, w_lo = split_weights(nc, ctx, "w3a", w3, [KM, KX, P])
        act_f = ctx.enter_context(nc.sbuf_tensor("act3_f", [P, 2, KM, PAIR], F32))
        act_hi = ctx.enter_context(nc.sbuf_tensor("act3_hi", [P, 2, KM, PAIR], F32R))
        act_lo = ctx.enter_context(nc.sbuf_tensor("act3_lo", [P, 2, KM, PAIR], F32R))
        y_out = ctx.enter_context(nc.sbuf_tensor("y_out", [P, 2, 2, KX, PIX], F32))
        acc = ctx.enter_context(nc.psum_tensor("conv3_acc", [P, KX, BANK], F32))
        act_made = ctx.enter_context(nc.semaphore("act3_made"))
        hi_made = ctx.enter_context(nc.semaphore("act3_hi_made"))
        lo_made = ctx.enter_context(nc.semaphore("act3_lo_made"))
        multiplied = ctx.enter_context(nc.semaphore("conv3_multiplied"))
        y_written = ctx.enter_context(nc.semaphore("y_written"))
        counted = ctx.enter_context(nc.semaphore("y_counted"))
        y_stored = [ctx.enter_context(nc.semaphore(f"y_stored{s}")) for s in range(2)]
        block = ctx.enter_context(nc.Block())

        @block.sync
        def _(sp):
            def store(pair, lap, slot):
                at_least_alone(sp, y_written, 4 * pair + 4, (y_written, 1))
                sp.dma_start(y3[pair], y_out[:, slot].rearrange("p i k s -> p i (k s)")).then_inc(y_stored[slot], 16)
            by_two(sp, store)
            for slot in range(2):
                sp.wait_ge(y_stored[slot], 16 * (PAIRS // 2))

        @block.scalar
        def _(act):
            def write_y(pair, lap, slot):
                at_least(act, y_stored[slot], 16 * lap)
                at_least(act, counted, pair - 1)
                for q in range(4):
                    at_least(act, multiplied, 4 * pair + q + 1)
                    nc.scalar.activation(
                        y_out[:, slot, :, 2 * q:2 * q + 2, :].rearrange("p i k s -> p k i s"),
                        acc[:, 2 * q:2 * q + 2, 0:PAIR].rearrange("p k (i s) -> p k i s", i=2),
                        ACT.Copy).then_inc(y_written, 1)

            def step(pair, lap, slot):
                at_least_alone(act, lo_made, pair - 1, (hi_made, 1))
                for t in range(KM):
                    last = nc.scalar.activation(act_f[:, slot, t, :], h[:, t, bass.ds(pair * PAIR, PAIR)], ACT.Relu,
                                                bias=shift[:, t:t + 1], scale=scale[:, t:t + 1])
                last.then_inc(act_made, 1)
                at_least(act, act_made, pair + 1)
                at_least(act, multiplied, 4 * (pair - 1))
                nc.scalar.activation(act_hi[:, slot], act_f[:, slot], ACT.Copy).then_inc(hi_made, 1)
                if not isinstance(pair, int) or pair > 0:
                    write_y(pair - 1, lap if slot else lap - 1, 1 - slot)
            by_two(act, step, unrolled=2)
            write_y(PAIRS - 1, PAIRS // 2 - 1, 1)

        @block.vector
        def _(dve):
            def count(pair, slot):
                for t in range(KX):
                    if t % 2 == 0:
                        at_least(dve, y_written, 4 * pair + t // 2 + 1)
                    last = nc.vector.bn_stats(stats[:, t, bass.ds(pair, 1), :].rearrange("p a b -> p (a b)"),
                                              y_out[:, slot, :, t, :])
                last.then_inc(counted, 1)

            def step(pair, lap, slot):
                at_least(dve, hi_made, pair + 1)
                at_least(dve, multiplied, 4 * (pair - 1))
                nc.vector.tensor_tensor(act_lo[:, slot], act_f[:, slot], act_hi[:, slot].bitcast(F32),
                                        ALU.subtract).then_inc(lo_made, 1)
                if not isinstance(pair, int) or pair > 0:
                    count(pair - 1, 1 - slot)
            by_two(dve, step)
            count(PAIRS - 1, 1)

        @block.tensor
        def _(pe):
            def step(pair, lap, slot):
                at_least(pe, lo_made, pair + 1)
                for t in range(KX):
                    if t % 2 == 0:
                        at_least(pe, y_written, 4 * (pair - 1) + t // 2 + 1)
                    for k in range(KM):
                        last = product3(nc, acc[:, t, 0:PAIR], w_hi[:, k, t, :], w_lo[:, k, t, :],
                                        act_hi[:, slot, k, :], act_lo[:, slot, k, :],
                                        start=(k == 0), stop=(k == KM - 1))
                    if t % 2:
                        last.then_inc(multiplied, 1)
            by_two(pe, step)


class Pair:

    def __init__(self, turn, c):
        self.n = 3 * turn + c
        self.buf = c % 3
        self.lap = turn + c // 3


def by_iteration(eng, step):
    def at(after):
        step(*(Pair(0, n) if 0 <= n < PAIRS else None for n in range(after - 2, after + 2)))

    turns = PAIRS // 3 - 1
    for after in range(-1, 3):
        at(after)
    with eng.Fori(0, turns) as turn:
        for after in range(3, 6):
            step(*(Pair(turn, n) for n in range(after - 2, after + 2)))
    for after in range(3 * (turns + 1), PAIRS + 2):
        at(after)


class GroupNorm:

    SQUARED, SUMMED_M2, REDUCED_MEAN, REDUCED, MOMENTS, MEAN2, VAR, SCALE, SHIFTED, COEF = range(1, 11)
    STEPS = 10

    def __init__(self, nc, ctx, name, tiles, gamma, beta):
        def sb(part, shape):
            return ctx.enter_context(nc.sbuf_tensor(f"{name}_{part}", [P] + shape, F32))
        self.nc, self.tiles, self.gamma, self.beta = nc, tiles, gamma, beta
        self.stats = sb("stats", [2, tiles, 6])
        self.square = sb("square", [2, tiles * 2])
        self.sums = sb("sums", [2, 2])
        self.moments = sb("moments", [2, 2])
        self.mean2 = sb("mean2", [2])
        self.var = sb("var", [2])
        self.rstd = sb("rstd", [2])
        self.scale = sb("scale", [2, tiles])
        self.product = sb("product", [2, tiles])
        self.shift = sb("shift", [2, tiles])
        self.done = ctx.enter_context(nc.semaphore(f"{name}_done"))
        self.counted = ctx.enter_context(nc.semaphore(f"{name}_counted"))
        self.grouped = ctx.enter_context(nc.semaphore(f"{name}_grouped"))
        self.rooted = ctx.enter_context(nc.semaphore(f"{name}_rooted"))

    def reduce(self, dve, n):
        nc, base = self.nc, self.STEPS * n
        parts = self.stats[:].rearrange("p i t (e k) -> p i (t e) k", k=3)
        dve.wait_ge(self.counted, n + 1)
        nc.vector.tensor_tensor(self.square[:], parts[:, :, :, 1], parts[:, :, :, 1],
                                ALU.mult).then_inc(self.done, 1)
        dve.wait_ge(self.done, base + self.SQUARED)
        nc.vector.scalar_tensor_tensor(self.square[:], parts[:, :, :, 2], 1.0 / HALF, self.square[:],
                                       ALU.mult, ALU.add).then_inc(self.done, 1)
        at_least(dve, self.grouped, n)
        nc.vector.tensor_reduce(self.sums[:, 0, :], parts[:, :, :, 1], AX_X, ALU.add).then_inc(self.done, 1)
        dve.wait_ge(self.done, base + self.SUMMED_M2)
        nc.vector.tensor_reduce(self.sums[:, 1, :], self.square[:], AX_X, ALU.add).then_inc(self.done, 1)

    def group(self, pe, n, ones, out):
        pe.wait_ge(self.done, self.STEPS * n + self.REDUCED)
        self.nc.tensor.matmul(out, ones[:], self.sums[:].rearrange("p m i -> p (m i)"), start=True,
                              stop=True).then_inc(self.grouped, 1)

    def root(self, pool, n, half_neg):
        pool.wait_ge(self.done, self.STEPS * n + self.VAR)
        self.nc.gpsimd.tensor_tensor(self.rstd[:], self.var[:], half_neg[:, 0:2], ALU.pow).then_inc(self.rooted, 1)

    def moments_of(self, dve, n, sums):
        nc, base = self.nc, self.STEPS * n
        dve.wait_ge(self.grouped, n + 1)
        nc.vector.tensor_scalar(self.moments[:].rearrange("p m i -> p (m i)"), sums, 1.0 / (4 * 2 * self.tiles), None,
                                ALU.mult).then_inc(self.done, 1)
        dve.wait_ge(self.done, base + self.MOMENTS)
        nc.vector.tensor_tensor(self.mean2[:], self.moments[:, 0, :], self.moments[:, 0, :],
                                ALU.mult).then_inc(self.done, 1)
        dve.wait_ge(self.done, base + self.MEAN2)
        nc.vector.scalar_tensor_tensor(self.var[:], self.moments[:, 1, :], EPS, self.mean2[:], ALU.add,
                                       ALU.subtract).then_inc(self.done, 1)

    def coefficients(self, dve, n):
        nc, base = self.nc, self.STEPS * n
        dve.wait_ge(self.rooted, n + 1)
        for i in range(2):
            last = nc.vector.tensor_scalar(self.scale[:, i, :], self.gamma, self.rstd[:, i:i + 1], None, ALU.mult)
        last.then_inc(self.done, 1)
        dve.wait_ge(self.done, base + self.SCALE)
        for i in range(2):
            last = nc.vector.tensor_scalar(self.product[:, i, :], self.scale[:, i, :], self.moments[:, 0, i:i + 1],
                                           None, ALU.mult)
        last.then_inc(self.done, 1)
        dve.wait_ge(self.done, base + self.SHIFTED)
        for i in range(2):
            last = nc.vector.tensor_tensor(self.shift[:, i, :], self.beta, self.product[:, i, :], ALU.subtract)
        last.then_inc(self.done, 1)


def deformable_phase(nc, x, y3, scale, shift, w, consts, sampled_at, hats_at, out):
    with ExitStack() as ctx:
        w1_hi, w1_lo = split_weights(nc, ctx, "w1b", w["w1"], [KX, KM, P])
        wo_hi, wo_lo = split_weights(nc, ctx, "wob", w["woff"], [KM, 3, 96])
        w2_hi, w2_lo = split_weights(nc, ctx, "w2b", w["w2"], [KM, TAPS, KM, P])
        w3_hi, w3_lo = split_weights(nc, ctx, "w3b", w["w3"], [KM, KX, P])

        def sb(name, shape, dt=F32):
            return ctx.enter_context(nc.sbuf_tensor(name, shape, dt))

        def ps(name, shape):
            return ctx.enter_context(nc.psum_tensor(name, shape, F32))

        def sem(name):
            return ctx.enter_context(nc.semaphore(name))

        x1 = sb("x1", [P, 3, 2, KX, PIX])
        x1_hi = sb("x1_hi", [P, RING, 2, PIX], F32R)
        x1_lo = sb("x1_lo", [P, RING, 2, PIX], F32R)
        a_f = sb("a_f", [P, KM, 2, PIX])
        a_hi = sb("a_hi", [P, KM, 2, PAD, SIDE], F32R)
        a_lo = sb("a_lo", [P, KM, 2, PAD, SIDE], F32R)
        aT_hi = sb("aT_hi", [HALF, 2, 2, CMID], F32R)
        aT_lo = sb("aT_lo", [HALF, 2, 2, CMID], F32R)
        om = sb("om", [OFFCH, 2, SIDE, SIDE])
        offs = sb("offs", [TAPS * SIDE, 3, 2, PIX])
        hats = sb("hats", [HALF, 2, 3, 2 * PIX])
        s_hi = sb("s_hi", [HALF, 2, 2, 2 * PIX], F32R)
        s_lo = sb("s_lo", [HALF, 2, 2, 2 * PIX], F32R)
        v_hi = sb("v_hi", [P, 2, KM, 2, 2, PIX], F32R)
        v_lo = sb("v_lo", [P, 2, KM, 2, 2, PIX], F32R)
        b_f = sb("b_f", [P, KM, 2, PIX])
        b_hi = sb("b_hi", [P, KM, PAIR], F32R)
        b_lo = sb("b_lo", [P, KM, PAIR], F32R)
        y = sb("y", [P, 2, KX, PIX])
        gn1 = GroupNorm(nc, ctx, "gn1", KM, consts["gn1_scale"], consts["gn1_bias"])
        gn2 = GroupNorm(nc, ctx, "gn2", KM, consts["gn2_scale"], consts["gn2_bias"])
        gn3 = GroupNorm(nc, ctx, "gn3", KX, consts["gn3_scale"], consts["gn3_bias"])


        work = ps("work", [P, 3, BANK])
        sample = ps("sample", [P, 2, BANK])
        deform = ps("deform", [P, KM, BANK])
        sums = ps("sums_ps", [P, BANK])

        x_loaded = [[sem(f"x1_loaded{b}_{i}") for i in range(2)] for b in range(3)]
        y_loaded = sem("y_loaded")
        plus_y = sem("plus_y")
        x1_made = sem("x1_made")
        x1_hi_made = sem("x1_hi_made")
        x1_lo_made = sem("x1_lo_made")
        conv1_used = sem("conv1_used")
        a_raw = sem("a_raw")
        a_made = sem("a_made")
        rows_cleared = sem("rows_cleared")
        a_hi_made = sem("a_hi_made")
        a_lo_made = sem("a_lo_made")
        offset_products = sem("offset_products")
        om_step = sem("om_step")
        om_stored = sem("om_stored")
        offs_loaded = sem("offs_loaded")
        distance = sem("distance")
        distance_abs = sem("distance_abs")
        hat_made = sem("hat_made")
        mask_made = sem("mask_made")
        masked = sem("masked")
        hats_stored = sem("hats_stored")
        hats_loaded = [sem(f"hats_loaded{s}") for s in range(2)]
        transposed = sem("transposed")
        aT_hi_made = sem("aT_hi_made")
        aT_lo_made = sem("aT_lo_made")
        s_made = [sem(f"s_made{s}") for s in range(2)]
        s_hi_made = sem("s_hi_made")
        s_lo_made = sem("s_lo_made")
        sampled = sem("sampled")
        v_hi_made = sem("v_hi_made")
        v_lo_made = sem("v_lo_made")
        deformed = sem("deformed")
        b_raw = sem("b_raw")
        b_made = sem("b_made")
        b_hi_made = sem("b_hi_made")
        b_lo_made = sem("b_lo_made")
        conv3_done = sem("conv3_done")
        y_written = sem("y_written")
        added = sem("added")
        rectified = sem("rectified")
        out_stored = [[sem(f"out_stored{b}_{i}") for i in range(2)] for b in range(3)]
        half_neg, ones, ident = consts["half_neg"], consts["ones"], consts["ident"]
        block = ctx.enter_context(nc.Block())

        def inner_rows(t):
            return t[:, :, :, 1:1 + SIDE, :].rearrange("p k i y x -> p (k i) (y x)")

        def taps_of(g):
            return 2 if g < GROUPS - 1 else 1

        def cols(g):
            return taps_of(g) * PIX

        def make_weights(engine, eng, p, u):
            n = cols(u // 2)
            eng.wait_ge(hats_loaded[u % 2], 48 * (GROUPS * p.n + u // 2 + 1))
            engine.tensor_tensor(hats[:, u % 2, 0:2, 0:n], hats[:, u % 2, 0:2, 0:n],
                                 hats[:, u % 2, 2:3, 0:n].broadcast_to([HALF, 2, n]), ALU.mult).then_inc(s_made[u % 2], 1)

        @block.sync
        def _(sp):
            def load_y(p, i):
                if isinstance(p.n, int) and p.n < 3:
                    at_least(sp, plus_y, 8 * p.n)
                at_least_alone(sp, added, 4 * (p.n - 3) + 2 * i + 2, (hats_stored, 16))
                sp.dma_start(y[:, i].rearrange("p k s -> p (k s)"), y3[p.n][:, i, :]).then_inc(y_loaded, 16)

            def load_hats(p, u):
                g, i = divmod(u, 2)
                slot, n = u % 2, cols(g)
                at_least(sp, s_lo_made, UNITS * p.n + u - 1)
                t0 = 2 * g * PIX
                for half in range(2):
                    src = hats_at[0, i, half * ROWS:(half + 1) * ROWS, t0:t0 + n]
                    sp.dma_start(hats[:, slot, half, 0:n], src.unsqueeze(1).broadcast_to([ROWS, SIDE, n])
                                 ).then_inc(hats_loaded[slot], 16)
                src = hats_at[1, i, :, t0:t0 + n]
                sp.dma_start(hats[:, slot, 2, 0:n], src.unsqueeze(0).broadcast_to([ROWS, SIDE, n])
                             ).then_inc(hats_loaded[slot], 16)

            def move_offsets(p):
                sp.wait_ge(om_step, 3 * (p.n + 1))
                sp.dma_start(sampled_at[:, :], om[:].rearrange("p i y x -> p (i y x)")).then_inc(om_stored, 16)
                sp.wait_ge(om_stored, 16 * (p.n + 1))
                for c, first in enumerate((TAPS, 0, 2 * TAPS)):
                    sp.dma_start(offs[:, c].rearrange("p i s -> p (i s)"),
                                 sampled_at[first:first + TAPS, :].unsqueeze(1).broadcast_to([TAPS, SIDE, PAIR])
                                 ).then_inc(offs_loaded, 16)

            def store_hats(p, now):
                if now is not None:
                    for s in range(2):
                        sp.wait_ge(hats_loaded[s], 48 * GROUPS * p.n)
                sp.wait_ge(masked, p.n + 1)
                for yx in range(2):
                    for i in range(2):
                        sp.dma_start(hats_at[yx, i].rearrange("q (k s) -> k q s", s=PIX), offs[:, yx, i, :]
                                     ).then_inc(hats_stored, 16)
                sp.wait_ge(hats_stored, 64 * (p.n + 1))

            def step(before, now, after, coming):
                if now is not None:
                    for u in range(2, 7):
                        load_hats(now, u)
                if after is not None:
                    move_offsets(after)
                for i in range(2):
                    if now is not None:
                        load_hats(now, 7 + i)
                    if coming is not None:
                        load_y(coming, i)
                if now is not None:
                    load_hats(now, 9)
                if after is not None:
                    store_hats(after, now)
                    load_hats(after, 0)
                    load_hats(after, 1)
            by_iteration(sp, step)

        @block.scalar
        def _(act):
            def load_x(p, i):
                at_least(act, out_stored[p.buf][i], 16 * p.lap)
                act.dma_start(x1[:, p.buf, i].rearrange("p k s -> p (k s)"),
                              x[p.n][:, i, :]).then_inc(x_loaded[p.buf][i], 16)

            def store_out(p, i):
                act.wait_ge(rectified, 2 * p.n + i + 1)
                act.dma_start(out[p.n][:, i, :], x1[:, p.buf, i].rearrange("p k s -> p (k s)")
                              ).then_inc(out_stored[p.buf][i], 16)

            def make_x1(p, k):
                at_least(act, plus_y, 8 * p.n + k + 1)
                nc.scalar.activation(x1[:, p.buf, :, k, :], x1[:, p.buf, :, k, :], ACT.Relu,
                                     bias=shift[:, k:k + 1]).then_inc(x1_made, 1)
                at_least(act, x1_made, 8 * p.n + k + 1)
                at_least(act, conv1_used, 8 * p.n + k + 1 - RING)
                nc.scalar.activation(x1_hi[:, k % RING], x1[:, p.buf, :, k, :], ACT.Copy).then_inc(x1_hi_made, 1)

            def raw_a(p):
                at_least(act, conv1_used, 8 * (p.n + 1))
                at_least(act, transposed, 2 * p.n)
                nc.scalar.activation(a_f[:].rearrange("p k i s -> p k (i s)"), work[:, 0:2, 0:PAIR],
                                     ACT.Copy).then_inc(a_raw, 1)

            def make_a(p):
                act.wait_ge(gn1.done, gn1.STEPS * p.n + gn1.COEF)
                for k in range(KM):
                    for i in range(2):
                        last = nc.scalar.activation(a_f[:, k, i, :], a_f[:, k, i, :], ACT.Relu,
                                                    bias=gn1.shift[:, i, k:k + 1], scale=gn1.scale[:, i, k:k + 1])
                last.then_inc(a_made, 1)
                act.wait_ge(a_made, p.n + 1)
                at_least(act, offset_products, p.n)
                nc.scalar.activation(inner_rows(a_hi), a_f[:].rearrange("p k i s -> p (k i) s"),
                                     ACT.Copy).then_inc(a_hi_made, 1)

            def make_hats(p):
                act.wait_ge(distance, p.n + 1)
                flat = offs[:, 0:2].rearrange("p c i s -> p (c i s)")
                nc.scalar.activation(flat, flat, ACT.Abs).then_inc(distance_abs, 1)
                act.wait_ge(distance_abs, p.n + 1)
                nc.scalar.activation(flat, flat, ACT.Relu, bias=1.0, scale=-1.0).then_inc(hat_made, 1)
                mask = offs[:, 2].rearrange("p i s -> p (i s)")
                nc.scalar.activation(mask, mask, ACT.Sigmoid).then_inc(mask_made, 1)

            def transposed_hi(p, i):
                act.wait_ge(transposed, 2 * p.n + i + 1)
                if i == 0:
                    at_least(act, sampled, TILES * p.n)
                nc.scalar.activation(aT_hi[:, i].rearrange("p h c -> p (h c)"), work[0:HALF, i, :],
                                     ACT.Copy).then_inc(aT_hi_made, 1)

            def weights_hi(p, u):
                g = u // 2
                at_least(act, s_made[u % 2], GROUPS * p.n + u // 2 + 1)
                at_least(act, sampled, TILES * p.n + 2 * (u - 1))
                nc.scalar.activation(s_hi[:, u % 2, :, 0:cols(g)], hats[:, u % 2, 0:2, 0:cols(g)],
                                     ACT.Copy).then_inc(s_hi_made, 1)

            def sampled_hi(p, t):
                g, i, c = t // 4, t // 2 % 2, t % 2
                at_least(act, sampled, TILES * p.n + t + 1)
                if t % 4 == 0:
                    at_least(act, deformed, GROUPS * p.n + (g - 1 if g > 1 else 0))
                nc.scalar.activation(v_hi[:, g % 2, c, 0:taps_of(g), i, :],
                                     sample[:, t % 2, 0:cols(g)].rearrange("p (k s) -> p k s", s=PIX),
                                     ACT.Copy).then_inc(v_hi_made, 1)

            def raw_b(p):
                act.wait_ge(deformed, GROUPS * (p.n + 1))
                nc.scalar.activation(b_f[:].rearrange("p k i s -> p k (i s)"), deform[:, :, 0:PAIR],
                                     ACT.Copy).then_inc(b_raw, 1)

            def make_b(p):
                act.wait_ge(gn2.done, gn2.STEPS * p.n + gn2.COEF)
                for k in range(KM):
                    for i in range(2):
                        last = nc.scalar.activation(b_f[:, k, i, :], b_f[:, k, i, :], ACT.Relu,
                                                    bias=gn2.shift[:, i, k:k + 1], scale=gn2.scale[:, i, k:k + 1])
                last.then_inc(b_made, 1)
                act.wait_ge(b_made, p.n + 1)
                at_least(act, conv3_done, 8 * p.n)
                nc.scalar.activation(b_hi[:], b_f[:].rearrange("p k i s -> p k (i s)"), ACT.Copy).then_inc(b_hi_made, 1)

            def write_y(p, k, after):
                if k == 0 and after is not None:
                    at_least(act, plus_y, 8 * (after.n + 1))
                elif k == 0:
                    at_least(act, added, 4 * p.n)
                at_least(act, conv3_done, 8 * p.n + k + 1)
                nc.scalar.activation(y[:, :, k, :], work[:, (k + 2) % 3, 0:PAIR].rearrange("p (i s) -> p i s", i=2),
                                     ACT.Copy).then_inc(y_written, 1)

            def rectify(p, first, end):
                act.wait_ge(added, 4 * p.n + (end - 1) // (KX // 2) + 1)
                for c in range(first, end):
                    i, k = divmod(c, KX)
                    last = nc.scalar.activation(x1[:, p.buf, i, k, :], x1[:, p.buf, i, k, :], ACT.Relu,
                                                bias=gn3.shift[:, i, k:k + 1])
                if end % KX == 0:
                    last.then_inc(rectified, 1)

            def step(before, now, after, coming):
                if before is not None:
                    raw_b(before)
                if after is not None:
                    for k in range(4, KX):
                        make_x1(after, k)
                if now is not None:
                    weights_hi(now, 0)
                if before is not None:
                    make_b(before)
                if now is not None:
                    weights_hi(now, 1)
                if after is not None:
                    raw_a(after)
                for t in range(4):
                    if now is not None:
                        sampled_hi(now, t)
                    if before is not None and t:
                        write_y(before, 2 * t - 2, after)
                        write_y(before, 2 * t - 1, after)
                    if t == 2 and now is not None:
                        weights_hi(now, 2)
                if now is not None:
                    weights_hi(now, 3)
                if before is not None:
                    write_y(before, 6, after)
                    write_y(before, 7, after)
                for t in range(4, TILES):
                    if now is not None:
                        sampled_hi(now, t)
                        if t % 2 and t < 16:
                            weights_hi(now, t // 2 + 2)
                    if t == 4 and after is not None:
                        make_a(after)
                    if t in RECTIFY_AT and before is not None:
                        rectify(before, *RECTIFY_AT[t])
                    if t in STORE_AT and before is not None:
                        store_out(before, STORE_AT.index(t))
                    if t in LOAD_AT and coming is not None:
                        load_x(coming, LOAD_AT.index(t))
                    if t == HATS_AT and after is not None:
                        make_hats(after)
                    if t >= 18 and coming is not None:
                        make_x1(coming, t - 18)
                if after is not None:
                    transposed_hi(after, 0)
                    transposed_hi(after, 1)
                if coming is not None:
                    make_x1(coming, 2)
                    make_x1(coming, 3)
            by_iteration(act, step)
            for b in range(3):
                for i in range(2):
                    act.wait_ge(out_stored[b][i], 16 * ((PAIRS - b + 2) // 3))

        @block.gpsimd
        def _(pool):
            def distances(p):
                pool.wait_ge(offs_loaded, 48 * (p.n + 1))
                for c in range(2):
                    last = nc.gpsimd.tensor_tensor(offs[:, c], offs[:, c],
                                                   consts["grid"][:, c, :].unsqueeze(1).broadcast_to([TAPS * SIDE, 2, PIX]), ALU.add)
                last.then_inc(distance, 1)

            def mask_hats(p):
                pool.wait_ge(hat_made, p.n + 1)
                pool.wait_ge(mask_made, p.n + 1)
                nc.gpsimd.tensor_tensor(offs[:, 0], offs[:, 0], offs[:, 2], ALU.mult).then_inc(masked, 1)

            def weights(p, first, end):
                if p is not None:
                    for u in range(first, end):
                        if u in POOL_UNITS:
                            make_weights(nc.gpsimd, pool, p, u)

            def step(before, now, after, coming):
                weights(now, 0, 2)
                if before is not None:
                    gn2.root(pool, before.n, half_neg)
                weights(now, 2, 4)
                if after is not None:
                    gn1.root(pool, after.n, half_neg)
                weights(now, 4, 5)
                if before is not None:
                    gn3.root(pool, before.n, half_neg)
                weights(now, 5, UNITS)
                if after is not None:
                    distances(after)
                    mask_hats(after)
            by_iteration(pool, step)

        @block.vector
        def _(dve):
            nc.vector.memset(a_hi[:].bitcast(F32), 0.0)
            nc.vector.memset(a_lo[:].bitcast(F32), 0.0).then_inc(rows_cleared, 1)
            dve.wait_ge(rows_cleared, 1)

            def add_y(p, k):
                if k == 0:
                    for i in range(2):
                        dve.wait_ge(x_loaded[p.buf][i], 16 * (p.lap + 1))
                    dve.wait_ge(y_loaded, 32 * (p.n + 1))
                nc.vector.scalar_tensor_tensor(x1[:, p.buf, :, k, :], y[:, :, k, :],
                                               scale[:, k:k + 1], x1[:, p.buf, :, k, :], ALU.mult,
                                               ALU.add).then_inc(plus_y, 1)

            def x1_rest(p, k):
                at_least(dve, x1_hi_made, 8 * p.n + k + 1)
                at_least(dve, conv1_used, 8 * p.n + k + 1 - RING)
                nc.vector.tensor_tensor(x1_lo[:, k % RING], x1[:, p.buf, :, k, :], x1_hi[:, k % RING].bitcast(F32),
                                        ALU.subtract).then_inc(x1_lo_made, 1)

            def count(gn, t, raw, n):
                dve.wait_ge(raw, n + 1)
                for i in range(2):
                    for k in range(KM):
                        last = nc.vector.bn_stats(gn.stats[:, i, k, :], t[:, k, i, :])
                last.then_inc(gn.counted, 1)
                gn.reduce(dve, n)

            def a_rest(p):
                dve.wait_ge(a_hi_made, p.n + 1)
                at_least(dve, offset_products, p.n)
                nc.vector.tensor_tensor(inner_rows(a_lo), a_f[:].rearrange("p k i s -> p (k i) s"),
                                        inner_rows(a_hi).bitcast(F32), ALU.subtract).then_inc(a_lo_made, 1)

            def b_rest(p):
                dve.wait_ge(b_hi_made, p.n + 1)
                at_least(dve, conv3_done, 8 * p.n)
                nc.vector.tensor_tensor(b_lo[:], b_f[:].rearrange("p k i s -> p k (i s)"), b_hi[:].bitcast(F32),
                                        ALU.subtract).then_inc(b_lo_made, 1)

            def add_taps(p):
                dve.wait_ge(offset_products, p.n + 1)
                at_least(dve, om_stored, 16 * p.n)
                for done, column in enumerate((1, 0, 2)):
                    dx = column - 1
                    prod = work[32 * column:32 * column + OFFCH, 0, 0:PAIR].rearrange("p (i y x) -> p i y x", i=2, y=SIDE)
                    if dx == 0:
                        nc.vector.tensor_scalar(om[:], prod, consts["b_off"], None, ALU.add).then_inc(om_step, 1)
                        continue
                    dve.wait_ge(om_step, 3 * p.n + done)
                    z0, z1 = max(0, -dx), SIDE - max(0, dx)
                    nc.vector.tensor_tensor(om[:, :, :, z0:z1], prod[:, :, :, z0 + dx:z1 + dx], om[:, :, :, z0:z1],
                                            ALU.add).then_inc(om_step, 1)

            def transposed_rest(p, i):
                dve.wait_ge(aT_hi_made, 2 * p.n + i + 1)
                nc.vector.tensor_tensor(aT_lo[:, i].rearrange("p h c -> p (h c)"), work[0:HALF, i, :],
                                        aT_hi[:, i].rearrange("p h c -> p (h c)").bitcast(F32),
                                        ALU.subtract).then_inc(aT_lo_made, 1)

            def weights_rest(p, u):
                n = cols(u // 2)
                dve.wait_ge(s_hi_made, UNITS * p.n + u + 1)
                at_least(dve, sampled, TILES * p.n + 2 * (u - 1))
                nc.vector.tensor_tensor(s_lo[:, u % 2, :, 0:n], hats[:, u % 2, 0:2, 0:n],
                                        s_hi[:, u % 2, :, 0:n].bitcast(F32), ALU.subtract).then_inc(s_lo_made, 1)

            def sampled_rest(p, t):
                g, i, c = t // 4, t // 2 % 2, t % 2
                at_least(dve, v_hi_made, TILES * p.n + t + 1)
                if t % 4 == 0:
                    at_least(dve, deformed, GROUPS * p.n + (g - 1 if g > 1 else 0))
                nc.vector.tensor_tensor(v_lo[:, g % 2, c, 0:taps_of(g), i, :],
                                        sample[:, t % 2, 0:cols(g)].rearrange("p (k s) -> p k s", s=PIX),
                                        v_hi[:, g % 2, c, 0:taps_of(g), i, :].bitcast(F32),
                                        ALU.subtract).then_inc(v_lo_made, 1)

            def count_y(p, k):
                dve.wait_ge(y_written, 8 * p.n + k + 1)
                for i in range(2):
                    last = nc.vector.bn_stats(gn3.stats[:, i, k, :], y[:, i, k, :])
                if k == KX - 1:
                    last.then_inc(gn3.counted, 1)

            def add_x1(p, half):
                i, first = half // 2, half % 2 * (KX // 2)
                if half == 0:
                    dve.wait_ge(gn3.done, gn3.STEPS * p.n + gn3.COEF)
                for k in range(first, first + KX // 2):
                    last = nc.vector.scalar_tensor_tensor(x1[:, p.buf, i, k, :], y[:, i, k, :],
                                                          gn3.scale[:, i, k:k + 1], x1[:, p.buf, i, k, :],
                                                          ALU.mult, ALU.add)
                last.then_inc(added, 1)

            def my_weights(p, u):
                if u not in POOL_UNITS:
                    make_weights(nc.vector, dve, p, u)

            def step(before, now, after, coming):
                if after is not None:
                    add_y(after, 4)
                    add_y(after, 5)
                if now is not None:
                    my_weights(now, 0)
                    my_weights(now, 1)
                if before is not None:
                    count(gn2, b_f, b_raw, before.n)
                if after is not None:
                    add_y(after, 6)
                    x1_rest(after, 4)
                if before is not None:
                    gn2.moments_of(dve, before.n, sums[:, 4:8])
                if after is not None:
                    add_y(after, 7)
                    x1_rest(after, 5)
                if before is not None:
                    gn2.coefficients(dve, before.n)
                if after is not None:
                    x1_rest(after, 6)
                    x1_rest(after, 7)
                if now is not None:
                    weights_rest(now, 0)
                    weights_rest(now, 1)
                if before is not None:
                    b_rest(before)
                for t in range(4):
                    if now is not None:
                        sampled_rest(now, t)
                    if t == 1 and after is not None:
                        count(gn1, a_f, a_raw, after.n)
                    if before is not None and t:
                        count_y(before, 2 * t - 2)
                        count_y(before, 2 * t - 1)
                    if t == 2 and now is not None:
                        my_weights(now, 2)
                        weights_rest(now, 2)
                if now is not None:
                    my_weights(now, 3)
                    weights_rest(now, 3)
                if after is not None:
                    gn1.moments_of(dve, after.n, sums[:, 0:4])
                if before is not None:
                    count_y(before, 6)
                if after is not None:
                    gn1.coefficients(dve, after.n)
                for t in range(4, TILES):
                    if now is not None:
                        sampled_rest(now, t)
                        if t % 2 and t < 16:
                            my_weights(now, t // 2 + 2)
                    if before is not None:
                        if t == 4:
                            count_y(before, 7)
                            gn3.reduce(dve, before.n)
                        if t == 6:
                            gn3.moments_of(dve, before.n, sums[:, 8:12])
                        if t == 7:
                            gn3.coefficients(dve, before.n)
                    if t == 5 and after is not None:
                        a_rest(after)
                    if now is not None and t % 2 and t < 16:
                        weights_rest(now, t // 2 + 2)
                    if t in (7, 9, 10, 11) and before is not None:
                        add_x1(before, (7, 9, 10, 11).index(t))
                    if t == 8 and after is not None:
                        add_taps(after)
                    if t >= 18 and coming is not None:
                        add_y(coming, t - 18)
                        if t > 18:
                            x1_rest(coming, t - 19)
                if coming is not None:
                    add_y(coming, 2)
                    add_y(coming, 3)
                    x1_rest(coming, 1)
                if after is not None:
                    transposed_rest(after, 0)
                    transposed_rest(after, 1)
                if coming is not None:
                    x1_rest(coming, 2)
                    x1_rest(coming, 3)
            by_iteration(dve, step)

        @block.tensor
        def _(pe):
            def conv1(p, k):
                if k == 0:
                    at_least(pe, aT_lo_made, 2 * p.n)
                at_least(pe, x1_lo_made, 8 * p.n + k + 1)
                for t in range(KM):
                    last = product3(nc, work[:, t, 0:PAIR].rearrange("p (i s) -> p i s", i=2),
                                    w1_hi[:, k, t, :], w1_lo[:, k, t, :], x1_hi[:, k % RING], x1_lo[:, k % RING],
                                    start=(k == 0), stop=(k == KX - 1))
                last.then_inc(conv1_used, 1)

            def offsets(p):
                pe.wait_ge(a_lo_made, p.n + 1)
                for row in range(3):
                    for k in range(KM):
                        last = product3(nc, work[0:96, 0, 0:PAIR].rearrange("p (i s) -> p i s", i=2),
                                        wo_hi[:, k, row, :], wo_lo[:, k, row, :],
                                        a_hi[:, k, :, row:row + SIDE, :].rearrange("p i y x -> p i (y x)"),
                                        a_lo[:, k, :, row:row + SIDE, :].rearrange("p i y x -> p i (y x)"),
                                        start=(row == 0 and k == 0), stop=(row == 2 and k == KM - 1))
                last.then_inc(offset_products, 1)

            def transposes(p):
                at_least(pe, om_step, 3 * (p.n + 1))
                for i in range(2):
                    for h in range(2):
                        for k in range(KM):
                            last = nc.tensor.transpose(work[0:HALF, i, (h * KM + k) * P:(h * KM + k + 1) * P],
                                                       a_f[:, k, i, h * HALF:(h + 1) * HALF], ident[:])
                    last.then_inc(transposed, 1)

            def sample_tile(p, t):
                g, i, c = t // 4, t // 2 % 2, t % 2
                u, n = t // 2, cols(g)
                if t == 0:
                    at_least(pe, aT_lo_made, 2 * p.n + 2)
                if c == 0:
                    at_least(pe, s_lo_made, UNITS * p.n + u + 1)
                at_least(pe, v_lo_made, TILES * p.n + t - 1)
                for h in range(2):
                    last = product3(nc, sample[:, t % 2, 0:n], aT_hi[:, i, h, c * P:(c + 1) * P],
                                    aT_lo[:, i, h, c * P:(c + 1) * P], s_hi[:, u % 2, h, 0:n], s_lo[:, u % 2, h, 0:n],
                                    start=(h == 0), stop=(h == 1))
                last.then_inc(sampled, 1)

            def deform_part(p, g, part):
                k, t = divmod(part, 2)
                if part == 0:
                    at_least(pe, v_lo_made, TILES * p.n + 4 * g + 4)
                    if g == 0:
                        at_least(pe, b_raw, p.n)
                for tap in range(taps_of(g)):
                    last = product3(nc, deform[:, t, 0:PAIR], w2_hi[:, k, 2 * g + tap, t, :],
                                    w2_lo[:, k, 2 * g + tap, t, :],
                                    v_hi[:, g % 2, k, tap].rearrange("p i s -> p (i s)"),
                                    v_lo[:, g % 2, k, tap].rearrange("p i s -> p (i s)"),
                                    start=(g == 0 and k == 0 and tap == 0),
                                    stop=(g == GROUPS - 1 and k == KM - 1 and tap == taps_of(g) - 1))
                if part == 3:
                    last.then_inc(deformed, 1)

            def conv3(p, k, now, after):
                bank = (k + 2) % 3
                if k == 0:
                    pe.wait_ge(b_lo_made, p.n + 1)
                if k == 1 and after is not None:
                    pe.wait_ge(a_raw, after.n + 1)
                if k >= 3:
                    at_least(pe, y_written, 8 * p.n + k - 2)
                if k == 1 and after is None:
                    if now is not None:
                        pe.wait_ge(aT_lo_made, 2 * (now.n + 1))
                    pe.wait_ge(y_written, 8 * p.n)
                for c in range(KM):
                    last = product3(nc, work[:, bank, 0:PAIR], w3_hi[:, c, k, :], w3_lo[:, c, k, :],
                                    b_hi[:, c, :], b_lo[:, c, :], start=(c == 0), stop=(c == KM - 1))
                last.then_inc(conv3_done, 1)

            def step(before, now, after, coming):
                for k in range(KX):
                    if after is not None:
                        conv1(after, k)
                    if k == 3 and before is not None:
                        at_least(pe, added, 4 * before.n)
                        gn2.group(pe, before.n, ones, sums[:, 4:8])
                for t in range(4):
                    if now is not None:
                        sample_tile(now, t)
                    if before is not None and t:
                        conv3(before, 2 * t - 2, now, after)
                        conv3(before, 2 * t - 1, now, after)
                if after is not None:
                    if before is not None:
                        pe.wait_ge(gn2.done, gn2.STEPS * before.n + gn2.MOMENTS)
                    gn1.group(pe, after.n, ones, sums[:, 0:4])
                if before is not None:
                    conv3(before, 6, now, after)
                    conv3(before, 7, now, after)
                for t in range(4, TILES):
                    if now is not None:
                        sample_tile(now, t)
                        deform_part(now, t // 4 - 1, t % 4)
                    if t == 5 and before is not None:
                        if after is not None:
                            pe.wait_ge(gn1.done, gn1.STEPS * after.n + gn1.MOMENTS)
                        else:
                            pe.wait_ge(gn2.done, gn2.STEPS * before.n + gn2.MOMENTS)
                        gn3.group(pe, before.n, ones, sums[:, 8:12])
                    if t == 6 and after is not None:
                        if before is not None:
                            pe.wait_ge(y_written, 8 * (before.n + 1))
                        else:
                            pe.wait_ge(a_raw, after.n + 1)
                        offsets(after)
                if after is not None:
                    transposes(after)
                if now is not None:
                    for q in range(4):
                        deform_part(now, GROUPS - 1, q)
            by_iteration(pe, step)


def build(nc, x, w, vectors, grid, ident, ones, b_off, out):
    y3 = nc.dram_tensor("y3_scratch", [PAIRS, P, 2, KX * PIX], F32).ap()
    offsets_at = nc.dram_tensor("offset_scratch", [OFFCH, PAIR], F32).ap()
    hats_at = nc.dram_tensor("hat_scratch", [2, 2, SIDE, TAPS * PIX], F32).ap()
    x_v = x.rearrange("(g i) (p k) s -> g p i (k s)", i=2, p=P)
    out_v = out.rearrange("(g i) (p k) s -> g p i (k s)", i=2, p=P)
    with ExitStack() as ctx:
        def sb(name, shape, dt=F32):
            return ctx.enter_context(nc.sbuf_tensor(name, shape, dt))
        vec = {n: sb("v_" + n, [P, a.shape[0] // P]) for n, a in vectors.items()}
        resid = sb("v_resid", [P, 1])
        grid_s = sb("grid_s", [TAPS * SIDE, 2, PIX])
        ident_s = sb("ident_s", [P, P])
        ones_s = sb("ones_s", [P, P])
        b_off_s = sb("b_off_s", [OFFCH, 1])
        half_neg = sb("half_neg", [P, KX])
        scale1, shift1 = sb("scale1", [P, KM]), sb("shift1", [P, KM])
        scale2, shift2 = sb("scale2", [P, KM]), sb("shift2", [P, KM])
        scale3, shift3 = sb("scale3", [P, KX]), sb("shift3", [P, KX])
        with ExitStack() as inner:
            loaded = inner.enter_context(nc.semaphore("consts_loaded"))
            block = inner.enter_context(nc.Block())

            @block.sync
            def _(sp):
                pieces = [(t[:], vectors[n].rearrange("(p k) -> p k", p=P)) for n, t in vec.items()]
                pieces += [(resid[:], w["residual"].unsqueeze(0).broadcast_to([P, 1])), (grid_s[:], grid),
                           (ident_s[:], ident), (ones_s[:], ones), (b_off_s[:], b_off)]
                for dst, src in pieces:
                    sp.dma_start(dst, src).then_inc(loaded, 16)
                sp.wait_ge(loaded, 16 * len(pieces))

            @block.vector
            def _(dve):
                nc.vector.memset(half_neg[:], -0.5)

        with ExitStack() as inner:
            h = inner.enter_context(nc.sbuf_tensor("h", [P, KM, PAIRS * PAIR], F32))
            with nc.sbuf_tensor("stats1", [P, KM, PAIRS, 6], F32) as stats:
                conv1_phase(nc, x_v, w["w1a"], h, stats)
                bn_coefficients(nc, "bn1", stats, KM, vec["g1"][:], vec["be1"][:], vec["b1"][:], half_neg, scale1, shift1)
            with nc.sbuf_tensor("stats2", [P, KM, PAIRS, 6], F32) as stats:
                conv2_phase(nc, w["w2a"], h, scale1, shift1, stats)
                bn_coefficients(nc, "bn2", stats, KM, vec["g2"][:], vec["be2"][:], vec["b2"][:], half_neg, scale2, shift2)
            with nc.sbuf_tensor("stats3", [P, KX, PAIRS, 6], F32) as stats:
                conv3_phase(nc, w["w3a"], h, scale2, shift2, stats, y3)
                bn_coefficients(nc, "bn3", stats, KX, vec["g3"][:], vec["be3"][:], vec["b3"][:], half_neg, scale3, shift3,
                                residual=resid[:])
        consts = {n: vec[n][:] for n in vec} | {
            "grid": grid_s, "ident": ident_s, "ones": ones_s, "b_off": b_off_s[:], "half_neg": half_neg}
        deformable_phase(nc, x_v, y3, scale3, shift3,
                         {"w1": w["w1b"], "woff": w["woff"], "w2": w["w2b"], "w3": w["w3b"]},
                         consts, offsets_at, hats_at, out_v)


def _conv1x1(a, kin, kout):
    return a.reshape(P, kout, P, kin).transpose(2, 3, 1, 0).reshape(P, kin * kout * P)


def _conv3x3(a):
    return a.reshape(P, KM, P, KM, TAPS).transpose(2, 3, 4, 1, 0).reshape(P, KM * TAPS * KM * P)


def kernel(**inputs):
    import numpy as np
    import concourse.bacc as bacc
    from concourse.bass_utils import run_bass_kernel_spmd

    a = {n: np.asarray(v) for n, v in inputs.items()}
    woff = np.zeros((P, KM, 3, 3, 32), np.float32)
    woff[..., 0:OFFCH] = a["L1_conv_w_off"].reshape(OFFCH, P, KM, 3, 3).transpose(1, 2, 3, 4, 0)
    tap, q, iy, ix = np.meshgrid(np.arange(TAPS), np.arange(SIDE), np.arange(SIDE), np.arange(SIDE), indexing="ij")
    grid = np.stack([iy + tap // 3 - 1 - q, ix + tap % 3 - 1 - q], axis=2)
    arrays = {
        "x": a["x"].reshape(NIMG, CIN, PIX),
        "w1a": _conv1x1(a["L0_conv_w1"], KX, KM), "w2a": _conv3x3(a["L0_conv_w2"]),
        "w3a": _conv1x1(a["L0_conv_w3"], KM, KX), "residual": a["L0_conv_residual_scale"],
        "w1b": _conv1x1(a["L1_conv_w1"], KX, KM), "w2b": _conv3x3(a["L1_conv_w2"]),
        "w3b": _conv1x1(a["L1_conv_w3"], KM, KX), "woff": woff.reshape(P, KM * 3 * 96),
        "grid": grid.reshape(TAPS * SIDE, 2, PIX).astype(np.float32),
        "ident": np.eye(P, dtype=np.float32),
        "ones": np.kron(np.eye(P // 4, dtype=np.float32), np.ones((4, 4), np.float32)),
        "b_off": a["L1_conv_b_off"].reshape(OFFCH, 1),
    }
    vectors = {n: a["L0_conv_" + n] for n in ("b1", "g1", "be1", "b2", "g2", "be2", "b3", "g3", "be3")}
    vectors |= {n: a["L1_conv_" + n] for n in ("gn1_scale", "gn1_bias", "gn2_scale", "gn2_bias", "gn3_scale", "gn3_bias")}
    nc = bacc.Bacc("TRN2", target_bir_lowering=False, num_devices=1, dynamic_dma_scratch_size=1024)
    feeds = {"in_" + n: np.ascontiguousarray(v) for n, v in (arrays | vectors).items()}
    t = {n[3:]: nc.dram_tensor(n, v.shape, F32, kind="ExternalInput").ap() for n, v in feeds.items()}
    out = nc.dram_tensor("out", (NIMG, CIN, PIX), F32, kind="ExternalOutput").ap()
    w = {n: t[n] for n in ("w1a", "w2a", "w3a", "w1b", "w2b", "w3b", "woff", "residual")}
    build(nc, t["x"], w, {n: t[n] for n in vectors}, t["grid"], t["ident"], t["ones"], t["b_off"], out)
    got = run_bass_kernel_spmd(nc, [feeds], core_ids=[0])
    return got.results[0]["out"].reshape(NIMG, CIN, SIDE, SIDE)
```

```python
from contextlib import ExitStack

import concourse.bass as bass
from concourse import mybir

F32 = mybir.dt.float32
F32R = mybir.dt.float32r
ALU = mybir.AluOpType
ACT = mybir.ActivationFunctionType
AX_X = mybir.AxisListType.X

P = 128
NIMG, CIN, CMID, SIDE = 64, 1024, 256, 14
PIX = SIDE * SIDE
PAIR = 2 * PIX
PAIRS = NIMG // 2
KX = CIN // P
KM = CMID // P
TAPS = 9
EPS = 1e-5
PAD = SIDE + 2
BANK = 512
HALF = PIX // 2
ROWS = SIDE // 2
GROUPS = 5
UNITS = 2 * GROUPS
TILES = 2 * UNITS
OFFCH = 27
RING = 4
HATS_SLOT = [u % 3 for u in range(UNITS - 1)] + [1]
RECTIFY_AT = {8: (0, 2), 9: (2, 4), 10: (4, 8), 11: (8, 10), 12: (10, 16)}
STORE_AT = (10, 12)
LOAD_AT = (12, 14)
HATS_AT = (13, 14, 15)
TAPS_AT = 7
ADD_AT = (8, 9, 10, 11)
AHEAD_AT = 17
POOL_UNITS = (0, 1, 2, 4, 5, 6, 7, 8)


def at_least(eng, sem, value):
    if not isinstance(value, int) or value > 0:
        eng.wait_ge(sem, value)


def at_least_alone(eng, sem, value, past):
    if not isinstance(value, int):
        eng.wait_ge(past[0], past[1])
    at_least(eng, sem, value)


def product3(nc, out, w_hi, w_lo, x_hi, x_lo, start, stop):
    nc.tensor.matmul(out, w_hi, x_hi, start=start, stop=False)
    nc.tensor.matmul(out, w_hi, x_lo, start=False, stop=False)
    return nc.tensor.matmul(out, w_lo, x_hi, start=False, stop=stop)


def by_two(eng, step, unrolled=1):
    for lap in range(unrolled):
        step(2 * lap, lap, 0)
        step(2 * lap + 1, lap, 1)
    with eng.Fori(unrolled, PAIRS // 2) as lap:
        step(2 * lap, lap, 0)
        step(2 * lap + 1, lap, 1)


class Weights:

    def __init__(self, nc, ctx, name, shape):
        self.nc = nc
        self.hi = ctx.enter_context(nc.sbuf_tensor(name + "_hi", [P] + shape, F32R))
        self.lo = ctx.enter_context(nc.sbuf_tensor(name + "_lo", [P] + shape, F32R))
        self.loaded = ctx.enter_context(nc.semaphore(name + "_loaded"))
        self.hi_made = ctx.enter_context(nc.semaphore(name + "_hi_made"))
        self.lo_made = ctx.enter_context(nc.semaphore(name + "_lo_made"))
        self.columns = 1
        for size in shape:
            self.columns *= size
        letters = " ".join("abcd"[: len(shape)])
        self.flat = f"p {letters} -> p ({letters})"

    def load(self, queue, stage, source):
        queue.dma_start(stage, source).then_inc(self.loaded, 16)

    def make_hi(self, act, stage, n, first=0, end=None):
        act.wait_ge(self.loaded, 16 * n)
        self.nc.scalar.activation(self.hi[:].rearrange(self.flat)[:, first:end or self.columns], stage,
                                  ACT.Copy).then_inc(self.hi_made, 1)

    def make_lo(self, dve, stage, n, first=0, end=None):
        dve.wait_ge(self.hi_made, n)
        lo, hi = (t[:].rearrange(self.flat)[:, first:end or self.columns] for t in (self.lo, self.hi))
        self.nc.vector.tensor_tensor(lo, stage, hi.bitcast(F32), ALU.subtract).then_inc(self.lo_made, 1)


def bn_coefficients(nc, name, stats, tiles, gamma, beta, bias, half_neg, scale, shift, residual=None):
    with ExitStack() as ctx:
        mv = ctx.enter_context(nc.sbuf_tensor(name + "_mv", [P, tiles, 2], F32))
        var = ctx.enter_context(nc.sbuf_tensor(name + "_var", [P, tiles], F32))
        rstd = ctx.enter_context(nc.sbuf_tensor(name + "_rstd", [P, tiles], F32))
        mean = ctx.enter_context(nc.sbuf_tensor(name + "_mean", [P, tiles], F32))
        soft = ctx.enter_context(nc.sbuf_tensor(name + "_soft", [P, 4], F32))
        step = ctx.enter_context(nc.semaphore(name + "_step"))
        var_ready = ctx.enter_context(nc.semaphore(name + "_var_ready"))
        rstd_ready = ctx.enter_context(nc.semaphore(name + "_rstd_ready"))
        soft_abs = ctx.enter_context(nc.semaphore(name + "_soft_abs"))
        soft_exp = ctx.enter_context(nc.semaphore(name + "_soft_exp"))
        soft_ln = ctx.enter_context(nc.semaphore(name + "_soft_ln"))
        block = ctx.enter_context(nc.Block())

        @block.scalar
        def _(act):
            if residual is not None:
                nc.scalar.activation(soft[:, 0:1], residual, ACT.Abs).then_inc(soft_abs, 1)
                act.wait_ge(soft_abs, 1)
                nc.scalar.activation(soft[:, 1:2], soft[:, 0:1], ACT.Exp, scale=-1.0).then_inc(soft_exp, 1)
                act.wait_ge(soft_exp, 1)
                nc.scalar.activation(soft[:, 2:3], soft[:, 1:2], ACT.Ln, bias=1.0).then_inc(soft_ln, 1)

        @block.gpsimd
        def _(pool):
            pool.wait_ge(var_ready, 1)
            nc.gpsimd.tensor_tensor(rstd[:], var[:], half_neg[:, 0:tiles], ALU.pow).then_inc(rstd_ready, 1)

        @block.vector
        def _(dve):
            done = [0]

            def then(ins):
                done[0] += 1
                ins.then_inc(step, 1)
                dve.wait_ge(step, done[0])

            for t in range(tiles):
                last = nc.vector.bn_aggr(mv[:, t, :], stats[:, t, :, :].rearrange("p a b -> p (a b)"))
            then(last)
            nc.vector.tensor_scalar(var[:], mv[:, :, 1], EPS, None, ALU.add).then_inc(var_ready, 1)
            then(nc.vector.tensor_tensor(mean[:], mv[:, :, 0], bias, ALU.add))
            dve.wait_ge(rstd_ready, 1)
            then(nc.vector.tensor_tensor(scale[:], rstd[:], gamma, ALU.mult))
            then(nc.vector.tensor_tensor(mean[:], bias, mean[:], ALU.subtract))
            then(nc.vector.tensor_tensor(mean[:], mean[:], scale[:], ALU.mult))
            then(nc.vector.tensor_tensor(shift[:], mean[:], beta, ALU.add))
            if residual is not None:
                dve.wait_ge(soft_ln, 1)
                then(nc.vector.scalar_tensor_tensor(soft[:, 3:4], residual, 0.0, soft[:, 2:3], ALU.max, ALU.add))
                then(nc.vector.tensor_scalar(scale[:], scale[:], soft[:, 3:4], None, ALU.mult))
                then(nc.vector.tensor_scalar(shift[:], shift[:], soft[:, 3:4], None, ALU.mult))


def conv1_phase(nc, x, w1, w1_source, w2, w2_source, constants, half_neg, h, stats):
    with ExitStack() as ctx:
        w_hi, w_lo = w1.hi, w1.lo
        constants_loaded = ctx.enter_context(nc.semaphore("constants_loaded"))
        half = w2.columns // 2
        stage = ctx.enter_context(nc.sbuf_tensor("stage1", [P, half], F32))
        w1_stage = stage[:, 0:w1.columns]
        x_in = ctx.enter_context(nc.sbuf_tensor("x_in", [P, 2, 2, KX, PIX], F32))
        x_hi = ctx.enter_context(nc.sbuf_tensor("x_hi", [P, 2, 2, KX // 2, PIX], F32R))
        x_lo = ctx.enter_context(nc.sbuf_tensor("x_lo", [P, 2, 2, KX // 2, PIX], F32R))
        acc = ctx.enter_context(nc.psum_tensor("conv1_acc", [P, 2, KM, BANK], F32))
        x_loaded = [ctx.enter_context(nc.semaphore(f"x_loaded{s}")) for s in range(2)]
        hi_made = ctx.enter_context(nc.semaphore("x_hi_made"))
        lo_made = ctx.enter_context(nc.semaphore("x_lo_made"))
        half_multiplied = ctx.enter_context(nc.semaphore("half_multiplied"))
        h_written = ctx.enter_context(nc.semaphore("h_written"))
        hk = KX // 2
        block = ctx.enter_context(nc.Block())

        @block.sync
        def _(sp):
            w1.load(sp, w1_stage, w1_source)

            def load(pair, lap, slot):
                at_least_alone(sp, lo_made, 2 * (pair - 1), (lo_made, 1))
                sp.dma_start(x_in[:, slot].rearrange("p i k s -> p i (k s)"), x[pair]).then_inc(x_loaded[slot], 16)
            by_two(sp, load)
            w2.load(sp, stage[:], w2_source[:, 0:half])
            for dst, src in constants:
                sp.dma_start(dst, src).then_inc(constants_loaded, 16)
            sp.wait_ge(w2.lo_made, 1)
            w2.load(sp, stage[:], w2_source[:, half:])
            sp.wait_ge(constants_loaded, 16 * len(constants))

        @block.scalar
        def _(act):
            w1.make_hi(act, w1_stage, 1)

            def write_h(pair, slot):
                at_least_alone(act, half_multiplied, 2 * pair + 2, (hi_made, 1))
                nc.scalar.activation(h[:, :, bass.ds(pair * PAIR, PAIR)], acc[:, slot, :, 0:PAIR],
                                     ACT.Copy).then_inc(h_written, 1)

            def step(pair, lap, slot):
                act.wait_ge(x_loaded[slot], 16 * (lap + 1))
                for f in range(2):
                    at_least(act, half_multiplied, 2 * pair - 1 + f)
                    nc.scalar.activation(x_hi[:, f].rearrange("p i k s -> p i (k s)"),
                                         x_in[:, slot, :, f * hk:(f + 1) * hk].rearrange("p i k s -> p i (k s)"),
                                         ACT.Copy).then_inc(hi_made, 1)
                if not isinstance(pair, int) or pair > 0:
                    write_h(pair - 1, 1 - slot)
            by_two(act, step)
            w2.make_hi(act, stage[:], 1, 0, half)
            write_h(PAIRS - 1, (PAIRS - 1) % 2)
            w2.make_hi(act, stage[:], 2, half)

        @block.vector
        def _(dve):
            nc.vector.memset(half_neg[:], -0.5)
            w1.make_lo(dve, w1_stage, 1)

            def count(pair):
                at_least(dve, h_written, pair + 1)
                for t in range(KM):
                    nc.vector.bn_stats(stats[:, t, bass.ds(pair, 1), :].rearrange("p a b -> p (a b)"),
                                       h[:, t, bass.ds(pair * PAIR, PAIR)])

            def step(pair, lap, slot):
                for f in range(2):
                    at_least(dve, hi_made, 2 * pair + f + 1)
                    at_least(dve, half_multiplied, 2 * pair - 1 + f)
                    nc.vector.tensor_tensor(x_lo[:, f].rearrange("p i k s -> p i (k s)"),
                                            x_in[:, slot, :, f * hk:(f + 1) * hk].rearrange("p i k s -> p i (k s)"),
                                            x_hi[:, f].rearrange("p i k s -> p i (k s)").bitcast(F32),
                                            ALU.subtract).then_inc(lo_made, 1)
                if not isinstance(pair, int) or pair > 0:
                    count(pair - 1)
            by_two(dve, step)
            w2.make_lo(dve, stage[:], 1, 0, half)
            count(PAIRS - 1)
            w2.make_lo(dve, stage[:], 2, half)

        @block.tensor
        def _(pe):
            pe.wait_ge(w1.lo_made, 1)

            def step(pair, lap, slot):
                at_least(pe, h_written, pair - 1)
                for f in range(2):
                    at_least(pe, lo_made, 2 * pair + f + 1)
                    for t in range(KM):
                        for k in range(hk):
                            last = product3(nc, acc[:, slot, t, 0:PAIR].rearrange("p (i s) -> p i s", i=2),
                                            w_hi[:, f * hk + k, t, :], w_lo[:, f * hk + k, t, :],
                                            x_hi[:, f, :, k, :], x_lo[:, f, :, k, :],
                                            start=(f == 0 and k == 0), stop=(f == 1 and k == hk - 1))
                    last.then_inc(half_multiplied, 1)
            by_two(pe, step)


def conv2_phase(nc, w2, w3, w3_source, w1, w1_source, h, scale, shift, stats):
    with ExitStack() as ctx:
        w_hi, w_lo = w2.hi, w2.lo
        w3_stage = ctx.enter_context(nc.sbuf_tensor("w3_stage", [P, w3.columns], F32))
        w1_stage = ctx.enter_context(nc.sbuf_tensor("w1_stage", [P, w1.columns], F32))
        act_f = ctx.enter_context(nc.sbuf_tensor("act_f", [P, 2, KM, PAIR], F32))
        pad_hi = ctx.enter_context(nc.sbuf_tensor("pad_hi", [P, 2, 2 * KM, PAD, PAD], F32R))
        pad_lo = ctx.enter_context(nc.sbuf_tensor("pad_lo", [P, 2, 2 * KM, PAD, PAD], F32R))
        acc = ctx.enter_context(nc.psum_tensor("conv2_acc", [P, 2, KM, BANK], F32))
        cleared = ctx.enter_context(nc.semaphore("pads_cleared"))
        act_made = ctx.enter_context(nc.semaphore("act_made"))
        hi_made = ctx.enter_context(nc.semaphore("pad_hi_made"))
        lo_made = ctx.enter_context(nc.semaphore("pad_lo_made"))
        multiplied = ctx.enter_context(nc.semaphore("conv2_multiplied"))
        h_written = ctx.enter_context(nc.semaphore("h_rewritten"))
        block = ctx.enter_context(nc.Block())

        def inside(t, slot):
            return t[:, slot, :, 1:1 + SIDE, 1:1 + SIDE]

        def squares(t):
            return t.rearrange("p k (i y x) -> p (k i) y x", i=2, y=SIDE)

        @block.sync
        def _(sp):
            w3.load(sp, w3_stage[:], w3_source)
            w1.load(sp, w1_stage[:], w1_source)

        @block.scalar
        def _(act):
            act.wait_ge(cleared, 1)

            def write_h(pair, slot):
                at_least_alone(act, multiplied, pair + 1, (lo_made, 1))
                nc.scalar.activation(h[:, :, bass.ds(pair * PAIR, PAIR)], acc[:, slot, :, 0:PAIR],
                                     ACT.Copy).then_inc(h_written, 1)

            def step(pair, lap, slot):
                at_least_alone(act, lo_made, pair - 1, (hi_made, 1))
                for t in range(KM):
                    last = nc.scalar.activation(act_f[:, slot, t, :], h[:, t, bass.ds(pair * PAIR, PAIR)], ACT.Relu,
                                                bias=shift[:, t:t + 1], scale=scale[:, t:t + 1])
                last.then_inc(act_made, 1)
                at_least(act, act_made, pair + 1)
                at_least(act, multiplied, pair - 1)
                nc.scalar.activation(inside(pad_hi, slot), squares(act_f[:, slot]), ACT.Copy).then_inc(hi_made, 1)
                if not isinstance(pair, int) or pair > 0:
                    write_h(pair - 1, 1 - slot)
            by_two(act, step)
            w3.make_hi(act, w3_stage[:], 1)
            w1.make_hi(act, w1_stage[:], 2)
            write_h(PAIRS - 1, (PAIRS - 1) % 2)

        @block.vector
        def _(dve):
            for pad in (pad_hi, pad_lo):
                planes = pad[:].rearrange("p s k y x -> p (s k) y x").bitcast(F32)
                nc.vector.memset(planes[:, :, 0:PAD:PAD - 1, :], 0.0)
                last = nc.vector.memset(planes[:, :, 1:PAD - 1, 0:PAD:PAD - 1], 0.0)
            last.then_inc(cleared, 1)
            dve.wait_ge(cleared, 1)

            def count(pair):
                at_least(dve, h_written, pair + 1)
                for t in range(KM):
                    nc.vector.bn_stats(stats[:, t, bass.ds(pair, 1), :].rearrange("p a b -> p (a b)"),
                                       h[:, t, bass.ds(pair * PAIR, PAIR)])

            def step(pair, lap, slot):
                at_least(dve, hi_made, pair + 1)
                at_least(dve, multiplied, pair - 1)
                nc.vector.tensor_tensor(inside(pad_lo, slot), squares(act_f[:, slot]),
                                        inside(pad_hi, slot).bitcast(F32), ALU.subtract).then_inc(lo_made, 1)
                if not isinstance(pair, int) or pair > 0:
                    count(pair - 1)
            by_two(dve, step)
            w3.make_lo(dve, w3_stage[:], 1)
            w1.make_lo(dve, w1_stage[:], 2)
            count(PAIRS - 1)

        @block.tensor
        def _(pe):
            def step(pair, lap, slot):
                at_least(pe, h_written, pair - 1)
                at_least(pe, lo_made, pair + 1)
                for t in range(KM):
                    for k in range(KM):
                        for tap in range(TAPS):
                            y, z = divmod(tap, 3)
                            last = product3(nc, acc[:, slot, t, 0:PAIR].rearrange("p (i y x) -> p i y x", i=2, y=SIDE),
                                            w_hi[:, k, tap, t, :], w_lo[:, k, tap, t, :],
                                            pad_hi[:, slot, 2 * k:2 * k + 2, y:y + SIDE, z:z + SIDE],
                                            pad_lo[:, slot, 2 * k:2 * k + 2, y:y + SIDE, z:z + SIDE],
                                            start=(k == 0 and tap == 0), stop=(k == KM - 1 and tap == TAPS - 1))
                last.then_inc(multiplied, 1)
            by_two(pe, step)


def conv3_phase(nc, w3, w2, w2_source, h, scale, shift, stats, y3):
    with ExitStack() as ctx:
        w_hi, w_lo = w3.hi, w3.lo
        w2_stage = h[:, 0, 0:w2.columns]
        act_f = ctx.enter_context(nc.sbuf_tensor("act3_f", [P, KM, PAIR], F32))
        act_hi = ctx.enter_context(nc.sbuf_tensor("act3_hi", [P, 2, KM, PAIR], F32R))
        act_lo = ctx.enter_context(nc.sbuf_tensor("act3_lo", [P, 2, KM, PAIR], F32R))
        y_out = ctx.enter_context(nc.sbuf_tensor("y_out", [P, 2, 2, KX, PIX], F32))
        acc = ctx.enter_context(nc.psum_tensor("conv3_acc", [P, KX, BANK], F32))
        act_made = ctx.enter_context(nc.semaphore("act3_made"))
        hi_made = ctx.enter_context(nc.semaphore("act3_hi_made"))
        lo_made = ctx.enter_context(nc.semaphore("act3_lo_made"))
        multiplied = ctx.enter_context(nc.semaphore("conv3_multiplied"))
        y_written = ctx.enter_context(nc.semaphore("y_written"))
        counted = ctx.enter_context(nc.semaphore("y_counted"))
        y_stored = [ctx.enter_context(nc.semaphore(f"y_stored{s}")) for s in range(2)]
        block = ctx.enter_context(nc.Block())

        @block.sync
        def _(sp):
            def store(pair, lap, slot):
                at_least_alone(sp, y_written, 4 * pair + 4, (y_written, 1))
                sp.dma_start(y3[pair], y_out[:, slot].rearrange("p i k s -> p i (k s)")).then_inc(y_stored[slot], 16)
            by_two(sp, store)
            for slot in range(2):
                sp.wait_ge(y_stored[slot], 16 * (PAIRS // 2))

        @block.scalar
        def _(act):
            def write_y(pair, lap, slot):
                at_least(act, y_stored[slot], 16 * lap)
                at_least(act, counted, pair - 1)
                for q in range(4):
                    at_least(act, multiplied, 4 * pair + q + 1)
                    nc.scalar.activation(
                        y_out[:, slot, :, 2 * q:2 * q + 2, :].rearrange("p i k s -> p k i s"),
                        acc[:, 2 * q:2 * q + 2, 0:PAIR].rearrange("p k (i s) -> p k i s", i=2),
                        ACT.Copy).then_inc(y_written, 1)

            def step(pair, lap, slot):
                at_least_alone(act, lo_made, pair, (hi_made, 1))
                for t in range(KM):
                    last = nc.scalar.activation(act_f[:, t, :], h[:, t, bass.ds(pair * PAIR, PAIR)], ACT.Relu,
                                                bias=shift[:, t:t + 1], scale=scale[:, t:t + 1])
                last.then_inc(act_made, 1)
                at_least(act, act_made, pair + 1)
                at_least(act, multiplied, 4 * (pair - 1))
                nc.scalar.activation(act_hi[:, slot], act_f[:], ACT.Copy).then_inc(hi_made, 1)
                if not isinstance(pair, int) or pair > 0:
                    write_y(pair - 1, lap if slot else lap - 1, 1 - slot)
            by_two(act, step, unrolled=2)
            act.wait_ge(act_made, PAIRS)
            w2.load(act, w2_stage, w2_source)
            write_y(PAIRS - 1, PAIRS // 2 - 1, 1)
            w2.make_hi(act, w2_stage, 3)

        @block.vector
        def _(dve):
            def count(pair, slot):
                for t in range(KX):
                    if t % 2 == 0:
                        at_least(dve, y_written, 4 * pair + t // 2 + 1)
                    last = nc.vector.bn_stats(stats[:, t, bass.ds(pair, 1), :].rearrange("p a b -> p (a b)"),
                                              y_out[:, slot, :, t, :])
                last.then_inc(counted, 1)

            def step(pair, lap, slot):
                at_least(dve, hi_made, pair + 1)
                at_least(dve, multiplied, 4 * (pair - 1))
                nc.vector.tensor_tensor(act_lo[:, slot], act_f[:], act_hi[:, slot].bitcast(F32),
                                        ALU.subtract).then_inc(lo_made, 1)
                if not isinstance(pair, int) or pair > 0:
                    count(pair - 1, 1 - slot)
            by_two(dve, step)
            count(PAIRS - 1, 1)
            w2.make_lo(dve, w2_stage, 3)

        @block.tensor
        def _(pe):
            def step(pair, lap, slot):
                at_least(pe, lo_made, pair + 1)
                for t in range(KX):
                    if t % 2 == 0:
                        at_least(pe, y_written, 4 * (pair - 1) + t // 2 + 1)
                    for k in range(KM):
                        last = product3(nc, acc[:, t, 0:PAIR], w_hi[:, k, t, :], w_lo[:, k, t, :],
                                        act_hi[:, slot, k, :], act_lo[:, slot, k, :],
                                        start=(k == 0), stop=(k == KM - 1))
                    if t % 2:
                        last.then_inc(multiplied, 1)
            by_two(pe, step)


class Pair:

    def __init__(self, turn, c):
        self.n = 3 * turn + c
        self.buf = c % 3
        self.lap = turn + c // 3


def by_iteration(eng, step):
    def at(after):
        step(*(Pair(0, n) if 0 <= n < PAIRS else None for n in range(after - 2, after + 2)))

    turns = PAIRS // 3 - 1
    for after in range(-1, 3):
        at(after)
    with eng.Fori(0, turns) as turn:
        for after in range(3, 6):
            step(*(Pair(turn, n) for n in range(after - 2, after + 2)))
    for after in range(3 * (turns + 1), PAIRS + 2):
        at(after)


class GroupNorm:

    SQUARED, SUMMED_M2, REDUCED_MEAN, REDUCED, MOMENTS, MEAN2, VAR, SCALE, SHIFTED, COEF = range(1, 11)
    STEPS = 10

    def __init__(self, nc, ctx, name, tiles, gamma, beta):
        def sb(part, shape):
            return ctx.enter_context(nc.sbuf_tensor(f"{name}_{part}", [P] + shape, F32))
        self.nc, self.tiles, self.gamma, self.beta = nc, tiles, gamma, beta
        self.stats = sb("stats", [2, tiles, 6])
        self.square = sb("square", [2, tiles * 2])
        self.sums = sb("sums", [2, 2])
        self.moments = sb("moments", [2, 2])
        self.mean2 = sb("mean2", [2])
        self.var = sb("var", [2])
        self.rstd = sb("rstd", [2])
        self.scale = sb("scale", [2, tiles])
        self.product = sb("product", [2, tiles])
        self.shift = sb("shift", [2, tiles])
        self.done = ctx.enter_context(nc.semaphore(f"{name}_done"))
        self.counted = ctx.enter_context(nc.semaphore(f"{name}_counted"))
        self.grouped = ctx.enter_context(nc.semaphore(f"{name}_grouped"))
        self.rooted = ctx.enter_context(nc.semaphore(f"{name}_rooted"))

    def reduce(self, dve, n):
        nc, base = self.nc, self.STEPS * n
        parts = self.stats[:].rearrange("p i t (e k) -> p i (t e) k", k=3)
        dve.wait_ge(self.counted, n + 1)
        nc.vector.tensor_tensor(self.square[:], parts[:, :, :, 1], parts[:, :, :, 1],
                                ALU.mult).then_inc(self.done, 1)
        dve.wait_ge(self.done, base + self.SQUARED)
        nc.vector.scalar_tensor_tensor(self.square[:], parts[:, :, :, 2], 1.0 / HALF, self.square[:],
                                       ALU.mult, ALU.add).then_inc(self.done, 1)
        at_least(dve, self.grouped, n)
        nc.vector.tensor_reduce(self.sums[:, 0, :], parts[:, :, :, 1], AX_X, ALU.add).then_inc(self.done, 1)
        dve.wait_ge(self.done, base + self.SUMMED_M2)
        nc.vector.tensor_reduce(self.sums[:, 1, :], self.square[:], AX_X, ALU.add).then_inc(self.done, 1)

    def group(self, pe, n, ones, out):
        pe.wait_ge(self.done, self.STEPS * n + self.REDUCED)
        self.nc.tensor.matmul(out, ones[:], self.sums[:].rearrange("p m i -> p (m i)"), start=True,
                              stop=True).then_inc(self.grouped, 1)

    def root(self, pool, n, half_neg):
        pool.wait_ge(self.done, self.STEPS * n + self.VAR)
        self.nc.gpsimd.tensor_tensor(self.rstd[:], self.var[:], half_neg[:, 0:2], ALU.pow).then_inc(self.rooted, 1)

    def moments_of(self, dve, n, sums):
        nc, base = self.nc, self.STEPS * n
        dve.wait_ge(self.grouped, n + 1)
        nc.vector.tensor_scalar(self.moments[:].rearrange("p m i -> p (m i)"), sums, 1.0 / (4 * 2 * self.tiles), None,
                                ALU.mult).then_inc(self.done, 1)
        dve.wait_ge(self.done, base + self.MOMENTS)
        nc.vector.tensor_tensor(self.mean2[:], self.moments[:, 0, :], self.moments[:, 0, :],
                                ALU.mult).then_inc(self.done, 1)
        dve.wait_ge(self.done, base + self.MEAN2)
        nc.vector.scalar_tensor_tensor(self.var[:], self.moments[:, 1, :], EPS, self.mean2[:], ALU.add,
                                       ALU.subtract).then_inc(self.done, 1)

    def coefficients(self, dve, n):
        nc, base = self.nc, self.STEPS * n
        dve.wait_ge(self.rooted, n + 1)
        for i in range(2):
            last = nc.vector.tensor_scalar(self.scale[:, i, :], self.gamma, self.rstd[:, i:i + 1], None, ALU.mult)
        last.then_inc(self.done, 1)
        dve.wait_ge(self.done, base + self.SCALE)
        for i in range(2):
            last = nc.vector.tensor_scalar(self.product[:, i, :], self.scale[:, i, :], self.moments[:, 0, i:i + 1],
                                           None, ALU.mult)
        last.then_inc(self.done, 1)
        dve.wait_ge(self.done, base + self.SHIFTED)
        for i in range(2):
            last = nc.vector.tensor_tensor(self.shift[:, i, :], self.beta, self.product[:, i, :], ALU.subtract)
        last.then_inc(self.done, 1)


def deformable_phase(nc, x, y3, scale, shift, w1, w2, w3_source, woff_source, consts, sampled_at, hats_at, out):
    with ExitStack() as ctx:
        w3 = Weights(nc, ctx, "w3b", [KM, KX, P])
        wo = Weights(nc, ctx, "wob", [KM, 3, 96])
        w1_hi, w1_lo, w2_hi, w2_lo = w1.hi, w1.lo, w2.hi, w2.lo
        w3_hi, w3_lo, wo_hi, wo_lo = w3.hi, w3.lo, wo.hi, wo.lo

        def sb(name, shape, dt=F32):
            return ctx.enter_context(nc.sbuf_tensor(name, shape, dt))

        def ps(name, shape):
            return ctx.enter_context(nc.psum_tensor(name, shape, F32))

        def sem(name):
            return ctx.enter_context(nc.semaphore(name))

        x1 = sb("x1", [P, 3, 2, KX, PIX])
        x1_hi = sb("x1_hi", [P, RING, 2, PIX], F32R)
        x1_lo = sb("x1_lo", [P, RING, 2, PIX], F32R)
        a_f = sb("a_f", [P, KM, 2, PIX])
        a_hi = sb("a_hi", [P, KM, 2, PAD, SIDE], F32R)
        a_lo = sb("a_lo", [P, KM, 2, PAD, SIDE], F32R)
        aT_hi = sb("aT_hi", [HALF, 2, 2, CMID], F32R)
        aT_lo = sb("aT_lo", [HALF, 2, 2, CMID], F32R)
        om = sb("om", [OFFCH, 2, SIDE, SIDE])
        offs = sb("offs", [TAPS * SIDE, 3, 2, PIX])
        hats = sb("hats", [HALF, 3, 3, 2 * PIX])
        s_hi = sb("s_hi", [HALF, 2, 2, 2 * PIX], F32R)
        s_lo = sb("s_lo", [HALF, 2, 2, 2 * PIX], F32R)
        v_hi = sb("v_hi", [P, 2, KM, 2, 2, PIX], F32R)
        v_lo = sb("v_lo", [P, 2, KM, 2, 2, PIX], F32R)
        b_f = sb("b_f", [P, KM, 2, PIX])
        b_hi = sb("b_hi", [P, KM, PAIR], F32R)
        b_lo = sb("b_lo", [P, KM, PAIR], F32R)
        y = sb("y", [P, 2, KX, PIX])
        gn1 = GroupNorm(nc, ctx, "gn1", KM, consts["gn1_scale"], consts["gn1_bias"])
        gn2 = GroupNorm(nc, ctx, "gn2", KM, consts["gn2_scale"], consts["gn2_bias"])
        gn3 = GroupNorm(nc, ctx, "gn3", KX, consts["gn3_scale"], consts["gn3_bias"])


        work = ps("work", [P, 3, BANK])
        sample = ps("sample", [P, 2, BANK])
        deform = ps("deform", [P, KM, BANK])
        sums = ps("sums_ps", [P, BANK])

        x_loaded = [[sem(f"x1_loaded{b}_{i}") for i in range(2)] for b in range(3)]
        y_loaded = sem("y_loaded")
        plus_y = sem("plus_y")
        x1_made = sem("x1_made")
        x1_hi_made = sem("x1_hi_made")
        x1_lo_made = sem("x1_lo_made")
        conv1_used = sem("conv1_used")
        a_raw = sem("a_raw")
        a_made = sem("a_made")
        rows_cleared = sem("rows_cleared")
        a_hi_made = sem("a_hi_made")
        a_lo_made = sem("a_lo_made")
        offset_products = sem("offset_products")
        om_step = sem("om_step")
        om_stored = sem("om_stored")
        offs_loaded = sem("offs_loaded")
        distance = sem("distance")
        distance_abs = sem("distance_abs")
        hat_made = sem("hat_made")
        mask_made = sem("mask_made")
        masked = sem("masked")
        hats_stored = sem("hats_stored")
        hats_loaded = [sem(f"hats_loaded{s}") for s in range(3)]
        transposed = sem("transposed")
        aT_hi_made = sem("aT_hi_made")
        aT_lo_made = sem("aT_lo_made")
        s_made = [sem(f"s_made{s}") for s in range(3)]
        s_hi_made = sem("s_hi_made")
        s_lo_made = sem("s_lo_made")
        sampled = sem("sampled")
        v_hi_made = sem("v_hi_made")
        v_lo_made = sem("v_lo_made")
        deformed = sem("deformed")
        b_raw = sem("b_raw")
        b_made = sem("b_made")
        b_hi_made = sem("b_hi_made")
        b_lo_made = sem("b_lo_made")
        conv3_done = sem("conv3_done")
        y_written = sem("y_written")
        added = sem("added")
        rectified = sem("rectified")
        out_stored = [[sem(f"out_stored{b}_{i}") for i in range(2)] for b in range(3)]
        half_neg, ones, ident = consts["half_neg"], consts["ones"], consts["ident"]
        block = ctx.enter_context(nc.Block())

        def inner_rows(t):
            return t[:, :, :, 1:1 + SIDE, :].rearrange("p k i y x -> p (k i) (y x)")

        free = x1[:, 2].rearrange("p i k s -> p (i k s)")
        wo_stage, w3_stage = free[:, 0:wo.columns], free[:, wo.columns:wo.columns + w3.columns]

        def taps_of(g):
            return 2 if g < GROUPS - 1 else 1

        def cols(g):
            return taps_of(g) * PIX

        def turns_of(p, u):
            return HATS_SLOT.count(HATS_SLOT[u]) * p.n + HATS_SLOT[:u + 1].count(HATS_SLOT[u])

        def make_weights(engine, eng, p, u):
            n, slot = cols(u // 2), HATS_SLOT[u]
            eng.wait_ge(hats_loaded[slot], 48 * turns_of(p, u))
            engine.tensor_tensor(hats[:, slot, 0:2, 0:n], hats[:, slot, 0:2, 0:n],
                                 hats[:, slot, 2:3, 0:n].broadcast_to([HALF, 2, n]), ALU.mult).then_inc(s_made[slot], 1)

        @block.sync
        def _(sp):
            def load_y(p, i):
                if isinstance(p.n, int) and p.n < 3:
                    at_least(sp, plus_y, 8 * p.n)
                at_least_alone(sp, added, 4 * (p.n - 3) + 2 * i + 2, (hats_stored, 16))
                sp.dma_start(y[:, i].rearrange("p k s -> p (k s)"), y3[p.n][:, i, :]).then_inc(y_loaded, 16)

            def load_hats(p, u):
                g, i = divmod(u, 2)
                slot, n = HATS_SLOT[u], cols(g)
                earlier = [v for v in range(u) if HATS_SLOT[v] == slot]
                last = earlier[-1] if earlier else max(v for v in range(UNITS) if HATS_SLOT[v] == slot) - UNITS
                at_least(sp, s_lo_made, UNITS * p.n + last + 1)
                t0 = 2 * g * PIX
                for half in range(2):
                    src = hats_at[0, i, half * ROWS:(half + 1) * ROWS, t0:t0 + n]
                    sp.dma_start(hats[:, slot, half, 0:n], src.unsqueeze(1).broadcast_to([ROWS, SIDE, n])
                                 ).then_inc(hats_loaded[slot], 16)
                src = hats_at[1, i, :, t0:t0 + n]
                sp.dma_start(hats[:, slot, 2, 0:n], src.unsqueeze(0).broadcast_to([ROWS, SIDE, n])
                             ).then_inc(hats_loaded[slot], 16)

            def store_offsets(p):
                sp.wait_ge(om_step, 3 * (p.n + 1))
                sp.dma_start(sampled_at[:, :], om[:].rearrange("p i y x -> p (i y x)")).then_inc(om_stored, 16)

            def load_offsets(p):
                sp.wait_ge(om_stored, 16 * (p.n + 1))
                for c, first in enumerate((TAPS, 0, 2 * TAPS)):
                    sp.dma_start(offs[:, c].rearrange("p i s -> p (i s)"),
                                 sampled_at[first:first + TAPS, :].unsqueeze(1).broadcast_to([TAPS, SIDE, PAIR])
                                 ).then_inc(offs_loaded, 16)

            def store_hats(p, now):
                for i in range(2):
                    if now is not None:
                        slot = HATS_SLOT[8 + i]
                        sp.wait_ge(hats_loaded[slot], 48 * HATS_SLOT.count(slot) * p.n)
                    if i == 0:
                        sp.wait_ge(masked, p.n + 1)
                    for yx in range(2):
                        sp.dma_start(hats_at[yx, i].rearrange("q (k s) -> k q s", s=PIX), offs[:, yx, i, :]
                                     ).then_inc(hats_stored, 16)
                sp.wait_ge(hats_stored, 64 * (p.n + 1))

            def step(before, now, after, coming):
                if after is None and now is None and before is None:
                    for i in range(2):
                        load_y(coming, i)
                    wo.load(sp, wo_stage, woff_source)
                    w3.load(sp, w3_stage, w3_source)
                    return
                if now is not None:
                    for u in range(3, 8):
                        load_hats(now, u)
                if now is None and coming is not None:
                    load_y(coming, 0)
                    load_y(coming, 1)
                if after is not None:
                    store_offsets(after)
                    load_offsets(after)
                if now is not None:
                    load_hats(now, 8)
                if now is not None and coming is not None:
                    load_y(coming, 0)
                    load_y(coming, 1)
                if now is not None:
                    load_hats(now, 9)
                if after is not None:
                    store_hats(after, now)
                    for u in range(3):
                        load_hats(after, u)
            by_iteration(sp, step)

        @block.scalar
        def _(act):
            def load_x(p, i):
                if isinstance(p.n, int) and p.n == 2:
                    act.wait_ge(w3.lo_made, 1)
                at_least(act, out_stored[p.buf][i], 16 * p.lap)
                act.dma_start(x1[:, p.buf, i].rearrange("p k s -> p (k s)"),
                              x[p.n][:, i, :]).then_inc(x_loaded[p.buf][i], 16)

            def store_out(p, i):
                act.wait_ge(rectified, 2 * p.n + i + 1)
                act.dma_start(out[p.n][:, i, :], x1[:, p.buf, i].rearrange("p k s -> p (k s)")
                              ).then_inc(out_stored[p.buf][i], 16)

            def make_x1(p, k):
                at_least(act, plus_y, 8 * p.n + k + 1)
                nc.scalar.activation(x1[:, p.buf, :, k, :], x1[:, p.buf, :, k, :], ACT.Relu,
                                     bias=shift[:, k:k + 1]).then_inc(x1_made, 1)
                at_least(act, x1_made, 8 * p.n + k + 1)
                at_least(act, conv1_used, 8 * p.n + k + 1 - RING)
                nc.scalar.activation(x1_hi[:, k % RING], x1[:, p.buf, :, k, :], ACT.Copy).then_inc(x1_hi_made, 1)

            def raw_a(p):
                at_least(act, conv1_used, 8 * (p.n + 1))
                at_least(act, transposed, 2 * p.n)
                nc.scalar.activation(a_f[:].rearrange("p k i s -> p k (i s)"), work[:, 0:2, 0:PAIR],
                                     ACT.Copy).then_inc(a_raw, 1)

            def make_a(p, part):
                if part < KM:
                    act.wait_ge(gn1.done, gn1.STEPS * p.n + gn1.COEF)
                    for i in range(2):
                        last = nc.scalar.activation(a_f[:, part, i, :], a_f[:, part, i, :], ACT.Relu,
                                                    bias=gn1.shift[:, i, part:part + 1],
                                                    scale=gn1.scale[:, i, part:part + 1])
                    last.then_inc(a_made, 1)
                    return
                act.wait_ge(a_made, KM * (p.n + 1))
                at_least(act, offset_products, p.n)
                nc.scalar.activation(inner_rows(a_hi), a_f[:].rearrange("p k i s -> p (k i) s"),
                                     ACT.Copy).then_inc(a_hi_made, 1)

            def make_hats(p, part):
                flat = offs[:, 0:2].rearrange("p c i s -> p (c i s)")
                if part == 0:
                    act.wait_ge(distance, p.n + 1)
                    nc.scalar.activation(flat, flat, ACT.Abs).then_inc(distance_abs, 1)
                elif part == 1:
                    act.wait_ge(distance_abs, p.n + 1)
                    nc.scalar.activation(flat, flat, ACT.Relu, bias=1.0, scale=-1.0).then_inc(hat_made, 1)
                else:
                    mask = offs[:, 2].rearrange("p i s -> p (i s)")
                    nc.scalar.activation(mask, mask, ACT.Sigmoid).then_inc(mask_made, 1)

            def transposed_hi(p, i):
                act.wait_ge(transposed, 2 * p.n + i + 1)
                if i == 0:
                    at_least(act, sampled, TILES * p.n)
                nc.scalar.activation(aT_hi[:, i].rearrange("p h c -> p (h c)"), work[0:HALF, i, :],
                                     ACT.Copy).then_inc(aT_hi_made, 1)

            def weights_hi(p, u):
                g = u // 2
                at_least(act, s_made[HATS_SLOT[u]], turns_of(p, u))
                at_least(act, sampled, TILES * p.n + 2 * (u - 1))
                nc.scalar.activation(s_hi[:, u % 2, :, 0:cols(g)], hats[:, HATS_SLOT[u], 0:2, 0:cols(g)],
                                     ACT.Copy).then_inc(s_hi_made, 1)

            def sampled_hi(p, t):
                g, i, c = t // 4, t // 2 % 2, t % 2
                at_least(act, sampled, TILES * p.n + t + 1)
                if t % 4 == 0:
                    at_least(act, deformed, GROUPS * p.n + (g - 1 if g > 1 else 0))
                nc.scalar.activation(v_hi[:, g % 2, c, 0:taps_of(g), i, :],
                                     sample[:, t % 2, 0:cols(g)].rearrange("p (k s) -> p k s", s=PIX),
                                     ACT.Copy).then_inc(v_hi_made, 1)

            def raw_b(p):
                act.wait_ge(deformed, GROUPS * (p.n + 1))
                nc.scalar.activation(b_f[:].rearrange("p k i s -> p k (i s)"), deform[:, :, 0:PAIR],
                                     ACT.Copy).then_inc(b_raw, 1)

            def make_b(p):
                act.wait_ge(gn2.done, gn2.STEPS * p.n + gn2.COEF)
                for k in range(KM):
                    for i in range(2):
                        last = nc.scalar.activation(b_f[:, k, i, :], b_f[:, k, i, :], ACT.Relu,
                                                    bias=gn2.shift[:, i, k:k + 1], scale=gn2.scale[:, i, k:k + 1])
                last.then_inc(b_made, 1)
                act.wait_ge(b_made, p.n + 1)
                at_least(act, conv3_done, 8 * p.n)
                nc.scalar.activation(b_hi[:], b_f[:].rearrange("p k i s -> p k (i s)"), ACT.Copy).then_inc(b_hi_made, 1)

            def write_y(p, k, after):
                if k == 0 and after is not None:
                    at_least(act, plus_y, 8 * (after.n + 1))
                elif k == 0:
                    at_least(act, added, 4 * p.n)
                at_least(act, conv3_done, 8 * p.n + k + 1)
                nc.scalar.activation(y[:, :, k, :], work[:, (k + 2) % 3, 0:PAIR].rearrange("p (i s) -> p i s", i=2),
                                     ACT.Copy).then_inc(y_written, 1)

            def rectify(p, first, end):
                act.wait_ge(added, 4 * p.n + (end - 1) // (KX // 2) + 1)
                for c in range(first, end):
                    i, k = divmod(c, KX)
                    last = nc.scalar.activation(x1[:, p.buf, i, k, :], x1[:, p.buf, i, k, :], ACT.Relu,
                                                bias=gn3.shift[:, i, k:k + 1])
                if end % KX == 0:
                    last.then_inc(rectified, 1)

            def step(before, now, after, coming):
                if before is not None:
                    raw_b(before)
                if after is not None:
                    make_x1(after, 4)
                    make_x1(after, 5)
                if now is not None:
                    weights_hi(now, 0)
                if after is not None:
                    make_x1(after, 6)
                    make_x1(after, 7)
                if before is not None:
                    make_b(before)
                if now is not None:
                    weights_hi(now, 1)
                if after is not None:
                    raw_a(after)
                for t in range(4):
                    if now is not None:
                        sampled_hi(now, t)
                    if before is not None and t:
                        write_y(before, 2 * t - 2, after)
                        write_y(before, 2 * t - 1, after)
                    if t == 2 and now is not None:
                        weights_hi(now, 2)
                if after is not None:
                    make_a(after, 0)
                    make_a(after, 1)
                if now is not None:
                    weights_hi(now, 3)
                if before is not None:
                    write_y(before, 6, after)
                    write_y(before, 7, after)
                if after is not None:
                    make_a(after, 2)
                for t in range(4, TILES):
                    if now is not None:
                        sampled_hi(now, t)
                    if now is not None:
                        if t % 2 and t < 16:
                            weights_hi(now, t // 2 + 2)
                    if t in RECTIFY_AT and before is not None:
                        rectify(before, *RECTIFY_AT[t])
                    if t in STORE_AT and before is not None:
                        store_out(before, STORE_AT.index(t))
                    if coming is not None:
                        if before is None and t == LOAD_AT[0]:
                            load_x(coming, 0)
                            load_x(coming, 1)
                        elif before is not None and t in LOAD_AT:
                            load_x(coming, LOAD_AT.index(t))
                    if t in HATS_AT and after is not None:
                        make_hats(after, HATS_AT.index(t))
                    if AHEAD_AT <= t < TILES - 1 and coming is not None:
                        make_x1(coming, t - AHEAD_AT)
                if after is not None:
                    transposed_hi(after, 0)
                    transposed_hi(after, 1)
                if coming is not None:
                    for k in range(TILES - 1 - AHEAD_AT, RING):
                        make_x1(coming, k)
                if after is None and now is None and before is None:
                    wo.make_hi(act, wo_stage, 1)
                    w3.make_hi(act, w3_stage, 1)
            by_iteration(act, step)
            for b in range(3):
                for i in range(2):
                    act.wait_ge(out_stored[b][i], 16 * ((PAIRS - b + 2) // 3))

        @block.gpsimd
        def _(pool):
            def distances(p):
                pool.wait_ge(offs_loaded, 48 * (p.n + 1))
                for c in range(2):
                    last = nc.gpsimd.tensor_tensor(offs[:, c], offs[:, c],
                                                   consts["grid"][:, c, :].unsqueeze(1).broadcast_to([TAPS * SIDE, 2, PIX]), ALU.add)
                last.then_inc(distance, 1)

            def mask_hats(p):
                pool.wait_ge(hat_made, p.n + 1)
                pool.wait_ge(mask_made, p.n + 1)
                nc.gpsimd.tensor_tensor(offs[:, 0], offs[:, 0], offs[:, 2], ALU.mult).then_inc(masked, 1)

            def weights(p, first, end):
                if p is not None:
                    for u in range(first, end):
                        if u in POOL_UNITS:
                            make_weights(nc.gpsimd, pool, p, u)

            def step(before, now, after, coming):
                weights(now, 0, 2)
                if before is not None:
                    gn2.root(pool, before.n, half_neg)
                weights(now, 2, 4)
                if after is not None:
                    gn1.root(pool, after.n, half_neg)
                weights(now, 4, 5)
                if before is not None:
                    gn3.root(pool, before.n, half_neg)
                weights(now, 5, UNITS)
                if after is not None:
                    distances(after)
                if after is not None:
                    mask_hats(after)
            by_iteration(pool, step)

        @block.vector
        def _(dve):
            nc.vector.memset(a_hi[:].bitcast(F32), 0.0)
            nc.vector.memset(a_lo[:].bitcast(F32), 0.0).then_inc(rows_cleared, 1)
            dve.wait_ge(rows_cleared, 1)

            def add_y(p, k):
                if k == 0:
                    for i in range(2):
                        dve.wait_ge(x_loaded[p.buf][i], 16 * (p.lap + 1))
                    dve.wait_ge(y_loaded, 32 * (p.n + 1))
                nc.vector.scalar_tensor_tensor(x1[:, p.buf, :, k, :], y[:, :, k, :],
                                               scale[:, k:k + 1], x1[:, p.buf, :, k, :], ALU.mult,
                                               ALU.add).then_inc(plus_y, 1)

            def x1_rest(p, k):
                at_least(dve, x1_hi_made, 8 * p.n + k + 1)
                at_least(dve, conv1_used, 8 * p.n + k + 1 - RING)
                nc.vector.tensor_tensor(x1_lo[:, k % RING], x1[:, p.buf, :, k, :], x1_hi[:, k % RING].bitcast(F32),
                                        ALU.subtract).then_inc(x1_lo_made, 1)

            def count(gn, t, raw, n):
                dve.wait_ge(raw, n + 1)
                for i in range(2):
                    for k in range(KM):
                        last = nc.vector.bn_stats(gn.stats[:, i, k, :], t[:, k, i, :])
                last.then_inc(gn.counted, 1)
                gn.reduce(dve, n)

            def a_rest(p):
                dve.wait_ge(a_hi_made, p.n + 1)
                at_least(dve, offset_products, p.n)
                nc.vector.tensor_tensor(inner_rows(a_lo), a_f[:].rearrange("p k i s -> p (k i) s"),
                                        inner_rows(a_hi).bitcast(F32), ALU.subtract).then_inc(a_lo_made, 1)

            def b_rest(p):
                dve.wait_ge(b_hi_made, p.n + 1)
                at_least(dve, conv3_done, 8 * p.n)
                nc.vector.tensor_tensor(b_lo[:], b_f[:].rearrange("p k i s -> p k (i s)"), b_hi[:].bitcast(F32),
                                        ALU.subtract).then_inc(b_lo_made, 1)

            def add_taps(p):
                dve.wait_ge(offset_products, p.n + 1)
                at_least(dve, om_stored, 16 * p.n)
                for done, column in enumerate((1, 0, 2)):
                    dx = column - 1
                    prod = work[32 * column:32 * column + OFFCH, 0, 0:PAIR].rearrange("p (i y x) -> p i y x", i=2, y=SIDE)
                    if dx == 0:
                        nc.vector.tensor_scalar(om[:], prod, consts["b_off"], None, ALU.add).then_inc(om_step, 1)
                        continue
                    dve.wait_ge(om_step, 3 * p.n + done)
                    z0, z1 = max(0, -dx), SIDE - max(0, dx)
                    nc.vector.tensor_tensor(om[:, :, :, z0:z1], prod[:, :, :, z0 + dx:z1 + dx], om[:, :, :, z0:z1],
                                            ALU.add).then_inc(om_step, 1)

            def transposed_rest(p, i):
                dve.wait_ge(aT_hi_made, 2 * p.n + i + 1)
                nc.vector.tensor_tensor(aT_lo[:, i].rearrange("p h c -> p (h c)"), work[0:HALF, i, :],
                                        aT_hi[:, i].rearrange("p h c -> p (h c)").bitcast(F32),
                                        ALU.subtract).then_inc(aT_lo_made, 1)

            def weights_rest(p, u):
                n = cols(u // 2)
                dve.wait_ge(s_hi_made, UNITS * p.n + u + 1)
                at_least(dve, sampled, TILES * p.n + 2 * (u - 1))
                nc.vector.tensor_tensor(s_lo[:, u % 2, :, 0:n], hats[:, HATS_SLOT[u], 0:2, 0:n],
                                        s_hi[:, u % 2, :, 0:n].bitcast(F32), ALU.subtract).then_inc(s_lo_made, 1)

            def sampled_rest(p, t):
                g, i, c = t // 4, t // 2 % 2, t % 2
                at_least(dve, v_hi_made, TILES * p.n + t + 1)
                if t % 4 == 0:
                    at_least(dve, deformed, GROUPS * p.n + (g - 1 if g > 1 else 0))
                nc.vector.tensor_tensor(v_lo[:, g % 2, c, 0:taps_of(g), i, :],
                                        sample[:, t % 2, 0:cols(g)].rearrange("p (k s) -> p k s", s=PIX),
                                        v_hi[:, g % 2, c, 0:taps_of(g), i, :].bitcast(F32),
                                        ALU.subtract).then_inc(v_lo_made, 1)

            def count_y(p, k):
                dve.wait_ge(y_written, 8 * p.n + k + 1)
                for i in range(2):
                    last = nc.vector.bn_stats(gn3.stats[:, i, k, :], y[:, i, k, :])
                if k == KX - 1:
                    last.then_inc(gn3.counted, 1)

            def add_x1(p, half):
                i, first = half // 2, half % 2 * (KX // 2)
                if half == 0:
                    dve.wait_ge(gn3.done, gn3.STEPS * p.n + gn3.COEF)
                for k in range(first, first + KX // 2):
                    last = nc.vector.scalar_tensor_tensor(x1[:, p.buf, i, k, :], y[:, i, k, :],
                                                          gn3.scale[:, i, k:k + 1], x1[:, p.buf, i, k, :],
                                                          ALU.mult, ALU.add)
                last.then_inc(added, 1)

            def my_weights(p, u):
                if u not in POOL_UNITS:
                    make_weights(nc.vector, dve, p, u)

            def step(before, now, after, coming):
                if after is not None:
                    add_y(after, 4)
                    add_y(after, 5)
                if now is not None:
                    my_weights(now, 0)
                    my_weights(now, 1)
                if before is not None:
                    count(gn2, b_f, b_raw, before.n)
                if after is not None:
                    add_y(after, 6)
                    x1_rest(after, 4)
                if before is not None:
                    gn2.moments_of(dve, before.n, sums[:, 4:8])
                if after is not None:
                    add_y(after, 7)
                    x1_rest(after, 5)
                if before is not None:
                    gn2.coefficients(dve, before.n)
                if after is not None:
                    x1_rest(after, 6)
                if now is not None:
                    weights_rest(now, 0)
                if after is not None:
                    x1_rest(after, 7)
                if before is not None:
                    b_rest(before)
                for t in range(4):
                    if now is not None:
                        sampled_rest(now, t)
                        if t == 0:
                            weights_rest(now, 1)
                    if t == 0 and after is not None:
                        count(gn1, a_f, a_raw, after.n)
                    if t == 2 and after is not None:
                        gn1.moments_of(dve, after.n, sums[:, 0:4])
                    if t == 3 and after is not None:
                        gn1.coefficients(dve, after.n)
                    if t == 3 and now is not None:
                        my_weights(now, 3)
                    if before is not None and t:
                        count_y(before, 2 * t - 2)
                        count_y(before, 2 * t - 1)
                    if t == 2 and now is not None:
                        my_weights(now, 2)
                        weights_rest(now, 2)
                if before is not None:
                    count_y(before, 6)
                if now is not None:
                    weights_rest(now, 3)
                if after is not None:
                    a_rest(after)
                for t in range(4, TILES):
                    if t == 6 and before is not None:
                        gn3.moments_of(dve, before.n, sums[:, 8:12])
                        gn3.coefficients(dve, before.n)
                    if now is not None:
                        sampled_rest(now, t)
                        if t % 2 and t < 16:
                            my_weights(now, t // 2 + 2)
                    if t == 4 and before is not None:
                        count_y(before, 7)
                    if now is not None and t % 2 == 0 and 6 <= t <= 16:
                        weights_rest(now, t // 2 + 1)
                    if t == 5 and before is not None:
                        gn3.reduce(dve, before.n)
                    if t == TAPS_AT and after is not None:
                        add_taps(after)
                    if t in ADD_AT and before is not None:
                        add_x1(before, ADD_AT.index(t))
                    if t >= AHEAD_AT and coming is not None:
                        add_y(coming, t - AHEAD_AT)
                        if t > AHEAD_AT:
                            x1_rest(coming, t - AHEAD_AT - 1)
                if coming is not None:
                    for k in range(TILES - AHEAD_AT, RING):
                        add_y(coming, k)
                if after is not None:
                    transposed_rest(after, 0)
                    transposed_rest(after, 1)
                if coming is not None:
                    for k in range(TILES - AHEAD_AT - 1, RING):
                        x1_rest(coming, k)
                if after is None and now is None and before is None:
                    wo.make_lo(dve, wo_stage, 1)
                    w3.make_lo(dve, w3_stage, 1)
            by_iteration(dve, step)

        @block.tensor
        def _(pe):
            def conv1(p, k):
                if k == 0:
                    at_least(pe, aT_lo_made, 2 * p.n)
                at_least(pe, x1_lo_made, 8 * p.n + k + 1)
                for t in range(KM):
                    last = product3(nc, work[:, t, 0:PAIR].rearrange("p (i s) -> p i s", i=2),
                                    w1_hi[:, k, t, :], w1_lo[:, k, t, :], x1_hi[:, k % RING], x1_lo[:, k % RING],
                                    start=(k == 0), stop=(k == KX - 1))
                last.then_inc(conv1_used, 1)

            def offsets(p, first, end):
                if first == 0 and isinstance(p.n, int) and p.n == 0:
                    pe.wait_ge(wo.lo_made, 1)
                pe.wait_ge(a_lo_made, p.n + 1)
                for row in range(first, end):
                    for k in range(KM):
                        last = product3(nc, work[0:96, 0, 0:PAIR].rearrange("p (i s) -> p i s", i=2),
                                        wo_hi[:, k, row, :], wo_lo[:, k, row, :],
                                        a_hi[:, k, :, row:row + SIDE, :].rearrange("p i y x -> p i (y x)"),
                                        a_lo[:, k, :, row:row + SIDE, :].rearrange("p i y x -> p i (y x)"),
                                        start=(row == 0 and k == 0), stop=(row == 2 and k == KM - 1))
                if end == 3:
                    last.then_inc(offset_products, 1)

            def transposes(p):
                at_least(pe, om_step, 3 * (p.n + 1))
                for i in range(2):
                    for h in range(2):
                        for k in range(KM):
                            last = nc.tensor.transpose(work[0:HALF, i, (h * KM + k) * P:(h * KM + k + 1) * P],
                                                       a_f[:, k, i, h * HALF:(h + 1) * HALF], ident[:])
                    last.then_inc(transposed, 1)

            def sample_tile(p, t):
                g, i, c = t // 4, t // 2 % 2, t % 2
                u, n = t // 2, cols(g)
                if t == 0:
                    at_least(pe, aT_lo_made, 2 * p.n + 2)
                if c == 0:
                    at_least(pe, s_lo_made, UNITS * p.n + u + 1)
                at_least(pe, v_lo_made, TILES * p.n + t - 1)
                for h in range(2):
                    last = product3(nc, sample[:, t % 2, 0:n], aT_hi[:, i, h, c * P:(c + 1) * P],
                                    aT_lo[:, i, h, c * P:(c + 1) * P], s_hi[:, u % 2, h, 0:n], s_lo[:, u % 2, h, 0:n],
                                    start=(h == 0), stop=(h == 1))
                last.then_inc(sampled, 1)

            def deform_part(p, g, part):
                k, t = divmod(part, 2)
                if part == 0:
                    at_least(pe, v_lo_made, TILES * p.n + 4 * g + 4)
                    if g == 0:
                        at_least(pe, b_raw, p.n)
                for tap in range(taps_of(g)):
                    last = product3(nc, deform[:, t, 0:PAIR], w2_hi[:, k, 2 * g + tap, t, :],
                                    w2_lo[:, k, 2 * g + tap, t, :],
                                    v_hi[:, g % 2, k, tap].rearrange("p i s -> p (i s)"),
                                    v_lo[:, g % 2, k, tap].rearrange("p i s -> p (i s)"),
                                    start=(g == 0 and k == 0 and tap == 0),
                                    stop=(g == GROUPS - 1 and k == KM - 1 and tap == taps_of(g) - 1))
                if part == 3:
                    last.then_inc(deformed, 1)

            def conv3(p, k, now, after):
                bank = (k + 2) % 3
                if k == 0 and isinstance(p.n, int) and p.n == 0:
                    pe.wait_ge(w3.lo_made, 1)
                if k == 0:
                    pe.wait_ge(b_lo_made, p.n + 1)
                if k == 1 and after is not None:
                    pe.wait_ge(a_raw, after.n + 1)
                if k >= 3:
                    at_least(pe, y_written, 8 * p.n + k - 2)
                if k == 1 and after is None:
                    if now is not None:
                        pe.wait_ge(aT_lo_made, 2 * (now.n + 1))
                    pe.wait_ge(y_written, 8 * p.n)
                for c in range(KM):
                    last = product3(nc, work[:, bank, 0:PAIR], w3_hi[:, c, k, :], w3_lo[:, c, k, :],
                                    b_hi[:, c, :], b_lo[:, c, :], start=(c == 0), stop=(c == KM - 1))
                last.then_inc(conv3_done, 1)

            def step(before, now, after, coming):
                for k in range(KX):
                    if after is not None:
                        conv1(after, k)
                    if k == 3 and before is not None:
                        at_least(pe, added, 4 * before.n)
                        gn2.group(pe, before.n, ones, sums[:, 4:8])
                for t in range(4):
                    if now is not None:
                        sample_tile(now, t)
                    if t == 2 and after is not None:
                        if before is not None:
                            pe.wait_ge(gn2.done, gn2.STEPS * before.n + gn2.MOMENTS)
                        gn1.group(pe, after.n, ones, sums[:, 0:4])
                    if before is not None and t:
                        conv3(before, 2 * t - 2, now, after)
                        conv3(before, 2 * t - 1, now, after)
                if before is not None:
                    conv3(before, 6, now, after)
                    conv3(before, 7, now, after)
                for t in range(4, TILES):
                    if now is not None:
                        sample_tile(now, t)
                        deform_part(now, t // 4 - 1, t % 4)
                    if t == 5 and after is not None:
                        if before is not None:
                            pe.wait_ge(y_written, 8 * (before.n + 1))
                        else:
                            pe.wait_ge(a_raw, after.n + 1)
                        offsets(after, 0, 2)
                    if t == 5 and before is not None:
                        if after is not None:
                            pe.wait_ge(gn1.done, gn1.STEPS * after.n + gn1.MOMENTS)
                        else:
                            pe.wait_ge(gn2.done, gn2.STEPS * before.n + gn2.MOMENTS)
                        gn3.group(pe, before.n, ones, sums[:, 8:12])
                    if t == 5 and after is not None:
                        offsets(after, 2, 3)
                if after is not None:
                    transposes(after)
                if now is not None:
                    for q in range(4):
                        deform_part(now, GROUPS - 1, q)
            by_iteration(pe, step)


def build(nc, x, w, vectors, grid, ident, ones, b_off, out):
    y3 = nc.dram_tensor("y3_scratch", [PAIRS, P, 2, KX * PIX], F32).ap()
    offsets_at = nc.dram_tensor("offset_scratch", [OFFCH, PAIR], F32).ap()
    hats_at = nc.dram_tensor("hat_scratch", [2, 2, SIDE, TAPS * PIX], F32).ap()
    x_v = x.rearrange("(g i) (p k) s -> g p i (k s)", i=2, p=P)
    out_v = out.rearrange("(g i) (p k) s -> g p i (k s)", i=2, p=P)
    with ExitStack() as ctx:
        def sb(name, shape, dt=F32):
            return ctx.enter_context(nc.sbuf_tensor(name, shape, dt))
        vec = {n: sb("v_" + n, [P, a.shape[0] // P]) for n, a in vectors.items()}
        resid = sb("v_resid", [P, 1])
        grid_s = sb("grid_s", [TAPS * SIDE, 2, PIX])
        ident_s = sb("ident_s", [P, P])
        ones_s = sb("ones_s", [P, P])
        b_off_s = sb("b_off_s", [OFFCH, 1])
        half_neg = sb("half_neg", [P, KX])
        scale1, shift1 = sb("scale1", [P, KM]), sb("shift1", [P, KM])
        scale2, shift2 = sb("scale2", [P, KM]), sb("shift2", [P, KM])
        scale3, shift3 = sb("scale3", [P, KX]), sb("shift3", [P, KX])
        constants = [(t[:], vectors[n].rearrange("(p k) -> p k", p=P)) for n, t in vec.items()]
        constants += [(resid[:], w["residual"].unsqueeze(0).broadcast_to([P, 1])), (grid_s[:], grid),
                      (ident_s[:], ident), (ones_s[:], ones), (b_off_s[:], b_off)]
        w1 = Weights(nc, ctx, "w1", [KX, KM, P])
        w2 = Weights(nc, ctx, "w2", [KM, TAPS, KM, P])
        with ExitStack() as inner:
            h = inner.enter_context(nc.sbuf_tensor("h", [P, KM, PAIRS * PAIR], F32))
            with nc.sbuf_tensor("stats1", [P, KM, PAIRS, 6], F32) as stats:
                conv1_phase(nc, x_v, w1, w["w1a"], w2, w["w2a"], constants, half_neg, h, stats)
                bn_coefficients(nc, "bn1", stats, KM, vec["g1"][:], vec["be1"][:], vec["b1"][:], half_neg, scale1, shift1)
            w3 = Weights(nc, inner, "w3a", [KM, KX, P])
            with nc.sbuf_tensor("stats2", [P, KM, PAIRS, 6], F32) as stats:
                conv2_phase(nc, w2, w3, w["w3a"], w1, w["w1b"], h, scale1, shift1, stats)
                bn_coefficients(nc, "bn2", stats, KM, vec["g2"][:], vec["be2"][:], vec["b2"][:], half_neg, scale2, shift2)
            with nc.sbuf_tensor("stats3", [P, KX, PAIRS, 6], F32) as stats:
                conv3_phase(nc, w3, w2, w["w2b"], h, scale2, shift2, stats, y3)
                bn_coefficients(nc, "bn3", stats, KX, vec["g3"][:], vec["be3"][:], vec["b3"][:], half_neg, scale3, shift3,
                                residual=resid[:])
        consts = {n: vec[n][:] for n in vec} | {
            "grid": grid_s, "ident": ident_s, "ones": ones_s, "b_off": b_off_s[:], "half_neg": half_neg}
        deformable_phase(nc, x_v, y3, scale3, shift3, w1, w2, w["w3b"], w["woff"], consts, offsets_at, hats_at, out_v)


def _conv1x1(a, kin, kout):
    return a.reshape(P, kout, P, kin).transpose(2, 3, 1, 0).reshape(P, kin * kout * P)


def _conv3x3(a):
    return a.reshape(P, KM, P, KM, TAPS).transpose(2, 3, 4, 1, 0).reshape(P, KM * TAPS * KM * P)


def kernel(**inputs):
    import numpy as np
    import concourse.bacc as bacc
    from concourse.bass_utils import run_bass_kernel_spmd

    a = {n: np.asarray(v) for n, v in inputs.items()}
    woff = np.zeros((P, KM, 3, 3, 32), np.float32)
    woff[..., 0:OFFCH] = a["L1_conv_w_off"].reshape(OFFCH, P, KM, 3, 3).transpose(1, 2, 3, 4, 0)
    tap, q, iy, ix = np.meshgrid(np.arange(TAPS), np.arange(SIDE), np.arange(SIDE), np.arange(SIDE), indexing="ij")
    grid = np.stack([iy + tap // 3 - 1 - q, ix + tap % 3 - 1 - q], axis=2)
    arrays = {
        "x": a["x"].reshape(NIMG, CIN, PIX),
        "w1a": _conv1x1(a["L0_conv_w1"], KX, KM), "w2a": _conv3x3(a["L0_conv_w2"]),
        "w3a": _conv1x1(a["L0_conv_w3"], KM, KX), "residual": a["L0_conv_residual_scale"],
        "w1b": _conv1x1(a["L1_conv_w1"], KX, KM), "w2b": _conv3x3(a["L1_conv_w2"]),
        "w3b": _conv1x1(a["L1_conv_w3"], KM, KX), "woff": woff.reshape(P, KM * 3 * 96),
        "grid": grid.reshape(TAPS * SIDE, 2, PIX).astype(np.float32),
        "ident": np.eye(P, dtype=np.float32),
        "ones": np.kron(np.eye(P // 4, dtype=np.float32), np.ones((4, 4), np.float32)),
        "b_off": a["L1_conv_b_off"].reshape(OFFCH, 1),
    }
    vectors = {n: a["L0_conv_" + n] for n in ("b1", "g1", "be1", "b2", "g2", "be2", "b3", "g3", "be3")}
    vectors |= {n: a["L1_conv_" + n] for n in ("gn1_scale", "gn1_bias", "gn2_scale", "gn2_bias", "gn3_scale", "gn3_bias")}
    nc = bacc.Bacc("TRN2", target_bir_lowering=False, num_devices=1, dynamic_dma_scratch_size=1024)
    feeds = {"in_" + n: np.ascontiguousarray(v) for n, v in (arrays | vectors).items()}
    t = {n[3:]: nc.dram_tensor(n, v.shape, F32, kind="ExternalInput").ap() for n, v in feeds.items()}
    out = nc.dram_tensor("out", (NIMG, CIN, PIX), F32, kind="ExternalOutput").ap()
    w = {n: t[n] for n in ("w1a", "w2a", "w3a", "w1b", "w2b", "w3b", "woff", "residual")}
    build(nc, t["x"], w, {n: t[n] for n in vectors}, t["grid"], t["ident"], t["ones"], t["b_off"], out)
    got = run_bass_kernel_spmd(nc, [feeds], core_ids=[0])
    return got.results[0]["out"].reshape(NIMG, CIN, SIDE, SIDE)
```
